# Optimizing a Trainium2 kernel written in Bass

```python
import numpy as np
import jax
import jax.numpy as jnp

def _softmax(x, axis=-1):
    return jax.nn.softmax(x, axis=axis)

def _gelu(x):
    return jax.nn.gelu(x, approximate=True)

def _silu(x):
    return jax.nn.silu(x)

def _sigmoid(x):
    return jax.nn.sigmoid(x)

def _layernorm(x, axis=-1, eps=1e-05):
    m = jnp.mean(x, axis=axis, keepdims=True)
    v = jnp.var(x, axis=axis, keepdims=True)
    return (x - m) / jnp.sqrt(v + eps)

def _scatter_add(tgt, idx, src, axis=0):
    return tgt.at[idx].add(src)

def _segment_sum(src, seg, n):
    return jax.ops.segment_sum(src, seg, n)
kernel_name = 'mk_xattn_ffn_d2_seqx_r4_a445f1'

def setup_inputs(seed: int=0):
    np.random.seed(seed)
    _w = jnp.asarray

    def _rec_inputs():
        import jax
        import jax.numpy as jnp
        _rk = jax.random.key(seed)
        x = -0.0002928 + 1 * jax.random.normal(jax.random.fold_in(_rk, 1), (16, 128, 256), jnp.float32)
        _lenS = 128 - jax.random.randint(jax.random.fold_in(_rk, 7), (16,), 0, max(1, 128 // 4) + 1, jnp.int32)
        _lenS2 = 128 - jax.random.randint(jax.random.fold_in(_rk, 8), (16,), 0, max(1, 128 // 4) + 1, jnp.int32)
        _ctx_1024P = jax.random.normal(jax.random.fold_in(_rk, 11), (16, 16, 256), jnp.float32)
        _ctx_1024c = jax.random.dirichlet(jax.random.fold_in(_rk, 511), 0.3 * jnp.ones((16,), jnp.float32), (16, 128))
        _ctx_1024t = jnp.einsum('bsk,bkd->bsd', _ctx_1024c, _ctx_1024P)
        _ctx_1024t = _ctx_1024t * jax.lax.rsqrt(jnp.mean(jnp.square(_ctx_1024t)) + 1e-12) * 0.953939
        ctx_1024 = -1.39393e-06 + 0.999914 * (_ctx_1024t + 0.3 * jax.random.normal(jax.random.fold_in(_rk, 611), (16, 128, 256), jnp.float32))
        _validS = jnp.arange(128)[None, :] < _lenS[:, None]
        _validS2 = jnp.arange(128)[None, :] < _lenS2[:, None]
        _causal = jnp.tril(jnp.ones((128, 128), dtype=bool))
        mask_BxS2_if1 = jnp.where(jnp.ones((16, 128), dtype=bool), 1, 0).astype(jnp.int32)
        return (x, ctx_1024, mask_BxS2_if1)
    x, ctx_1024, mask_BxS2_if1 = _rec_inputs()

    def _L0_xattn_setup():
        import jax, jax.numpy as jnp
        import numpy as np
        B, S, D, NH = (2, 512, 256, 8)
        DH = D // NH
        EPS = 1e-06
        LN_EPS = 1e-05

        def _mlstm_cell(q, k, v, igate_w, igate_b, fgate_w, fgate_b, ln_scale):
            Slen = q.shape[0]
            ifg = jnp.concatenate([q, k, v], axis=-1)
            ig = (ifg @ igate_w.T + igate_b).T
            fg = (ifg @ fgate_w.T + fgate_b).T
            qh = q.reshape(Slen, NH, DH).transpose(1, 0, 2)
            kh = k.reshape(Slen, NH, DH).transpose(1, 0, 2)
            vh = v.reshape(Slen, NH, DH).transpose(1, 0, 2)
            log_f = jax.nn.log_sigmoid(fg)
            cs = jnp.cumsum(log_f, axis=1)
            fg_mat = cs[:, :, None] - cs[:, None, :]
            mask = jnp.tril(jnp.ones((Slen, Slen), dtype=bool))
            log_fg_mat = jnp.where(mask, fg_mat, -jnp.inf)
            log_D = log_fg_mat + ig[:, None, :]
            max_log_D = jnp.max(log_D, axis=-1, keepdims=True)
            D_mat = jnp.exp(log_D - max_log_D)
            qk = jnp.einsum('hsd,htd->hst', qh, kh) / np.sqrt(DH)
            C = qk * D_mat
            normalizer = jnp.maximum(jnp.abs(C.sum(axis=-1, keepdims=True)), jnp.exp(-max_log_D))
            h = jnp.einsum('hst,htd->hsd', C / (normalizer + EPS), vh)
            h = h.transpose(1, 0, 2).reshape(Slen, D)
            mu = h.mean(axis=-1, keepdims=True)
            var = h.var(axis=-1, keepdims=True)
            return (h - mu) / jnp.sqrt(var + LN_EPS) * ln_scale
        key = jax.random.key(seed)
        ks = jax.random.split(key, 8)
        rnd = lambda k, sh, s=1.0: jax.random.normal(k, sh, dtype=jnp.float32) * s
        return {'q': rnd(ks[0], (B, S, D)), 'k': rnd(ks[1], (B, S, D)), 'v': rnd(ks[2], (B, S, D)), 'igate_w': rnd(ks[3], (NH, 3 * D), 0.02), 'igate_b': jnp.linspace(3.0, 6.0, NH, dtype=jnp.float32), 'fgate_w': rnd(ks[4], (NH, 3 * D), 0.02), 'fgate_b': rnd(ks[5], (NH,), 0.3162278), 'ln_scale': jnp.ones((D,), dtype=jnp.float32)}
    _L0_xattn_all = _L0_xattn_setup()
    _L0_xattn_in = {k: v for k, v in _L0_xattn_all.items() if k in ('igate_w', 'igate_b', 'fgate_w', 'fgate_b', 'ln_scale')}
    del _L0_xattn_all

    def _L0_ffn_setup():
        import jax, jax.numpy as jnp
        import numpy as np
        DIM = 256
        HIDDEN = 768
        SCALE = 1.0 / 127.0

        def _dequant(w_int, dtype):
            return w_int.astype(dtype) * jnp.asarray(SCALE, dtype)
        key = jax.random.key(seed)
        k_x, k_g, k_u, k_d = jax.random.split(key, 4)
        x = jax.random.normal(k_x, (4, 512, DIM), dtype=jnp.float32)
        w_gate = jax.random.randint(k_g, (HIDDEN, DIM), -127, 128, dtype=jnp.int32)
        w_up = jax.random.randint(k_u, (HIDDEN, DIM), -127, 128, dtype=jnp.int32)
        w_down = jax.random.randint(k_d, (DIM, HIDDEN), -127, 128, dtype=jnp.int32)
        return {'x': x, 'w_gate': w_gate, 'w_up': w_up, 'w_down': w_down}
    _L0_ffn_all = _L0_ffn_setup()
    _L0_ffn_in = {k: v for k, v in _L0_ffn_all.items() if k in ('w_gate', 'w_up', 'w_down')}
    del _L0_ffn_all

    def _L1_xattn_setup():
        import jax, jax.numpy as jnp
        import numpy as np
        NEG = -10000.0
        key = jax.random.key(seed)
        k1, k2, k3 = jax.random.split(key, 3)
        B, L, D, H = (16, 512, 256, 256)
        x1 = jax.random.normal(k1, (B, L, D), dtype=jnp.float32)
        x2 = jax.random.normal(k2, (B, L, D), dtype=jnp.float32)
        x2_mask = jnp.ones((B, L), dtype=jnp.int64)
        W = jax.random.normal(k3, (H, D), dtype=jnp.float32) * (1.0 / np.sqrt(D))
        diagonal = jnp.ones((H,), dtype=jnp.float32)
        return {'x1': x1, 'x2': x2, 'x2_mask': x2_mask, 'W': W, 'diagonal': diagonal}
    _L1_xattn_all = _L1_xattn_setup()
    _L1_xattn_in = {k: v for k, v in _L1_xattn_all.items() if k in ('W', 'diagonal')}
    del _L1_xattn_all

    def _L1_ffn_setup():
        import jax, jax.numpy as jnp
        import numpy as np
        D_IN, D_HID = (256, 1024)

        def _ternary(key, shape):
            return jax.random.randint(key, shape, -1, 2).astype(jnp.float32)

        def _tlin(x, w, s):
            return jnp.einsum('bsi,oi->bso', x, w) * s
        key = jax.random.key(seed)
        ks = jax.random.split(key, 12)
        inv = lambda fan: 1.0 / np.sqrt(fan).astype(np.float32)
        return {'x': jax.random.normal(ks[0], (4, 512, D_IN), dtype=jnp.float32), 'w1_w': _ternary(ks[1], (D_HID, D_IN)), 'w1_s': jax.random.uniform(ks[2], (D_HID,), dtype=jnp.float32) * inv(D_IN), 'w2_w': _ternary(ks[3], (D_HID, D_IN)), 'w2_s': jax.random.uniform(ks[4], (D_HID,), dtype=jnp.float32) * inv(D_IN), 'h1_w': _ternary(ks[5], (D_HID, D_HID)), 'h1_s': jax.random.uniform(ks[6], (D_HID,), dtype=jnp.float32) * inv(D_HID), 'h2_w': _ternary(ks[7], (D_HID, D_HID)), 'h2_s': jax.random.uniform(ks[8], (D_HID,), dtype=jnp.float32) * inv(D_HID), 'w3_w': _ternary(ks[9], (D_IN, D_HID)), 'w3_s': jax.random.uniform(ks[10], (D_IN,), dtype=jnp.float32) * inv(D_HID)}
    _L1_ffn_all = _L1_ffn_setup()
    _L1_ffn_in = {k: v for k, v in _L1_ffn_all.items() if k in ('w1_w', 'w1_s', 'w2_w', 'w2_s', 'h1_w', 'h1_s', 'h2_w', 'h2_s', 'w3_w', 'w3_s')}
    del _L1_ffn_all
    return {'x': x, 'ctx_1024': ctx_1024, 'mask_BxS2_if1': mask_BxS2_if1, 'L0_xattn_igate_w': _L0_xattn_in['igate_w'], 'L0_xattn_igate_b': _L0_xattn_in['igate_b'], 'L0_xattn_fgate_w': _L0_xattn_in['fgate_w'], 'L0_xattn_fgate_b': _L0_xattn_in['fgate_b'], 'L0_xattn_ln_scale': _L0_xattn_in['ln_scale'], 'L0_ffn_w_gate': _L0_ffn_in['w_gate'], 'L0_ffn_w_up': _L0_ffn_in['w_up'], 'L0_ffn_w_down': _L0_ffn_in['w_down'], 'L1_xattn_W': _L1_xattn_in['W'], 'L1_xattn_diagonal': _L1_xattn_in['diagonal'], 'L1_ffn_w1_w': _L1_ffn_in['w1_w'], 'L1_ffn_w1_s': _L1_ffn_in['w1_s'], 'L1_ffn_w2_w': _L1_ffn_in['w2_w'], 'L1_ffn_w2_s': _L1_ffn_in['w2_s'], 'L1_ffn_h1_w': _L1_ffn_in['h1_w'], 'L1_ffn_h1_s': _L1_ffn_in['h1_s'], 'L1_ffn_h2_w': _L1_ffn_in['h2_w'], 'L1_ffn_h2_s': _L1_ffn_in['h2_s'], 'L1_ffn_w3_w': _L1_ffn_in['w3_w'], 'L1_ffn_w3_s': _L1_ffn_in['w3_s']}

def reference(x, ctx_1024, mask_BxS2_if1, L0_xattn_igate_w, L0_xattn_igate_b, L0_xattn_fgate_w, L0_xattn_fgate_b, L0_xattn_ln_scale, L0_ffn_w_gate, L0_ffn_w_up, L0_ffn_w_down, L1_xattn_W, L1_xattn_diagonal, L1_ffn_w1_w, L1_ffn_w1_s, L1_ffn_w2_w, L1_ffn_w2_s, L1_ffn_h1_w, L1_ffn_h1_s, L1_ffn_h2_w, L1_ffn_h2_s, L1_ffn_w3_w, L1_ffn_w3_s):
    import jax
    import jax.numpy as jnp

    def _L0_xattn_ref(q, k, v, igate_w, igate_b, fgate_w, fgate_b, ln_scale):
        import jax, jax.numpy as jnp
        import numpy as np
        B, S, D, NH = (2, 512, 256, 8)
        DH = D // NH
        EPS = 1e-06
        LN_EPS = 1e-05

        def _mlstm_cell(q, k, v, igate_w, igate_b, fgate_w, fgate_b, ln_scale):
            Slen = q.shape[0]
            ifg = jnp.concatenate([q, k, v], axis=-1)
            ig = (ifg @ igate_w.T + igate_b).T
            fg = (ifg @ fgate_w.T + fgate_b).T
            qh = q.reshape(Slen, NH, DH).transpose(1, 0, 2)
            kh = k.reshape(Slen, NH, DH).transpose(1, 0, 2)
            vh = v.reshape(Slen, NH, DH).transpose(1, 0, 2)
            log_f = jax.nn.log_sigmoid(fg)
            cs = jnp.cumsum(log_f, axis=1)
            fg_mat = cs[:, :, None] - cs[:, None, :]
            mask = jnp.tril(jnp.ones((Slen, Slen), dtype=bool))
            log_fg_mat = jnp.where(mask, fg_mat, -jnp.inf)
            log_D = log_fg_mat + ig[:, None, :]
            max_log_D = jnp.max(log_D, axis=-1, keepdims=True)
            D_mat = jnp.exp(log_D - max_log_D)
            qk = jnp.einsum('hsd,htd->hst', qh, kh) / np.sqrt(DH)
            C = qk * D_mat
            normalizer = jnp.maximum(jnp.abs(C.sum(axis=-1, keepdims=True)), jnp.exp(-max_log_D))
            h = jnp.einsum('hst,htd->hsd', C / (normalizer + EPS), vh)
            h = h.transpose(1, 0, 2).reshape(Slen, D)
            mu = h.mean(axis=-1, keepdims=True)
            var = h.var(axis=-1, keepdims=True)
            return (h - mu) / jnp.sqrt(var + LN_EPS) * ln_scale
        return jax.vmap(lambda qq, kk, vv: _mlstm_cell(qq, kk, vv, igate_w, igate_b, fgate_w, fgate_b, ln_scale))(q, k, v)

    def _L0_ffn_ref(x, w_gate, w_up, w_down):
        import jax, jax.numpy as jnp
        import numpy as np
        DIM = 256
        HIDDEN = 768
        SCALE = 1.0 / 127.0

        def _dequant(w_int, dtype):
            return w_int.astype(dtype) * jnp.asarray(SCALE, dtype)
        wg = _dequant(w_gate, x.dtype)
        wu = _dequant(w_up, x.dtype)
        wd = _dequant(w_down, x.dtype)
        gate = jnp.einsum('bsd,hd->bsh', x, wg)
        up = jnp.einsum('bsd,hd->bsh', x, wu)
        h = jax.nn.silu(gate) * up
        return jnp.einsum('bsh,dh->bsd', h, wd)

    def _L1_xattn_ref(x1, x2, x2_mask, W, diagonal):
        import jax, jax.numpy as jnp
        import numpy as np
        NEG = -10000.0
        x1_rep = jax.nn.relu(jnp.einsum('bld,hd->blh', x1, W))
        x2_rep = jax.nn.relu(jnp.einsum('bld,hd->blh', x2, W))
        scores = jnp.einsum('bih,bjh->bij', x1_rep * diagonal, x2_rep)
        m = (1.0 - x2_mask.astype(scores.dtype)) * NEG
        alpha = jax.nn.softmax(scores + m[:, None, :], axis=-1)
        return jnp.einsum('bij,bjd->bid', alpha, x2)

    def _L1_ffn_ref(x, w1_w, w1_s, w2_w, w2_s, h1_w, h1_s, h2_w, h2_s, w3_w, w3_s):
        import jax, jax.numpy as jnp
        import numpy as np
        D_IN, D_HID = (256, 1024)

        def _ternary(key, shape):
            return jax.random.randint(key, shape, -1, 2).astype(jnp.float32)

        def _tlin(x, w, s):
            return jnp.einsum('bsi,oi->bso', x, w) * s
        h = jax.nn.silu(_tlin(x, w1_w, w1_s)) * _tlin(x, w2_w, w2_s)
        h = jax.nn.gelu(_tlin(h, h1_w, h1_s), approximate=False)
        h = jax.nn.gelu(_tlin(h, h2_w, h2_s), approximate=False)
        return _tlin(h, w3_w, w3_s)
    x = x + _L0_xattn_ref(_layernorm(x, axis=-1), ctx_1024, ctx_1024, L0_xattn_igate_w, L0_xattn_igate_b, L0_xattn_fgate_w, L0_xattn_fgate_b, L0_xattn_ln_scale)
    x = x + _L0_ffn_ref(_layernorm(x, axis=-1), L0_ffn_w_gate, L0_ffn_w_up, L0_ffn_w_down)
    x = x + _L1_xattn_ref(_layernorm(x, axis=-1), ctx_1024, mask_BxS2_if1, L1_xattn_W, L1_xattn_diagonal)
    x = x + _L1_ffn_ref(_layernorm(x, axis=-1), L1_ffn_w1_w, L1_ffn_w1_s, L1_ffn_w2_w, L1_ffn_w2_s, L1_ffn_h1_w, L1_ffn_h1_s, L1_ffn_h2_w, L1_ffn_h2_s, L1_ffn_w3_w, L1_ffn_w3_s)
    return x

_drawn_inputs = setup_inputs


def setup_inputs(seed=0):
    import zlib

    import numpy as np

    out = dict(_drawn_inputs(seed))
    spreads = {'L0_xattn_ln_scale': (1.0, 0.2), 'L1_xattn_diagonal': (1.0, 0.2)}
    factors = {}
    for name, (base, spread) in spreads.items():
        noise = np.random.default_rng([zlib.crc32(name.encode()), seed]).standard_normal(out[name].shape)
        drawn = base * np.exp(spread * noise) if base else spread * noise
        out[name] = jnp.asarray(drawn.astype(out[name].dtype))
    for name, factor in factors.items():
        out[name] = (out[name] * factor).astype(out[name].dtype)
    return out
```

```python
from contextlib import ExitStack

import concourse.bass as bass
from concourse import mybir
from concourse.alu_op_type import AluOpType as ALU

ACT = mybir.ActivationFunctionType
F32 = mybir.dt.float32
F32R = mybir.dt.float32r
BF16 = mybir.dt.bfloat16
I32 = mybir.dt.int32
U16 = mybir.dt.uint16
AX = mybir.AxisListType

P = 128
NB, S, D = 16, 128, 256
NH, DH = 8, 32
KD = D // P
Q = 4
G = NB // Q
GT = Q * S
HB = 768
MB = HB // P
HD = 1024
MD = HD // P
VW = DH + 1
PVW = 3 * VW
UN = 2 * Q
RA = 3 + 3 * Q
MASKED = 1e30
BIG = 3e38
SCALE_B = 1.0 / 127.0
RS_DH = float(DH) ** -0.5
NEG = -10000.0
EPS = 1e-6
CONSTS = 16 * 11
NRAW = 2 * KD * 2 + MB + KD
TRASH = 7
W_ALL = 2 * KD * HD + MD * D + 2 * MD * HD
SEC_W1, SEC_W2 = 0, KD * HD
SEC_W3 = 2 * KD * HD
SEC_H1 = SEC_W3 + MD * D
SEC_H2 = SEC_H1 + MD * HD
FLAG_ITEMS = G * UN
FLAG_W = W_ALL // FLAG_ITEMS
RING = 2
ITEMS_G = 3 * MD + 2


class Chain:

    def __init__(self, eng, sem, per, index):
        self.eng, self.sem, self.per, self.base, self.n = eng, sem, per, index * per, 0

    def step(self, ins):
        ins.then_inc(self.sem, 1)
        self.n += 1

    def settle(self):
        self.eng.wait_ge(self.sem, self.base + self.n)

    def settle_apart(self):
        self.settle()
        self.eng.sem_inc(self.sem, 1)
        self.n += 1

    def start_apart(self):
        self.eng.sem_inc(self.sem, 1)
        self.n += 1

    def end(self):
        assert self.n == self.per, (self.n, self.per)


def two_layers(nc, x_in, ctx_in, ctxT_in, mask_in, gw_in, gb_in, lns_in, l0gu_in, l0d_in, xaw_in, diag_in,
               w_all_in, s_cols_in, s3_in, ident_in, tri_in, ones_rows_in, out):
    es = ExitStack()
    base = [(nc.sbuf_base + 63) // 64 * 64]
    sizes = {F32: 4, F32R: 4, I32: 4, BF16: 2, U16: 2}

    def place(at, name, shape, dt):
        n = sizes[dt]
        for d in shape[1:]:
            n *= d
        t = nc.alloc_sbuf_tensor_at(name, shape, dt, offset=at[0])
        at[0] += (n + 31) // 32 * 32
        return t

    def sem(name):
        return es.enter_context(nc.semaphore(name))

    with es:
        x = place(base, "x", [P, NB, D], F32)
        w1 = place(base, "w1", [P, KD, HD], F32R)
        w2 = place(base, "w2", [P, KD, HD], F32R)
        w3 = place(base, "w3", [P, MD, D], F32R)
        ring_at = [base[0] - 3 * KD * HD * 4]
        ring = place(ring_at, "ring", [P, RING, MD, P], F32)
        xT = place(base, "xT", [P, 2, 2, KD, GT], F32R)
        xn = place(base, "xn", [P, Q, D], F32)
        stage_at = [base[0]]
        stage = place(base, "stage", [P, 2, HD], F32)
        silD = place(stage_at, "silD", [P, 2, GT], F32)
        h32 = place(stage_at, "h32", [P, 2, GT], F32)
        xaw = place(base, "xaw", [P, 2, KD, D], F32R)
        idf = place(base, "idf", [P, P], F32)
        idb = place(base, "idb", [P, P], BF16)
        tri = place(base, "tri", [P, Q, S], BF16)
        lns = place(base, "lns", [P, D], F32)
        s3 = place(base, "s3", [P, D], F32)
        st6 = place(base, "st6", [P, Q, 6], F32)
        mv = place(base, "mv", [P, Q, 2], F32)
        ve = place(base, "ve", [P, Q], F32)
        rstd = place(base, "rstd", [P, Q], F32)
        mhalf = place(base, "mhalf", [P, Q], F32)
        h6 = place(base, "h6", [P, 6], F32)
        hmv = place(base, "hmv", [P, 2, 2], F32)
        hve = place(base, "hve", [P, 2], F32)
        hrs = place(base, "hrs", [P, 2], F32)
        scol = place(base, "scol", [P, 4, MD], F32)
        diag = place(base, "diag", [P, KD], F32)
        facc = place(base, "facc", [P, FLAG_ITEMS], F32)
        fsum = place(base, "fsum", [P, 1], F32)
        onec = place(base, "onec", [P, 1], F32)
        fint = place(base, "fint", [1, 1], I32)
        ot = place(base, "ot", [P, 2, D], F32)
        den = place(base, "den", [P, 3, Q], F32)
        smx = place(base, "smx", [P, Q], F32)
        nmx = place(base, "nmx", [P, Q], F32)
        rsm = place(base, "rsm", [P, Q], F32)
        rrs = place(base, "rrs", [P, Q], F32)
        r1 = [base[0]]
        l0 = place(r1, "l0", [P, 2, 2, KD, HB], F32R)
        l0d = place(r1, "l0d", [P, 2, MB, D], F32R)
        kT = place(r1, "kT", [P, 2, 2, KD, GT], F32R)
        V = place(r1, "V", [P, 2, Q, NH, VW], F32)
        raw = place([r1[0]], "raw", [P, 2, HB // 2], F32)
        mk = place(r1, "mk", [P, Q, S], I32)
        c1 = [base[0]]
        kstC = place(c1, "kstC", [P, KD, GT], F32)
        qr = place(c1, "qr", [P, KD, GT], F32)
        kr = place(c1, "kr", [P, KD, GT], F32)
        mf = place(c1, "mf", [P, Q, S], F32)
        sc = place(c1, "sc", [P, Q, S], F32)
        al = place(c1, "al", [P, Q, S], F32)
        alT = place(c1, "alT", [P, Q, S], F32)
        assert c1[0] <= base[0] + 36 * 1024
        d1 = [base[0]]
        hA = place(d1, "hA", [P, 2, MD, GT], F32R)
        hBt = place(d1, "hBt", [P, 2, MD, GT], F32R)
        r2 = [max(r1[0], d1[0])]
        r2b = [r2[0] + MD * HD * 4]
        h1 = place([r2[0]], "h1", [P, MD, HD], F32R)
        h2 = place([r2b[0]], "h2", [P, MD, HD], F32R)
        a2 = [r2[0]]
        Qb = place(a2, "Qb", [P, 2, 2, KD, Q, S], F32R)
        kstA = place(a2, "kstA", [P, KD, GT], F32)
        Dt = place(a2, "Dt", [P, 2, Q, S], F32)
        Ct = place(a2, "Ct", [P, 2, Q, S], F32)
        gw = place(a2, "gw", [P, 2, 2 * KD, P], F32R)
        assert a2[0] <= r2b[0]
        a3 = [r2b[0]]
        Rr = place(a3, "Rr", [RA, 2, NH, Q, S], BF16)
        Lr = place(a3, "Lr", [RA, 2, 2, Q, S], BF16)
        gsb = place(a3, "gsb", [2 * NH, GT], F32)
        NR = NH * Q
        gi = place(a3, "gi", [NR, S], F32)
        gf = place(a3, "gf", [NR, S], F32)
        gb = place(a3, "gb", [NR, 2], F32)
        fab = place(a3, "fab", [NR, S], F32)
        fmn = place(a3, "fmn", [NR, S], F32)
        fl = place(a3, "fl", [NR, S], F32)
        one_r = place(a3, "one_r", [NR, S], F32)
        cs = place(a3, "cs", [NR, S], F32)
        Z = place(a3, "Z", [NR, 2, S], F32)
        zr = place(a3, "zr", [NR, 2, S], F32)
        zp = place(a3, "zp", [NR, 3, 2, S], BF16)
        Er = place(a3, "Er", [NR, S], F32)
        ET = place(a3, "ET", [P, 2, NR], F32)
        hm = place(a3, "hm", [P, 2, NH, DH], F32)
        graw = place(a3, "graw", [P, 3 * KD, 2 * NH], F32)
        gsum = place(a3, "gsum", [P, KD, 2 * NH], F32)
        assert a3[0] <= nc.sbuf_usable_end, a3[0]
        b3 = [r2b[0]]
        hB = place(b3, "hB", [P, 2, MB, GT], F32R)
        silB = place(b3, "silB", [P, 2, GT], F32)
        hfB = place(b3, "hfB", [P, 2, GT], F32)
        assert b3[0] <= nc.sbuf_usable_end, b3[0]

        ps = es.enter_context(nc.psum_tensor("ps", [P, 8, GT], F32))
        TR, EX, QK, PV = 0, 2, 4, 6
        GB, UB, OB = 2, 4, 6
        PJ, SCB, ATB = 2, 4, 5

        names = """x_first x_rest ctxT_ld kst_free v_ld v_free gw_ld consts mask_ld mask_free raw_ld raw_used hi_ld
            gw_lo gw_cast const_set mv_ready rstd_ready xn_ready tr_done xhi_done xlo_done x_free
            khi_done klo_done gate_done gate_copied gate_moved ab_ready ln_ready ncs_ready er_ready z_ready
            z_moved er_turned et_ready expo_done d_ready qk_done c_ready pv_done pv_used hstat_ready hrs_ready
            flag_used flag_sums flag_tot flag_ready l0_lo gu_done silu_ready hf_ready hhi_ready hlo_ready
            down_done xA_done xB_done kr_done qr_done krc_done qrc_done sc_done sm_ready al_ready at_done at_ready
            av_done xC_done d_pre d_sil d_h32 d_hi d_lo d_act d_out xD_done ring_ld ring_free
            idb_ready dh_own ot_ready dve_prep dve_a2 dve_unit dve_b dve_c dve_d pool_own act_own out_done pe_own w_ld h1_ld h2_ld""".split()
        s = {n: sem(n) for n in names}
        qb_ld = [sem(f"qb_ld{i}") for i in range(2)]
        flag_ld = [sem(f"flag_ld{i}") for i in range(2)]
        ring_ld = [sem(f"ring_ld{i}") for i in range(RING)]
        raw_ld = [sem(f"raw_ld{i}") for i in range(2)]

        def tr_bank(c):
            return ps[:, TR + c, :]

        def move_rows(sp, u):
            for part in range(3):
                sp.dma_start(Rr[part:part + 1, u, :, :, :], zp[:, part, 0, :]).then_inc(s["z_moved"], 16)
                for quad in range(2):
                    sp.dma_start(Lr[3 + part * Q:3 + part * Q + Q, u, quad, :, :],
                                 zp[quad * Q * Q:(quad + 1) * Q * Q, part, 1, :]).then_inc(s["z_moved"], 16)

        block = es.enter_context(nc.Block())

        @block.sync
        def _(sp):
            sp.dma_start(x[:, 0:Q, :], x_in[0:Q].rearrange("b s d -> s b d")).then_inc(s["x_first"], 16)
            sp.dma_start(kstA[:, :, :], ctxT_in[:, :, 0:GT]).then_inc(s["ctxT_ld"], 16)
            sp.dma_start(graw[:, :, :], gw_in).then_inc(s["gw_ld"], 16)
            sp.dma_start(idf[:, :], ident_in).then_inc(s["consts"], 16)
            sp.dma_start(gb[:, :], gb_in).then_inc(s["consts"], 16)
            for u in range(2):
                sp.dma_start(Rr[3:RA, u, :, :, :], ones_rows_in[3:RA]).then_inc(s["consts"], 16)
                sp.dma_start(Lr[0:3, u, :, :, :], ones_rows_in[0:3, 0:2]).then_inc(s["consts"], 16)
            sp.dma_start(tri[:, :, :], tri_in).then_inc(s["consts"], 16)
            sp.dma_start(lns[:, :], lns_in.partition_broadcast(P)).then_inc(s["consts"], 16)
            sp.dma_start(s3[:, :], s3_in.partition_broadcast(P)).then_inc(s["consts"], 16)
            sp.dma_start(scol[:, :, :], s_cols_in).then_inc(s["consts"], 16)
            sp.dma_start(diag[:, :], diag_in).then_inc(s["consts"], 16)
            for g in range(1, G):
                sp.dma_start(x[:, Q * g:Q * g + Q, :], x_in[Q * g:Q * g + Q].rearrange("b s d -> s b d"))\
                    .then_inc(s["x_rest"], 16)
            sp.wait_ge(s["const_set"], 2)
            sp.wait_ge(s["z_ready"], 1)
            move_rows(sp, 0)
            with sp.Fori(0, 2) as i:
                for u in range(2):
                    g = 2 * i + u
                    gn = g + 1 if u == 0 else G // 2
                    for q in range(Q):
                        sp.dma_start(V[:, u, q, :, 0:DH],
                                     ctx_in[Q * g + q].rearrange("t (h d) -> t h d", d=DH))\
                            .then_inc(s["v_ld"], 16)
                    for q in range(Q):
                        if q == 1:
                            def next_ctx():
                                sp.wait_ge(s["klo_done"], g + 1)
                                sp.dma_start(kstA[:, :, :], ctxT_in[:, :, bass.ds(gn * GT, GT)])\
                                    .then_inc(s["ctxT_ld"], 16)
                            if u == 0:
                                next_ctx()
                            else:
                                with sp.If(i < 1):
                                    next_ctx()
                        if q == 0:
                            sp.wait_ge(s["xlo_done"], KD * (g + 1))
                            sp.wait_ge(s["xhi_done"], KD * (g + 1))
                        sp.wait_ge(s["qk_done"], UN * g + 2 * q + 2)
                        for j in range(Q):
                            sp.dma_start(Qb[DH * j:DH * j + DH, q % 2, :, :, j, :].bitcast(F32),
                                         xT[DH * j:DH * j + DH, u, :, :, q * S:(q + 1) * S].bitcast(F32))\
                                .then_inc(qb_ld[q % 2], 16)
                        for k in (2 * q, 2 * q + 1):
                            sp.wait_ge(s["flag_used"], UN * g + k + 1)
                            sp.dma_start(stage[:, k % 2, 0:FLAG_W],
                                         w_all_in[:, bass.ds((UN * g + k) * FLAG_W, FLAG_W)])\
                                .then_inc(flag_ld[k % 2], 16)

                    def parts_out():
                        sp.wait_ge(s["z_ready"], gn + 1)
                        move_rows(sp, 1 - u)
                    if u == 0:
                        parts_out()
                    else:
                        with sp.If(i < 1):
                            parts_out()
            sp.wait_ge(s["down_done"], Q * G)
            with sp.Fori(0, 2) as i:
                for u in range(2):
                    g = 2 * i + u
                    gn = g + 1 if u == 0 else G // 2
                    sp.wait_ge(s["klo_done"], G + g)
                    sp.dma_start(kstC[:, :, :], ctxT_in[:, :, bass.ds(g * GT, GT)]).then_inc(s["ctxT_ld"], 16)
                    sp.wait_ge(s["av_done"], Q * g + Q)
                    for q in range(Q):
                        sp.dma_start(V[:, u, q, :, 0:DH],
                                     ctx_in[Q * g + q].rearrange("t (h d) -> t h d", d=DH))\
                            .then_inc(s["v_ld"], 16)
                    sp.wait_ge(s["mask_free"], g + 1)
                    sp.dma_start(mk[:, :, :], mask_in[bass.ds(Q * g, Q), :].partition_broadcast(P))\
                        .then_inc(s["mask_ld"], 16)
            sp.wait_ge(s["flag_ready"], 1)
            fl_reg = sp.value_load(fint[0:1, 0:1])
            with sp.If(fl_reg > 0):
                sp.wait_ge(s["w_ld"], 48)
                with sp.Fori(0, G) as g:
                    n = 0

                    def block_in(dst, src):
                        nonlocal n
                        sp.wait_ge(s["ring_free"], g * ITEMS_G + n + 1)
                        sp.dma_start(dst, src).then_inc(ring_ld[n % RING], 16)
                        n += 1
                    for m in range(MD):
                        v = w_all_in[:, SEC_W1:SEC_W3].rearrange("p (a f) -> p a f", a=2 * KD)
                        block_in(ring[:, n % RING, 0:2 * KD, :], v[:, :, m * P:(m + 1) * P])
                    for sec in (SEC_H1, SEC_H2):
                        v = w_all_in[:, sec:sec + MD * HD].rearrange("p (a f) -> p a f", a=MD)
                        for m in range(MD):
                            block_in(ring[:, n % RING, :, :], v[:, :, m * P:(m + 1) * P])
                    for half in range(2):
                        v = w_all_in[:, SEC_W3 + half * HD:SEC_W3 + (half + 1) * HD]
                        block_in(ring[:, n % RING, :, :], v.rearrange("p (a f) -> p a f", a=MD))

        @block.gpsimd
        def _(pool):
            own = [0]

            def step(ins):
                ins.then_inc(s["pool_own"], 1)
                own[0] += 1

            def settle():
                pool.wait_ge(s["pool_own"], own[0])

            step(nc.gpsimd.memset(mhalf[:, :], -0.5))
            step(nc.gpsimd.memset(gw[:, :, :, :].bitcast(F32), 0.0))
            pool.wait_ge(s["gw_ld"], 16)
            step(nc.gpsimd.tensor_tensor(gsum[:, :, :], graw[:, KD:2 * KD, :], graw[:, 2 * KD:3 * KD, :], ALU.add))
            settle()
            W = 2 * NH
            step(nc.gpsimd.tensor_copy(gw[:, 0, 0:KD, 0:W], graw[:, 0:KD, :]))
            step(nc.gpsimd.tensor_copy(gw[:, 0, KD:2 * KD, 0:W], gsum[:, :, :]))
            settle()
            nc.gpsimd.tensor_tensor(gw[:, 1, 0:KD, 0:W], graw[:, 0:KD, :], gw[:, 0, 0:KD, 0:W], ALU.subtract)\
                .then_inc(s["gw_lo"], 1)
            nc.gpsimd.tensor_tensor(gw[:, 1, KD:2 * KD, 0:W], gsum[:, :, :], gw[:, 0, KD:2 * KD, 0:W], ALU.subtract)\
                .then_inc(s["gw_lo"], 1)

            def inv_root(n):
                pool.wait_ge(s["mv_ready"], n + 1)
                nc.gpsimd.tensor_tensor(rstd[:, :], ve[:, :], mhalf[:, :], ALU.pow).then_inc(s["rstd_ready"], 1)

            def k_lo(n, kst, u):
                pool.wait_ge(s["khi_done"], n + 1)
                nc.gpsimd.tensor_tensor(kT[:, u, 1, :, :], kst[:, :, :], kT[:, u, 0, :, :], ALU.subtract)\
                    .then_inc(s["klo_done"], 1)

            inv_root(0)
            k_lo(0, kstA, 0)
            pool.dma_start(l0[:, 0, :, :, :], l0gu_in).then_inc(s["hi_ld"], 16)
            pool.dma_start(l0d[:, 0, :, :], l0d_in).then_inc(s["hi_ld"], 16)
            pool.dma_start(xaw[:, 0, :, :], xaw_in).then_inc(s["hi_ld"], 16)
            pool.dma_start(w1[:, :, :], w_all_in[:, SEC_W1:SEC_W2].rearrange("p (k f) -> p k f", k=KD))\
                .then_inc(s["w_ld"], 16)
            pool.dma_start(w2[:, :, :], w_all_in[:, SEC_W2:SEC_W3].rearrange("p (k f) -> p k f", k=KD))\
                .then_inc(s["w_ld"], 16)
            pool.dma_start(w3[:, :, :], w_all_in[:, SEC_W3:SEC_H1].rearrange("p (k f) -> p k f", k=MD))\
                .then_inc(s["w_ld"], 16)
            pool.wait_ge(s["hi_ld"], 48)
            LC = HB // 2
            RAW = [(l0gu_in[:, a, c, h * LC:(h + 1) * LC], l0[:, 0, a, c, h * LC:(h + 1) * LC],
                    l0[:, 1, a, c, h * LC:(h + 1) * LC]) for a in range(2) for c in range(KD) for h in range(2)]
            RAW += [(l0d_in[:, m, :], l0d[:, 0, m, :], l0d[:, 1, m, :]) for m in range(MB)]
            RAW += [(xaw_in[:, c, :], xaw[:, 0, c, :], xaw[:, 1, c, :]) for c in range(KD)]
            raws = (raw[:, 0, :], raw[:, 1, :])
            assert len(RAW) == NRAW
            for n in range(2):
                src, hi, lo = RAW[n]
                pool.dma_start(raws[n][:, 0:lo.shape[-1]], src).then_inc(raw_ld[n], 16)
            done = 0

            def lows(k):
                nonlocal done
                for n in range(done, min(done + k, NRAW)):
                    src, hi, lo = RAW[n]
                    pool.wait_ge(raw_ld[n % 2], 16 * (n // 2 + 1))
                    nc.gpsimd.tensor_tensor(lo, raws[n % 2][:, 0:hi.shape[-1]], hi, ALU.subtract)\
                        .then_inc(s["l0_lo"], 1)
                    if n + 2 < NRAW:
                        pool.wait_ge(s["l0_lo"], n + 1)
                        src, hi, lo = RAW[n + 2]
                        pool.dma_start(raws[n % 2][:, 0:hi.shape[-1]], src).then_inc(raw_ld[n % 2], 16)
                done = min(done + k, NRAW)

            def h_root(b):
                pool.wait_ge(s["hstat_ready"], b + 1)
                nc.gpsimd.tensor_tensor(hrs[:, 0:1], hve[:, 0:1], mhalf[:, 0:1], ALU.pow)\
                    .then_inc(s["hrs_ready"], 1)

            lows(NRAW)
            with pool.Fori(0, 2) as i:
                for u in range(2):
                    g = 2 * i + u
                    gn = g + 1 if u == 0 else G // 2
                    inv_root(g + 1)
                    if u == 0:
                        k_lo(gn, kstA, 1 - u)
                    else:
                        with pool.If(i < 1):
                            k_lo(gn, kstA, 1 - u)
                    for q in range(Q):
                        h_root(Q * g + q)
            pool.wait_ge(s["xA_done"], NB)
            for k in range(MD):
                pool.dma_start(h1[:, k, :], w_all_in[:, SEC_H1 + k * HD:SEC_H1 + (k + 1) * HD])\
                    .then_inc(s["h1_ld"], 16)
            with pool.Fori(0, G) as g:
                inv_root(g + G + 1)
            pool.wait_ge(s["down_done"], Q * G)
            for k in range(MD):
                pool.dma_start(h2[:, k, :], w_all_in[:, SEC_H2 + k * HD:SEC_H2 + (k + 1) * HD])\
                    .then_inc(s["h2_ld"], 16)
            with pool.Fori(0, 2) as i:
                for u in range(2):
                    g = 2 * i + u
                    gn = g + 1 if u == 0 else G // 2
                    k_lo(G + g, kstC, u)
                    inv_root(g + 2 * G + 1)
            with pool.Fori(0, 2) as i:
                for u in range(2):
                    g = 2 * i + u
                    gn = g + 1 if u == 0 else G // 2
                    if u == 0:
                        inv_root(3 * G + gn)
                    else:
                        with pool.If(i < 1):
                            inv_root(3 * G + gn)
                    for q in range(Q):
                        pool.wait_ge(s["xD_done"], 2 + Q * g + q + 1)
                        pool.dma_start(out[Q * g + q], x[:, Q * g + q, :]).then_inc(s["out_done"], 16)
            pool.wait_ge(s["out_done"], 16 * NB)

        @block.tensor
        def _(pe):
            mm = nc.tensor.matmul
            pe.sem_inc(s["qk_done"], 4)
            pe.sem_inc(s["pv_done"], 2)
            pe.sem_inc(s["av_done"], 2 * Q)
            pe.sem_inc(s["ring_free"], RING)

            def turn_x(n, first=False):
                pe.wait_ge(s["xn_ready"], n + 1)
                if not first:
                    pe.wait_ge(s["xlo_done"], KD * n)
                for c in range(KD):
                    for q in range(Q):
                        last = nc.tensor.transpose(ps[:, TR + c, q * S:(q + 1) * S], xn[:, q, c * P:(c + 1) * P],
                                                   idf[:, :])
                last.then_inc(s["tr_done"], 1)

            def three(o, lhs, rhs, first, last):
                mm(o, lhs(0), rhs(0), start=first, stop=False)
                mm(o, lhs(0), rhs(1), start=False, stop=False)
                return mm(o, lhs(1), rhs(0), start=False, stop=last)

            def gates(g, u):
                pe.wait_ge(s["klo_done"], g + 1)
                pe.wait_ge(s["xlo_done"], KD * (g + 1))
                for c in range(2 * KD):
                    src = (lambda p, c=c: xT[:, u, p, c, :]) if c < KD else (lambda p, c=c: kT[:, u, p, c - KD, :])
                    last = three(tr_bank(0), lambda p, c=c: gw[:, p, c, :], src, c == 0, c == 2 * KD - 1)
                last.then_inc(s["gate_done"], 1)

            def turn_e(g):
                pe.wait_ge(s["er_ready"], g + 1)
                pe.sem_inc(s["pe_own"], 1)
                nc.tensor.transpose(ps[:, TR + 1, 0:NR], Er[:, :], idf[0:NR, 0:NR]).then_inc(s["er_turned"], 1)

            def expo(g, u, k):
                q, quad = k // 2, k % 2
                n = UN * g + k
                if k == 0:
                    pe.wait_ge(s["z_moved"], 144 * (g + 1))
                pe.wait_ge(s["d_ready"], n + 1)
                mm(ps[:, EX + quad, :], Lr[:, u, quad, q, :], Rr[:, u, Q * quad:Q * quad + Q, q, :],
                   start=True, stop=False)
                mm(ps[:, EX + quad, :], idb[:, :], tri[:, :, :], start=False, stop=True)\
                    .then_inc(s["expo_done"], 1)

            def qk(g, u, k):
                q, quad = k // 2, k % 2
                n = UN * g + k
                if quad == 0:
                    pe.wait_ge(qb_ld[q % 2], 64 * (2 * g + q // 2 + 1))
                pe.wait_ge(s["c_ready"], n + 1)
                three(ps[:, QK + quad, :], lambda p: kT[:, u, p, quad, q * S:(q + 1) * S],
                      lambda p: Qb[:, q % 2, p, quad, :, :], True, True).then_inc(s["qk_done"], 1)

            def pv(g, u, k):
                q, quad = k // 2, k % 2
                n = UN * g + k
                if k == 0:
                    pe.wait_ge(s["v_ld"], 64 * (g + 1))
                pe.wait_ge(s["c_ready"], n + 3)
                pe.wait_ge(s["pv_used"], n + 1)
                for j in range(Q):
                    lo = Q * quad + j - 2 * quad
                    last = mm(ps[:, PV + quad, j * PVW:(j + 1) * PVW], Ct[:, quad, j, :], V[:, u, q, lo:lo + 3, :],
                              start=True, stop=True)
                last.then_inc(s["pv_done"], 1)

            pe.wait_ge(s["consts"], CONSTS)
            turn_x(0, True)
            pe.wait_ge(s["gw_lo"], 2)
            pe.wait_ge(s["idb_ready"], 1)
            gates(0, 0)
            turn_e(0)
            with pe.Fori(0, 2) as i:
                for u in range(2):
                    g = 2 * i + u
                    gn = g + 1 if u == 0 else G // 2
                    more = (lambda f: f()) if u == 0 else (lambda f: if_more(pe, i, f))
                    for k in range(UN):
                        if k == 2:
                            pe.wait_ge(s["gate_copied"], g + 1)
                            pe.wait_ge(s["et_ready"], g + 1)
                            turn_x(g + 1)
                        if k == 4:
                            more(lambda: gates(gn, 1 - u))
                        expo(g, u, k)
                        qk(g, u, k)
                        if k:
                            pv(g, u, k - 1)
                    pv(g, u, UN - 1)
                    more(lambda: turn_e(gn))

            pe.wait_ge(s["flag_sums"], 1)
            pe.wait_ge(s["pv_used"], UN * G + 2)
            mm(ps[0:1, OB, 0:1], fsum[:, :], onec[:, :], start=True, stop=True).then_inc(s["flag_tot"], 1)
            pe.wait_ge(s["l0_lo"], NRAW)
            pe.wait_ge(s["flag_ready"], 1)
            with pe.Fori(0, 2) as i:
                for u in range(2):
                    g = 2 * i + u
                    gn = g + 1 if u == 0 else G // 2
                    pe.wait_ge(s["xlo_done"], KD * (G + g + 1))
                    for m in range(MB):
                        n = MB * g + m
                        if m == 3:
                            turn_x(G + g + 1)
                        for a, (bank, used) in enumerate(((GB, "silu_ready"), (UB, "hf_ready"))):
                            pe.wait_ge(s[used], n + 1)
                            for c in range(KD):
                                last = three(ps[:, bank + m % 2, :],
                                             lambda p: l0[:, p, a, c, m * P:(m + 1) * P],
                                             lambda p: xT[:, u, p, c, :], c == 0, c == KD - 1)
                        last.then_inc(s["gu_done"], 1)
                    for q in range(Q):
                        pe.wait_ge(s["xB_done"], Q * g + q + 1)
                        for k in range(MB):
                            if q == 0:
                                pe.wait_ge(s["hlo_ready"], MB * g + k + 3)
                            last = three(ps[:, OB + q % 2, 0:D], lambda p: hB[:, p, k, q * S:(q + 1) * S],
                                         lambda p: l0d[:, p, k, :], k == 0, k == MB - 1)
                        last.then_inc(s["down_done"], 1)

            pe.wait_ge(s["xB_done"], NB + 2)
            with pe.Fori(0, 2) as i:
                for u in range(2):
                    g = 2 * i + u
                    gn = g + 1 if u == 0 else G // 2
                    pe.wait_ge(s["klo_done"], G + g + 1)
                    for m in range(KD):
                        pe.wait_ge(s["qrc_done"], KD * g + m + 1)
                        for c in range(KD):
                            last = three(ps[:, PJ + m, :], lambda p: xaw[:, p, c, m * P:(m + 1) * P],
                                         lambda p: kT[:, u, p, c, :], c == 0, c == KD - 1)
                        last.then_inc(s["kr_done"], 1)
                    pe.wait_ge(s["xlo_done"], KD * (2 * G + g + 1))
                    for m in range(KD):
                        pe.wait_ge(s["krc_done"], KD * g + m + 1)
                        for c in range(KD):
                            last = three(ps[:, PJ + m, :], lambda p: xaw[:, p, c, m * P:(m + 1) * P],
                                         lambda p: xT[:, u, p, c, :], c == 0, c == KD - 1)
                        last.then_inc(s["qr_done"], 1)
                    pe.wait_ge(s["qrc_done"], KD * g + 2 * KD)
                    pe.wait_ge(s["sm_ready"], g + 1)
                    for q in range(Q):
                        for c in range(KD):
                            last = mm(ps[:, SCB, q * S:(q + 1) * S], qr[:, c, q * S:(q + 1) * S],
                                      kr[:, c, q * S:(q + 1) * S], start=(c == 0), stop=(c == KD - 1))
                    last.then_inc(s["sc_done"], 1)
                    turn_x(2 * G + g + 1)
                    pe.wait_ge(s["at_ready"], g + 1)
                    for q in range(Q):
                        pe.wait_ge(s["al_ready"], Q * g + q + 1)
                        last = nc.tensor.transpose(ps[:, ATB, q * S:(q + 1) * S], al[:, q, :], idf[:, :])
                    last.then_inc(s["at_done"], 1)
                    pe.wait_ge(s["at_ready"], g + 2)
                    pe.wait_ge(s["v_ld"], 64 * (G + g + 1))
                    for q in range(Q):
                        pe.wait_ge(s["xC_done"], Q * g + q + 1)
                        mm(ps[:, OB + q % 2, 0:D].rearrange("p (h d) -> p h d", d=DH), alT[:, q, :],
                           V[:, u, q, :, 0:DH], start=True, stop=True).then_inc(s["av_done"], 1)

            pe.wait_ge(s["xC_done"], NB + 2)
            pe.wait_ge(s["w_ld"], 48)
            pe.wait_ge(s["h1_ld"], 16 * MD)
            pe.wait_ge(s["h2_ld"], 16 * MD)

            def wide(o, lhs, rhs, k, n_k, general):
                for p in range(2):
                    a, b = lhs(k, p), rhs(k, p)
                    if general:
                        a, b = a.bitcast(F32), b.bitcast(F32)
                    last = mm(o, a, b, start=(k == 0 and p == 0), stop=(k == n_k - 1 and p == 1))
                return last

            def stage_d(general):
                with pe.Fori(0, 2) as i:
                    for u in range(2):
                        g = 2 * i + u
                        gn = g + 1 if u == 0 else G // 2
                        d0 = 3 * MD * g
                        item = 0

                        def block_wait():
                            if general:
                                pe.wait_ge(ring_ld[item % RING], 16 * ((ITEMS_G // RING) * g + item // RING + 1))

                        def block_free(last, name):
                            nonlocal item
                            last.then_inc(s[name], 1)
                            if general:
                                mm(ps[0:1, TRASH, 0:1], onec[:, :], onec[:, :], start=True, stop=True)\
                                    .then_inc(s["ring_free"], 1)
                            item += 1

                        pe.wait_ge(s["xlo_done"], KD * (3 * G + g + 1))
                        for m in range(MD):
                            block_wait()
                            if m < 2:
                                pe.wait_ge(s["d_act"], d0 + 1 + m)
                            else:
                                pe.wait_ge(s["d_act"], d0 + m + 1)
                                pe.wait_ge(s["d_h32"], MD * g + m + 1)
                            for a, (w, bank) in enumerate(((w1, 2), (w2, 4))):
                                for k in range(KD):
                                    if general:
                                        lhs = lambda k, p: ring[:, item % RING, a * KD + k, :]
                                    else:
                                        lhs = lambda k, p: w[:, k, m * P:(m + 1) * P]
                                    last = wide(ps[:, bank + m % 2, :], lhs, lambda k, p: xT[:, u, p, k, :],
                                                k, KD, general)
                            block_free(last, "d_pre")
                        for L, w in enumerate((h1, h2)):
                            src = (hA, hBt)[(L + u) % 2]
                            for m in range(MD):
                                if L == 1 and m == 4:
                                    nxt = lambda: turn_x(3 * G + gn)
                                    nxt() if u == 0 else if_more(pe, i, nxt)
                                block_wait()
                                idx = MD * (L + 1) + m
                                if L == 0 and m == 0:
                                    pe.wait_ge(s["d_act"], d0 + 2 + MD - 1)
                                if idx >= 12:
                                    pe.wait_ge(s["d_act"], d0 + 2 + idx - 3)
                                for k in range(MD):
                                    if m == 0:
                                        pe.wait_ge(s["d_lo"], d0 + 2 + MD * L + k + 1)
                                    if general:
                                        lhs = lambda k, p: ring[:, item % RING, k, :]
                                    else:
                                        lhs = lambda k, p: w[:, k, m * P:(m + 1) * P]
                                    last = wide(ps[:, 2 + m % 4, :], lhs, lambda k, p: src[:, p, k, :], k, MD, general)
                                block_free(last, "d_pre")
                        src = (hA, hBt)[u]
                        for half in range(2):
                            block_wait()
                            item += 1
                        item -= 2
                        for q in range(Q):
                            pe.wait_ge(s["xD_done"], Q * g + q + 1)
                            for k in range(MD):
                                if q == 0:
                                    pe.wait_ge(s["d_lo"], d0 + 2 + 2 * MD + k + 1)
                                if general:
                                    rhs = lambda k, p: ring[:, (item + k // Q) % RING, 2 * (k % Q):2 * (k % Q) + 2, :]
                                else:
                                    rhs = lambda k, p: w3[:, k, :]
                                last = wide(ps[:, OB + q % 2, 0:D], lambda k, p: src[:, p, k, q * S:(q + 1) * S],
                                            rhs, k, MD, general)
                            last.then_inc(s["d_out"], 1)
                        if general:
                            for half in range(2):
                                mm(ps[0:1, TRASH, 0:1], onec[:, :], onec[:, :], start=True, stop=True)\
                                    .then_inc(s["ring_free"], 1)

            flag_reg = pe.value_load(fint[0:1, 0:1])
            with pe.If(flag_reg > 0):
                stage_d(True)
            with pe.Else():
                stage_d(False)

        @block.scalar
        def _(act):
            fn = nc.scalar.activation
            act.sem_inc(s["flag_used"], 2)
            act.sem_inc(s["d_ready"], 2)
            act.sem_inc(s["silu_ready"], 2)
            act.sem_inc(s["d_act"], 2)

            def x_hi(n, par):
                for c in range(KD):
                    act.wait_ge(s["tr_done"], n + 1)
                    fn(xT[:, par, 0, c, :], tr_bank(c), ACT.Copy).then_inc(s["xhi_done"], 1)

            def k_hi(n, kst, par):
                act.wait_ge(s["ctxT_ld"], 16 * (n + 1))
                fn(kT[:, par, 0, :, :], kst[:, :, :], ACT.Copy).then_inc(s["khi_done"], 1)

            def gate_copy(g):
                act.wait_ge(s["gate_done"], g + 1)
                fn(gsb[:, :], ps[0:2 * NH, TR, :], ACT.Copy).then_inc(s["gate_copied"], 1)
                act.wait_ge(s["gate_copied"], g + 1)
                act.dma_start(gi[:, :], gsb[0:NH, :].rearrange("h (q t) -> h q t", q=Q)).then_inc(s["gate_moved"], 16)
                act.dma_start(gf[:, :], gsb[NH:2 * NH, :].rearrange("h (q t) -> h q t", q=Q))\
                    .then_inc(s["gate_moved"], 16)

            def log_part(g):
                act.wait_ge(s["ab_ready"], g + 1)
                fn(fl[:, :], fab[:, :], ACT.Exp, scale=-1.0).then_inc(s["act_own"], 1)
                act.wait_ge(s["act_own"], g + 1)
                fn(fl[:, :], fl[:, :], ACT.Ln, bias=1.0).then_inc(s["ln_ready"], 1)

            def floor_part(g):
                act.wait_ge(s["ncs_ready"], g + 1)
                fn(Er[:, :], Er[:, :], ACT.Exp).then_inc(s["er_ready"], 1)

            k_hi(0, kstA, 0)
            x_hi(0, 0)
            gate_copy(0)
            log_part(0)
            floor_part(0)
            with act.Fori(0, 2) as i:
                for u in range(2):
                    g = 2 * i + u
                    gn = g + 1 if u == 0 else G // 2
                    more = (lambda f: f()) if u == 0 else (lambda f: if_more(act, i, f))
                    for k in range(UN):
                        n = UN * g + k
                        quad = k % 2
                        act.wait_ge(s["expo_done"], n + 1)
                        act.wait_ge(s["c_ready"], n + 1)
                        fn(Dt[:, quad, :, :], ps[:, EX + quad, :].rearrange("p (j t) -> p j t", j=Q), ACT.Exp,
                           scale=-1.0).then_inc(s["d_ready"], 1)
                        if k == 1:
                            more(lambda: k_hi(gn, kstA, 1 - u))
                        if k == 2:
                            x_hi(g + 1, 1 - u)
                        if k == 4:
                            more(lambda: gate_copy(gn))
                        if k == 6:
                            more(lambda: log_part(gn))
                        if k == 7:
                            more(lambda: floor_part(gn))
                        act.wait_ge(flag_ld[k % 2], 16 * (Q * g + k // 2 + 1))
                        view = stage[:, k % 2, 0:FLAG_W]
                        low = view.bitcast(U16).rearrange("p (w a) -> p w a", a=2)[:, :, 0:1]
                        fn(view.rearrange("p (w a) -> p w a", a=1), low, ACT.Copy,
                           accum_out=facc[:, bass.ds(n, 1)]).then_inc(s["flag_used"], 1)
            act.wait_ge(s["flag_used"], FLAG_ITEMS + 2)
            fn(facc[:, :], facc[:, :], ACT.Copy, accum_out=fsum[:, :]).then_inc(s["flag_sums"], 1)

            act.wait_ge(s["xA_done"], NB)
            with act.Fori(0, 2) as i:
                for u in range(2):
                    g = 2 * i + u
                    gn = g + 1 if u == 0 else G // 2
                    for m in range(MB + 1):
                        n = MB * g + m
                        if m < MB:
                            act.wait_ge(s["gu_done"], n + 1)
                            act.wait_ge(s["hf_ready"], n + 1)
                            fn(silB[:, m % 2, :], ps[:, GB + m % 2, :], ACT.Silu, scale=SCALE_B)\
                                .then_inc(s["silu_ready"], 1)
                        if m:
                            act.wait_ge(s["hf_ready"], n + 2)
                            fn(hB[:, 0, m - 1, :], hfB[:, (m - 1) % 2, :], ACT.Copy).then_inc(s["hhi_ready"], 1)
                        if m == 3:
                            x_hi(G + g + 1, 1 - u)

            act.wait_ge(s["down_done"], NB)
            with act.Fori(0, 2) as i:
                for u in range(2):
                    g = 2 * i + u
                    gn = g + 1 if u == 0 else G // 2
                    k_hi(G + g, kstC, u)
                    for m in range(KD):
                        act.wait_ge(s["kr_done"], KD * g + m + 1)
                        fn(kr[:, m, :], ps[:, PJ + m, :], ACT.Relu).then_inc(s["krc_done"], 1)
                    x_hi(2 * G + g + 1, 1 - u)
                    act.wait_ge(s["sm_ready"], g + 2)
                    for q in range(Q):
                        fn(al[:, q, :], sc[:, q, :], ACT.Exp, bias=nmx[:, q:q + 1], accum_out=rsm[:, q:q + 1])\
                            .then_inc(s["al_ready"], 1)

            act.wait_ge(s["av_done"], NB + 2 * Q)
            with act.Fori(0, 2) as i:
                for u in range(2):
                    g = 2 * i + u
                    gn = g + 1 if u == 0 else G // 2
                    d0 = 3 * MD * g
                    dst = (hA, hBt)[u]
                    for m in range(MD + 1):
                        if m < MD:
                            act.wait_ge(s["d_pre"], d0 + m + 1)
                            act.wait_ge(s["d_h32"], MD * g + m + 1)
                            fn(silD[:, m % 2, :], ps[:, 2 + m % 2, :], ACT.Silu, scale=scol[:, 0, m:m + 1])\
                                .then_inc(s["d_act"], 1)
                        if m:
                            act.wait_ge(s["d_h32"], MD * g + m + 2)
                            fn(dst[:, 0, m - 1, :], h32[:, (m - 1) % 2, :], ACT.Copy).then_inc(s["d_hi"], 1)
                    for idx in range(MD, 3 * MD):
                        m, L = idx % MD, idx // MD
                        if L == 2 and m == 4:
                            nxt = lambda: x_hi(3 * G + gn, 1 - u)
                            nxt() if u == 0 else if_more(act, i, nxt)
                        act.wait_ge(s["d_pre"], d0 + idx + 1)
                        act.wait_ge(s["d_lo"], d0 + idx + 1)
                        fn(h32[:, m % 2, :], ps[:, 2 + m % 4, :], ACT.Gelu, scale=scol[:, L + 1, m:m + 1])\
                            .then_inc(s["d_act"], 1)

        @block.vector
        def _(dve):
            v = nc.vector
            dve.sem_inc(s["c_ready"], 2)
            dve.sem_inc(s["pv_used"], 2)
            dve.sem_inc(s["hf_ready"], 2)
            dve.sem_inc(s["hlo_ready"], 2)
            dve.sem_inc(s["xB_done"], 2)
            dve.sem_inc(s["xC_done"], 2)
            dve.sem_inc(s["xD_done"], 2)
            dve.sem_inc(s["mask_free"], 1)
            dve.sem_inc(s["qrc_done"], KD)
            dve.sem_inc(s["sm_ready"], 1)
            dve.sem_inc(s["at_ready"], 1)
            dve.sem_inc(s["d_h32"], 2)
            dve.sem_inc(s["d_lo"], 2)

            def x_stats(n, b0):
                ch = Chain(dve, s["dve_prep"], 2 * Q + 1, n)
                for q in range(Q):
                    ch.step(v.bn_stats(st6[:, q, :], x[:, b0 + q, :]))
                ch.settle_apart()
                for q in range(Q):
                    ch.step(v.bn_aggr(mv[:, q, :], st6[:, q, :]))
                ch.settle()
                ch.end()
                v.tensor_scalar(ve[:, :], mv[:, :, 1], 1e-5, None, ALU.add).then_inc(s["mv_ready"], 1)

            def x_norm(n, b0):
                dve.wait_ge(s["rstd_ready"], n + 1)
                for q in range(Q):
                    last = v.tensor_scalar(xn[:, q, :], x[:, b0 + q, :], mv[:, q, 0:1], rstd[:, q:q + 1],
                                           ALU.subtract, ALU.mult)
                last.then_inc(s["xn_ready"], 1)

            def x_lo(n, par):
                for c in range(KD):
                    dve.wait_ge(s["xhi_done"], KD * n + c + 1)
                    v.tensor_tensor(xT[:, par, 1, c, :], tr_bank(c), xT[:, par, 0, c, :], ALU.subtract)\
                        .then_inc(s["xlo_done"], 1)

            A2 = 9

            def gate_a(g):
                dve.wait_ge(s["gate_moved"], 32 * (g + 1))
                ch = Chain(dve, s["dve_a2"], A2, g)
                ch.step(v.tensor_scalar(fmn[:, :], gf[:, :], gb[:, 1:2], None, ALU.add))
                ch.settle()
                v.scalar_tensor_tensor(out=fab[:, :], in0=fmn[:, :], scalar=-1.0, in1=fmn[:, :], op0=ALU.mult,
                                       op1=ALU.max).then_inc(s["ab_ready"], 1)
                return ch

            def gate_b(g, ch):
                dve.wait_ge(s["ln_ready"], g + 1)
                ch.settle()
                ch.step(v.scalar_tensor_tensor(out=fl[:, :], in0=fmn[:, :], scalar=0.0, in1=fl[:, :],
                                               op0=ALU.min, op1=ALU.subtract))
                ch.settle()
                ch.step(v.tensor_tensor_scan(cs[:, :], one_r[:, :], fl[:, :], 0.0, ALU.mult, ALU.add))
                ch.settle()
                ch.step(v.scalar_tensor_tensor(out=Z[:, 1, :], in0=gi[:, :], scalar=gb[:, 0:1], in1=cs[:, :],
                                               op0=ALU.add, op1=ALU.subtract))
                ch.settle()
                ch.step(v.tensor_scalar(Z[:, 1, :], Z[:, 1, :], -1.0, None, ALU.mult))
                ch.settle()
                ch.step(v.tensor_tensor_scan(Z[:, 0, :], Z[:, 1, :], Z[:, 1, :], BIG, ALU.min, ALU.min))
                ch.settle()
                v.tensor_tensor(Er[:, :], Z[:, 0, :], cs[:, :], ALU.subtract).then_inc(s["ncs_ready"], 1)

            def gate_c(g, ch):
                ch.step(v.tensor_copy(zp[:, 0, :, :], Z[:, :, :]))
                ch.settle()
                ch.step(v.tensor_tensor(zr[:, :, :], Z[:, :, :], zp[:, 0, :, :], ALU.subtract))
                ch.settle()
                ch.step(v.tensor_copy(zp[:, 1, :, :], zr[:, :, :]))
                ch.settle()
                v.tensor_tensor(zp[:, 2, :, :], zr[:, :, :], zp[:, 1, :, :], ALU.subtract).then_inc(s["z_ready"], 1)
                ch.end()

            def floor_copy(g, par):
                dve.wait_ge(s["er_turned"], g + 1)
                v.tensor_scalar(ET[:, par, :], ps[:, TR + 1, 0:NR], EPS, None, ALU.add).then_inc(s["et_ready"], 1)

            def weigh(g, k):
                n, quad = UN * g + k, k % 2
                dve.wait_ge(s["d_ready"], n + 3)
                dve.wait_ge(s["qk_done"], n + 5)
                dve.wait_ge(s["pv_done"], n + 1)
                v.scalar_tensor_tensor(out=Ct[:, quad, :, :].rearrange("p j t -> p (j t)"), in0=ps[:, QK + quad, :],
                                       scalar=RS_DH, in1=Dt[:, quad, :, :].rearrange("p j t -> p (j t)"),
                                       op0=ALU.mult, op1=ALU.mult).then_inc(s["c_ready"], 1)

            def finish(g, u, k):
                n, q, quad = UN * g + k, k // 2, k % 2
                ch = Chain(dve, s["dve_unit"], 4, n)
                at = 2 * quad * VW
                pvb = ps[:, PV + quad, 0:Q * PVW].rearrange("p (j w) -> p j w", j=Q)
                floor = ET[:, u, :].rearrange("p (h q) -> p h q", q=Q)[:, Q * quad:Q * quad + Q, q]
                dve.wait_ge(s["pv_done"], n + 3)
                ch.step(v.tensor_scalar(den[:, 0, :], pvb[:, :, at + DH], -1.0, EPS, ALU.mult, ALU.add))
                ch.step(v.scalar_tensor_tensor(out=den[:, 1, :], in0=pvb[:, :, at + DH], scalar=EPS, in1=floor,
                                               op0=ALU.add, op1=ALU.max))
                ch.settle()
                ch.step(v.tensor_tensor(den[:, 1, :], den[:, 0, :], den[:, 1, :], ALU.max))
                ch.settle()
                ch.step(v.reciprocal(den[:, 2, :], den[:, 1, :]))
                ch.settle()
                v.tensor_tensor(hm[:, q % 2, Q * quad:Q * quad + Q, :], pvb[:, :, at:at + DH],
                                den[:, 2, :].rearrange("p (j a) -> p j a", a=1).to_broadcast([P, Q, DH]), ALU.mult)\
                    .then_inc(s["pv_used"], 1)
                ch.end()
                if quad:
                    b = Q * g + q
                    hc = Chain(dve, s["dve_b"], 3, b)
                    dve.wait_ge(s["pv_used"], n + 3)
                    hc.step(v.bn_stats(h6[:, :], hm[:, q % 2, :, :].rearrange("p h d -> p (h d)")))
                    hc.settle_apart()
                    hc.step(v.bn_aggr(hmv[:, 0, :], h6[:, :]))
                    hc.settle()
                    v.tensor_scalar(hve[:, 0:1], hmv[:, 0, 1:2], 1e-5, None, ALU.add).then_inc(s["hstat_ready"], 1)
                    hc.end()

            def head_norm(g, q):
                b = Q * g + q
                h = hm[:, q % 2, :, :].rearrange("p h d -> p (h d)")
                ch = Chain(dve, s["dve_c"], 1, b)
                dve.wait_ge(s["hrs_ready"], b + 1)
                ch.step(v.scalar_tensor_tensor(out=h, in0=h, scalar=hmv[:, 0, 0:1], in1=lns[:, :],
                                               op0=ALU.subtract, op1=ALU.mult))
                ch.settle()
                v.scalar_tensor_tensor(out=x[:, b, :], in0=h, scalar=hrs[:, 0:1], in1=x[:, b, :],
                                       op0=ALU.mult, op1=ALU.add).then_inc(s["xA_done"], 1)

            v.memset(one_r[:, :], 1.0)
            v.memset(onec[:, :], 1.0)
            dve.wait_ge(s["x_first"], 16)
            x_stats(0, 0)
            v.memset(Qb[:, :, :, :, :, :].bitcast(F32), 0.0).then_inc(s["const_set"], 1)
            v.memset(V[:, :, :, :, :], 1.0).then_inc(s["const_set"], 1)
            x_norm(0, 0)
            dve.wait_ge(s["consts"], CONSTS)
            v.tensor_copy(idb[:, :], idf[:, :]).then_inc(s["idb_ready"], 1)
            x_lo(0, 0)
            ch = gate_a(0)
            gate_b(0, ch)
            gate_c(0, ch)
            floor_copy(0, 0)
            dve.wait_ge(s["x_rest"], 16 * (G - 1))
            with dve.Fori(0, 2) as i:
                for u in range(2):
                    g = 2 * i + u
                    gn = g + 1 if u == 0 else G // 2
                    nb0 = 4 if u == 0 else None
                    b1 = Q * (g + 1) if u == 0 else 8 - 8 * i
                    more = (lambda f: f()) if u == 0 else (lambda f: if_more(dve, i, f))
                    state = {}
                    if u == 1:
                        dve.wait_ge(s["xA_done"], Q * g)
                    x_stats(g + 1, b1)
                    for k in range(UN):
                        if k == 1:
                            x_norm(g + 1, b1)
                        weigh(g, k)
                        if k:
                            finish(g, u, k - 1)
                        if k >= 3 and k % 2:
                            head_norm(g, (k - 3) // 2)
                        if k == 2:
                            x_lo(g + 1, 1 - u)
                        if k == 6:
                            more(lambda: state.update(ch=gate_a(gn)))
                        if k == 7:
                            def rest():
                                gate_b(gn, state["ch"])
                                gate_c(gn, state["ch"])
                            more(rest)
                    finish(g, u, UN - 1)
                    head_norm(g, Q - 1)
                    more(lambda: floor_copy(gn, 1 - u))

            dve.wait_ge(s["flag_tot"], 1)
            v.tensor_scalar(fint[:, :], ps[0:1, OB, 0:1], 0.0, None, ALU.is_gt).then_inc(s["flag_ready"], 1)
            dve.wait_ge(s["xA_done"], NB)
            with dve.Fori(0, 2) as i:
                for u in range(2):
                    g = 2 * i + u
                    gn = g + 1 if u == 0 else G // 2
                    b1 = Q * (g + 1) if u == 0 else 8 - 8 * i
                    dve.wait_ge(s["xB_done"], Q * g + 2)
                    x_stats(G + g + 1, b1)
                    for m in range(MB + 1):
                        n = MB * g + m
                        if m == 1:
                            x_norm(G + g + 1, b1)
                        if m < MB:
                            dve.wait_ge(s["hlo_ready"], n + 1)
                            dve.wait_ge(s["silu_ready"], n + 3)
                            v.scalar_tensor_tensor(out=hfB[:, m % 2, :], in0=ps[:, UB + m % 2, :], scalar=SCALE_B,
                                                   in1=silB[:, m % 2, :], op0=ALU.mult, op1=ALU.mult)\
                                .then_inc(s["hf_ready"], 1)
                        if m:
                            dve.wait_ge(s["hhi_ready"], n)
                            v.tensor_tensor(hB[:, 1, m - 1, :], hfB[:, (m - 1) % 2, :], hB[:, 0, m - 1, :],
                                            ALU.subtract).then_inc(s["hlo_ready"], 1)
                        if m == 4:
                            x_lo(G + g + 1, 1 - u)
                    for q in range(Q):
                        dve.wait_ge(s["down_done"], Q * g + q + 1)
                        b = Q * g + q
                        v.scalar_tensor_tensor(out=x[:, b, :], in0=ps[:, OB + q % 2, 0:D], scalar=SCALE_B,
                                               in1=x[:, b, :], op0=ALU.mult, op1=ALU.add).then_inc(s["xB_done"], 1)

            with dve.Fori(0, 2) as i:
                for u in range(2):
                    g = 2 * i + u
                    gn = g + 1 if u == 0 else G // 2
                    b1 = Q * (g + 1) if u == 0 else 8 - 8 * i
                    dve.wait_ge(s["mask_ld"], 16 * (g + 1))
                    v.tensor_scalar(mf[:, :, :], mk[:, :, :], -NEG, NEG, ALU.mult, ALU.add).then_inc(s["mask_free"], 1)
                    dve.wait_ge(s["xB_done"], NB + 2)
                    dve.wait_ge(s["xC_done"], Q * g + 2)
                    x_stats(2 * G + g + 1, b1)
                    for m in range(KD):
                        dve.wait_ge(s["qr_done"], KD * g + m + 1)
                        v.tensor_scalar(qr[:, m, :], ps[:, PJ + m, :], 0.0, diag[:, m:m + 1], ALU.max, ALU.mult)\
                            .then_inc(s["qrc_done"], 1)
                    x_norm(2 * G + g + 1, b1)
                    dve.wait_ge(s["sc_done"], g + 1)
                    dve.wait_ge(s["mask_free"], g + 2)
                    ch = Chain(dve, s["dve_d"], Q + 2, g)
                    ch.start_apart()
                    for q in range(Q):
                        ch.step(v.tensor_tensor_reduce(sc[:, q, :], ps[:, SCB, q * S:(q + 1) * S], mf[:, q, :], 1.0,
                                                       -BIG, ALU.add, ALU.max, smx[:, q:q + 1]))
                    ch.settle()
                    v.tensor_scalar(nmx[:, :], smx[:, :], -1.0, None, ALU.mult).then_inc(s["sm_ready"], 1)
                    x_lo(2 * G + g + 1, 1 - u)
                    dve.wait_ge(s["at_done"], g + 1)
                    v.tensor_copy(alT[:, :, :].rearrange("p q t -> p (q t)"), ps[:, ATB, :]).then_inc(s["at_ready"], 1)
                    ch.step(v.reciprocal(rrs[:, :], rsm[:, :]))
                    ch.settle()
                    ch.end()
                    for q in range(Q):
                        b = Q * g + q
                        dve.wait_ge(s["av_done"], b + 2 * Q + 1)
                        v.scalar_tensor_tensor(out=x[:, b, :], in0=ps[:, OB + q % 2, 0:D], scalar=rrs[:, q:q + 1],
                                               in1=x[:, b, :], op0=ALU.mult, op1=ALU.add).then_inc(s["xC_done"], 1)

            dve.wait_ge(s["av_done"], NB + 2 * Q)
            dve.wait_ge(s["xC_done"], NB + 2)
            with dve.Fori(0, 2) as i:
                for u in range(2):
                    g = 2 * i + u
                    gn = g + 1 if u == 0 else G // 2
                    d0 = 3 * MD * g
                    dst = (hA, hBt)[u]
                    for m in range(MD + 1):
                        if m < MD:
                            dve.wait_ge(s["d_lo"], d0 + m + 1)
                            dve.wait_ge(s["d_act"], d0 + m + 3)
                            v.scalar_tensor_tensor(out=h32[:, m % 2, :], in0=ps[:, 4 + m % 2, :],
                                                   scalar=scol[:, 1, m:m + 1], in1=silD[:, m % 2, :],
                                                   op0=ALU.mult, op1=ALU.mult).then_inc(s["d_h32"], 1)
                        if m:
                            dve.wait_ge(s["d_hi"], MD * g + m)
                            v.tensor_tensor(dst[:, 1, m - 1, :], h32[:, (m - 1) % 2, :], dst[:, 0, m - 1, :],
                                            ALU.subtract).then_inc(s["d_lo"], 1)
                    for idx in range(MD, 3 * MD):
                        m, L = idx % MD, idx // MD
                        dst = (hA, hBt)[(L + u) % 2]
                        if L == 2 and m == 0:
                            nxt = lambda: x_stats(3 * G + gn, Q * gn)
                            nxt() if u == 0 else if_more(dve, i, nxt)
                        if L == 2 and m == 2:
                            nxt = lambda: x_norm(3 * G + gn, Q * gn)
                            nxt() if u == 0 else if_more(dve, i, nxt)
                        if L == 2 and m == 5:
                            nxt = lambda: x_lo(3 * G + gn, 1 - u)
                            nxt() if u == 0 else if_more(dve, i, nxt)
                        dve.wait_ge(s["d_act"], d0 + idx + 3)
                        v.tensor_copy(dst[:, 0, m, :], h32[:, m % 2, :]).then_inc(s["dh_own"], 1)
                        dve.wait_ge(s["dh_own"], 2 * MD * g + idx - MD + 1)
                        v.tensor_tensor(dst[:, 1, m, :], h32[:, m % 2, :], dst[:, 0, m, :], ALU.subtract)\
                            .then_inc(s["d_lo"], 1)
                    for q in range(Q):
                        b = Q * g + q
                        dve.wait_ge(s["d_out"], b + 1)
                        dve.wait_ge(s["xD_done"], b + 1)
                        v.tensor_tensor(ot[:, q % 2, :], ps[:, OB + q % 2, 0:D], s3[:, :], ALU.mult)\
                            .then_inc(s["ot_ready"], 1)
                        dve.wait_ge(s["ot_ready"], b + 1)
                        v.tensor_tensor(x[:, b, :], x[:, b, :], ot[:, q % 2, :], ALU.add).then_inc(s["xD_done"], 1)


def if_more(eng, i, f):
    with eng.If(i < 1):
        f()


def kernel(x, ctx_1024, mask_BxS2_if1, L0_xattn_igate_w, L0_xattn_igate_b, L0_xattn_fgate_w, L0_xattn_fgate_b,
           L0_xattn_ln_scale, L0_ffn_w_gate, L0_ffn_w_up, L0_ffn_w_down, L1_xattn_W, L1_xattn_diagonal,
           L1_ffn_w1_w, L1_ffn_w1_s, L1_ffn_w2_w, L1_ffn_w2_s, L1_ffn_h1_w, L1_ffn_h1_s, L1_ffn_h2_w,
           L1_ffn_h2_s, L1_ffn_w3_w, L1_ffn_w3_s):
    import numpy as np
    import concourse.bacc as _bacc
    from concourse.bass_utils import run_bass_kernel_spmd as _run

    def rows(w):
        t = np.asarray(w).T
        return np.ascontiguousarray(t.reshape(t.shape[0] // P, P, t.shape[1]).transpose(1, 0, 2))

    def cols(v):
        return np.asarray(v).reshape(-1, P).T

    x, ctx = np.asarray(x), np.asarray(ctx_1024)
    gate_w = np.concatenate([np.asarray(L0_xattn_igate_w), np.asarray(L0_xattn_fgate_w)], axis=0)
    gate_b = np.stack([np.repeat(np.asarray(L0_xattn_igate_b), Q), np.repeat(np.asarray(L0_xattn_fgate_b), Q)], 1)
    scales = np.zeros((P, 4, MD), np.float32)
    for n, v in enumerate((L1_ffn_w1_s, L1_ffn_w2_s, L1_ffn_h1_s, L1_ffn_h2_s)):
        scales[:, n, :] = cols(v)
    w_all = np.concatenate([rows(w).reshape(P, -1) for w in (L1_ffn_w1_w, L1_ffn_w2_w, L1_ffn_w3_w, L1_ffn_h1_w,
                                                             L1_ffn_h2_w)], axis=1)
    import ml_dtypes
    bf = np.dtype(ml_dtypes.bfloat16)
    tri = np.zeros((P, Q, S), np.float32)
    t_, s_ = np.meshgrid(np.arange(P), np.arange(S), indexing="ij")
    tri[:, :, :] = np.where(t_ > s_, MASKED, 0.0)[:, None, :]
    ones_rows = np.zeros((RA, NH, Q, S), np.float32)
    ones_rows[0:3] = -1.0
    for r in range(3, RA):
        ones_rows[r, (r - 3) % Q::Q] = 1.0
    arrays = {
        "x_in": x,
        "ctx_in": ctx,
        "ctxT_in": np.ascontiguousarray(ctx.reshape(NB * S, KD, P).transpose(2, 1, 0)),
        "mask_in": np.asarray(mask_BxS2_if1),
        "gw_in": rows(gate_w),
        "gb_in": gate_b,
        "lns_in": np.asarray(L0_xattn_ln_scale),
        "l0gu_in": np.stack([rows(L0_ffn_w_gate), rows(L0_ffn_w_up)], axis=1),
        "l0d_in": rows(L0_ffn_w_down),
        "xaw_in": rows(L1_xattn_W),
        "diag_in": cols(L1_xattn_diagonal),
        "w_all_in": w_all,
        "s_cols_in": scales,
        "s3_in": np.asarray(L1_ffn_w3_s),
        "ident_in": np.eye(P, dtype=np.float32),
        "tri_in": tri.astype(bf),
        "ones_rows_in": ones_rows.astype(bf),
    }
    nc = _bacc.Bacc("TRN2", target_bir_lowering=False, num_devices=1)
    arrays = {k: np.ascontiguousarray(a) for k, a in arrays.items()}
    args = {k: nc.dram_tensor(k, a.shape, mybir.dt.from_np(a.dtype), kind="ExternalInput").ap()
            for k, a in arrays.items()}
    args["out"] = nc.dram_tensor("out", (NB, S, D), F32, kind="ExternalOutput").ap()
    two_layers(nc, **args)
    r = _run(nc, [arrays], core_ids=[0])
    return r.results[0]["out"]
```

```python
from contextlib import ExitStack

import concourse.bass as bass
from concourse import mybir
from concourse.alu_op_type import AluOpType as ALU

ACT = mybir.ActivationFunctionType
F32 = mybir.dt.float32
F32R = mybir.dt.float32r
BF16 = mybir.dt.bfloat16
I32 = mybir.dt.int32
U16 = mybir.dt.uint16
AX = mybir.AxisListType

P = 128
NB, S, D = 16, 128, 256
NH, DH = 8, 32
KD = D // P
Q = 4
G = NB // Q
GT = Q * S
HB = 768
MB = HB // P
HD = 1024
MD = HD // P
VW = DH + 1
PVW = 3 * VW
UN = 2 * Q
RA = 3 + 3 * Q
MOVES = 16 * 6
MASKED = 1e30
BIG = 3e38
SCALE_B = 1.0 / 127.0
RS_DH = float(DH) ** -0.5
NEG = -10000.0
EPS = 1e-6
CONSTS = 16 * 11
NRAW = 2 * G
W_ALL = 2 * KD * HD + MD * D + 2 * MD * HD
SEC_W1, SEC_W2 = 0, KD * HD
SEC_W3 = 2 * KD * HD
SEC_H1 = SEC_W3 + MD * D
SEC_H2 = SEC_H1 + MD * HD
FLAG_ITEMS = G * UN
FLAG_W = W_ALL // FLAG_ITEMS
RING = 2
ITEMS_G = 3 * MD + 2


class Chain:

    def __init__(self, eng, sem, per, index):
        self.eng, self.sem, self.per, self.base, self.n = eng, sem, per, index * per, 0

    def step(self, ins):
        ins.then_inc(self.sem, 1)
        self.n += 1

    def settle(self):
        self.eng.wait_ge(self.sem, self.base + self.n)

    def settle_apart(self):
        self.settle()
        self.eng.sem_inc(self.sem, 1)
        self.n += 1

    def start_apart(self):
        self.eng.sem_inc(self.sem, 1)
        self.n += 1

    def end(self):
        assert self.n == self.per, (self.n, self.per)


def two_layers(nc, x_in, ctx_in, ctxT_in, mask_in, gw_in, gb_in, lns_in, l0gu_in, l0d_in, xaw_in, diag_in,
               w_all_in, s_cols_in, s3_in, ident_in, tri_in, ones_rows_in, out):
    es = ExitStack()
    base = [(nc.sbuf_base + 63) // 64 * 64]
    sizes = {F32: 4, F32R: 4, I32: 4, BF16: 2, U16: 2}

    def place(at, name, shape, dt):
        n = sizes[dt]
        for d in shape[1:]:
            n *= d
        t = nc.alloc_sbuf_tensor_at(name, shape, dt, offset=at[0])
        at[0] += (n + 31) // 32 * 32
        return t

    def sem(name):
        return es.enter_context(nc.semaphore(name))

    with es:
        x = place(base, "x", [P, NB, D], F32)
        w1 = place(base, "w1", [P, KD, HD], F32R)
        w2 = place(base, "w2", [P, KD, HD], F32R)
        w3 = place(base, "w3", [P, MD, D], F32R)
        ring_at = [base[0] - 3 * KD * HD * 4]
        rawgu = place([ring_at[0]], "rawgu", [P, 2, KD, HB], F32)
        ring = place(ring_at, "ring", [P, RING, MD, P], F32)
        rawd_at = [ring_at[0] + 2 * KD * HB * 4 - RING * MD * P * 4]
        rawd = place(rawd_at, "rawd", [P, 2, MB // 2, D], F32)
        rawx = place(rawd_at, "rawx", [P, KD, D], F32)
        assert rawd_at[0] <= base[0]
        xT = place(base, "xT", [P, 2, 2, KD, GT], F32R)
        xn = place(base, "xn", [P, Q, D], F32)
        stage_at = [base[0]]
        stage = place(base, "stage", [P, 2, HD], F32)
        kstC = place([stage_at[0]], "kstC", [P, 2, KD, GT], F32)
        silD = place(stage_at, "silD", [P, 2, GT], F32)
        h32 = place(stage_at, "h32", [P, 2, GT], F32)
        xaw = place(base, "xaw", [P, 2, KD, D], F32R)
        idf = place(base, "idf", [P, P], F32)
        idb = place(base, "idb", [P, P], BF16)
        tri = place(base, "tri", [P, Q, S], BF16)
        lns = place(base, "lns", [P, D], F32)
        s3 = place(base, "s3", [P, D], F32)
        st6 = place(base, "st6", [P, Q, 6], F32)
        mv = place(base, "mv", [P, Q, 2], F32)
        ve = place(base, "ve", [P, Q], F32)
        rstd = place(base, "rstd", [P, Q], F32)
        mhalf = place(base, "mhalf", [P, Q], F32)
        h6 = place(base, "h6", [P, 6], F32)
        hmv = place(base, "hmv", [P, 2, 2], F32)
        hve = place(base, "hve", [P, 2], F32)
        hrs = place(base, "hrs", [P, 2], F32)
        scol = place(base, "scol", [P, 4, MD], F32)
        diag = place(base, "diag", [P, KD], F32)
        facc = place(base, "facc", [P, FLAG_ITEMS + 2 * G], F32)
        fsum = place(base, "fsum", [P, 1], F32)
        onec = place(base, "onec", [P, 1], F32)
        fint = place(base, "fint", [1, 1], I32)
        ot = place(base, "ot", [P, 2, D], F32)
        den = place(base, "den", [P, 3, Q], F32)
        smx = place(base, "smx", [P, Q], F32)
        nmx = place(base, "nmx", [P, Q], F32)
        rsm = place(base, "rsm", [P, Q], F32)
        rrs = place(base, "rrs", [P, Q], F32)
        r1 = [base[0]]
        l0 = place(r1, "l0", [P, 2, 2, KD, HB], F32R)
        l0d = place(r1, "l0d", [P, 2, MB, D], F32R)
        kT = place(r1, "kT", [P, 2, 2, KD, GT], F32R)
        V = place(r1, "V", [P, 2, Q, NH, VW], F32)
        mk = place(r1, "mk", [P, Q, S], I32)
        c1 = [base[0]]
        qr = place(c1, "qr", [P, KD, GT], F32)
        kr = place(c1, "kr", [P, KD, GT], F32)
        mf = place(c1, "mf", [P, Q, S], F32)
        sc = place(c1, "sc", [P, Q, S], F32)
        al = place(c1, "al", [P, Q, S], F32)
        alT = place(c1, "alT", [P, Q, S], F32)
        assert c1[0] <= base[0] + 36 * 1024
        d1 = [base[0]]
        hA = place(d1, "hA", [P, 2, MD, GT], F32R)
        hBt = place(d1, "hBt", [P, 2, MD, GT], F32R)
        r2 = [max(r1[0], d1[0])]
        r2b = [r2[0] + MD * HD * 4]
        h1 = place([r2[0]], "h1", [P, MD, HD], F32R)
        h2 = place([r2b[0]], "h2", [P, MD, HD], F32R)
        a2 = [r2[0]]
        Qb = place(a2, "Qb", [P, 2, 2, KD, Q, S], F32R)
        kstA = place(a2, "kstA", [P, KD, GT], F32)
        Dt = place(a2, "Dt", [P, 2, Q, S], F32)
        Ct = place(a2, "Ct", [P, 2, Q, S], F32)
        gw = place(a2, "gw", [P, 2, 2 * KD, P], F32R)
        assert a2[0] <= r2b[0]
        a3 = [r2b[0]]
        Rr = place(a3, "Rr", [RA, 2, Q, 2, Q, S], BF16)
        Lr = place(a3, "Lr", [RA, 2, 2, Q, S], BF16)
        gsb = place(a3, "gsb", [2 * NH, GT], F32)
        NR = NH * Q
        gi = place(a3, "gi", [NR, S], F32)
        gf = place(a3, "gf", [NR, S], F32)
        gb = place(a3, "gb", [NR, 2], F32)
        fab = place(a3, "fab", [NR, S], F32)
        fmn = place(a3, "fmn", [NR, S], F32)
        fl = place(a3, "fl", [NR, S], F32)
        one_r = place(a3, "one_r", [NR, S], F32)
        cs = place(a3, "cs", [NR, S], F32)
        Z = place(a3, "Z", [NR, 2, S], F32)
        zr = place(a3, "zr", [NR, 2, S], F32)
        zp = place(a3, "zp", [NR, 3, 2, S], BF16)
        Er = place(a3, "Er", [NR, S], F32)
        ET = place(a3, "ET", [P, 2, NR], F32)
        hm = place(a3, "hm", [P, 2, NH, DH], F32)
        graw = place(a3, "graw", [P, 3 * KD, 2 * NH], F32)
        gsum = place(a3, "gsum", [P, KD, 2 * NH], F32)
        assert a3[0] <= nc.sbuf_usable_end, a3[0]
        b3 = [r2b[0]]
        hB = place(b3, "hB", [P, 2, MB, GT], F32R)
        silB = place(b3, "silB", [P, 2, GT], F32)
        hfB = place(b3, "hfB", [P, 2, GT], F32)
        assert b3[0] <= nc.sbuf_usable_end, b3[0]

        ps = es.enter_context(nc.psum_tensor("ps", [P, 8, GT], F32))
        TR, EX, QK, PV = 0, 2, 4, 6
        GB, UB, OB = 2, 4, 6
        PJ, SCB, ATB = 2, 4, 5

        names = """x_first x_rest gw_ld consts mask_ld mask_free hi_ld
            raw_seen gw_lo gw_cast const_set mv_ready rstd_ready xn_ready tr_done xhi_done xlo_done x_free
            khi_done klo_done gate_done gate_copied gate_moved ab_ready ln_ready ncs_ready er_ready z_ready
            z_moved er_turned et_ready expo_done d_ready qk_done c_ready pv_done pv_used hstat_ready hrs_ready
            flag_used flag_sums flag_tot flag_ready l0_lo gu_done silu_ready hf_ready hhi_ready hlo_ready
            down_done xA_done xB_done kr_done qr_done krc_done qrc_done sc_done sm_ready al_ready at_done at_ready
            av_done xC_done d_pre d_sil d_h32 d_hi d_lo d_act d_out xD_done
            idb_ready dh_own ot_ready dve_prep dve_a2 dve_unit dve_b dve_c dve_d pool_own act_own out_done pe_own w_ld h1_ld h2_ld""".split()
        s = {n: sem(n) for n in names}
        qb_ld = [sem(f"qb_ld{i}") for i in range(2)]
        flag_ld = [sem(f"flag_ld{i}") for i in range(2)]
        ring_ld = [sem(f"ring_ld{i}") for i in range(RING)]
        ctxT_ld = [sem(f"ctxT_ld{i}") for i in range(2)]
        v_ld = [sem(f"v_ld{i}") for i in range(2)]

        def tr_bank(c):
            return ps[:, TR + c, :]

        def move_rows(sp, u):
            for part in range(3):
                sp.dma_start(Rr[part:part + 1, u, :, :, :, :], zp[:, part, 0, :]).then_inc(s["z_moved"], 16)
                sp.dma_start(Lr[3 + part * Q:3 + part * Q + Q, u, :, :, :], zp[:, part, 1, :])\
                    .then_inc(s["z_moved"], 16)

        block = es.enter_context(nc.Block())

        @block.sync
        def _(sp):
            sp.dma_start(x[:, 0:Q, :], x_in[0:Q].rearrange("b s d -> s b d")).then_inc(s["x_first"], 16)
            sp.dma_start(kstA[:, :, :], ctxT_in[:, :, 0:GT]).then_inc(ctxT_ld[0], 16)
            sp.dma_start(graw[:, :, :], gw_in).then_inc(s["gw_ld"], 16)
            sp.dma_start(idf[:, :], ident_in).then_inc(s["consts"], 16)
            sp.dma_start(gb[:, :], gb_in).then_inc(s["consts"], 16)
            for u in range(2):
                sp.dma_start(Rr[3:RA, u, :, :, :, :], ones_rows_in[3:RA]).then_inc(s["consts"], 16)
                sp.dma_start(Lr[0:3, u, :, :, :], ones_rows_in[0:3, 0]).then_inc(s["consts"], 16)
            sp.dma_start(tri[:, :, :], tri_in).then_inc(s["consts"], 16)
            sp.dma_start(lns[:, :], lns_in.partition_broadcast(P)).then_inc(s["consts"], 16)
            sp.dma_start(s3[:, :], s3_in.partition_broadcast(P)).then_inc(s["consts"], 16)
            sp.dma_start(scol[:, :, :], s_cols_in).then_inc(s["consts"], 16)
            sp.dma_start(diag[:, :], diag_in).then_inc(s["consts"], 16)
            for g in range(1, G):
                sp.dma_start(x[:, Q * g:Q * g + Q, :], x_in[Q * g:Q * g + Q].rearrange("b s d -> s b d"))\
                    .then_inc(s["x_rest"], 16)
            sp.wait_ge(s["klo_done"], 1)
            sp.dma_start(kstA[:, :, :], ctxT_in[:, :, GT:2 * GT]).then_inc(ctxT_ld[1], 16)
            sp.wait_ge(s["const_set"], 2)
            sp.wait_ge(s["z_ready"], 1)
            move_rows(sp, 0)
            with sp.Fori(0, 2) as i:
                for u in range(2):
                    g = 2 * i + u
                    gn = g + 1 if u == 0 else G // 2
                    for q in range(Q):
                        sp.dma_start(V[:, u, q, :, 0:DH],
                                     ctx_in[Q * g + q].rearrange("t (h d) -> t h d", d=DH))\
                            .then_inc(v_ld[u], 16)
                    for q in range(Q):
                        if q == 2:
                            with sp.If(i < 1):
                                sp.wait_ge(s["klo_done"], 2 + u)
                                sp.dma_start(kstA[:, :, :], ctxT_in[:, :, (2 + u) * GT:(3 + u) * GT])\
                                    .then_inc(ctxT_ld[u], 16)
                        if q == 0:
                            sp.wait_ge(s["xlo_done"], KD * (g + 1))
                            sp.wait_ge(s["xhi_done"], KD * (g + 1))
                        sp.wait_ge(s["qk_done"], UN * g + 2 * q + 2)
                        for j in range(Q):
                            sp.dma_start(Qb[DH * j:DH * j + DH, q % 2, :, :, j, :].bitcast(F32),
                                         xT[DH * j:DH * j + DH, u, :, :, q * S:(q + 1) * S].bitcast(F32))\
                                .then_inc(qb_ld[q % 2], 16)
                        for k in (2 * q, 2 * q + 1):
                            sp.wait_ge(s["flag_used"], UN * g + k + 1)
                            sp.dma_start(stage[:, k % 2, 0:FLAG_W],
                                         w_all_in[:, bass.ds((UN * g + k) * FLAG_W, FLAG_W)])\
                                .then_inc(flag_ld[k % 2], 16)

                    def parts_out():
                        sp.wait_ge(s["z_ready"], gn + 1)
                        move_rows(sp, 1 - u)
                    if u == 0:
                        parts_out()
                    else:
                        with sp.If(i < 1):
                            parts_out()
            sp.wait_ge(s["flag_used"], FLAG_ITEMS + 2)
            for u in range(2):
                sp.dma_start(kstC[:, u, :, :], ctxT_in[:, :, u * GT:(u + 1) * GT]).then_inc(ctxT_ld[u], 16)
            sp.wait_ge(s["pv_done"], UN * G + 2)
            with sp.Fori(0, 2) as i:
                for u in range(2):
                    g = 2 * i + u
                    gn = g + 1 if u == 0 else G // 2
                    sp.wait_ge(s["av_done"], Q * g + Q)
                    for q in range(Q):
                        sp.dma_start(V[:, u, q, :, 0:DH],
                                     ctx_in[Q * g + q].rearrange("t (h d) -> t h d", d=DH))\
                            .then_inc(v_ld[u], 16)
                    sp.wait_ge(s["mask_free"], g + 1)
                    sp.dma_start(mk[:, :, :], mask_in[bass.ds(Q * g, Q), :].partition_broadcast(P))\
                        .then_inc(s["mask_ld"], 16)
                    with sp.If(i < 1):
                        sp.wait_ge(s["klo_done"], G + u + 1)
                        sp.dma_start(kstC[:, u, :, :], ctxT_in[:, :, (2 + u) * GT:(3 + u) * GT])\
                            .then_inc(ctxT_ld[u], 16)
            sp.wait_ge(s["flag_ready"], 1)
            fl_reg = sp.value_load(fint[0:1, 0:1])
            with sp.If(fl_reg > 0):
                sp.wait_ge(s["w_ld"], 48)
                with sp.Fori(0, G) as g:
                    n = 0

                    def block_in(dst, src):
                        nonlocal n
                        if n < RING:
                            sp.wait_ge(s["d_out"], Q * g + 1)
                        else:
                            sp.wait_ge(s["d_pre"], 3 * MD * g + n - RING + 1)
                        sp.dma_start(dst, src).then_inc(ring_ld[n % RING], 16)
                        n += 1
                    for m in range(MD):
                        v = w_all_in[:, SEC_W1:SEC_W3].rearrange("p (a f) -> p a f", a=2 * KD)
                        block_in(ring[:, n % RING, 0:2 * KD, :], v[:, :, m * P:(m + 1) * P])
                    for sec in (SEC_H1, SEC_H2):
                        v = w_all_in[:, sec:sec + MD * HD].rearrange("p (a f) -> p a f", a=MD)
                        for m in range(MD):
                            block_in(ring[:, n % RING, :, :], v[:, :, m * P:(m + 1) * P])
                    for half in range(2):
                        v = w_all_in[:, SEC_W3 + half * HD:SEC_W3 + (half + 1) * HD]
                        block_in(ring[:, n % RING, :, :], v.rearrange("p (a f) -> p a f", a=MD))

        @block.gpsimd
        def _(pool):
            own = [0]

            def step(ins):
                ins.then_inc(s["pool_own"], 1)
                own[0] += 1

            def settle():
                pool.wait_ge(s["pool_own"], own[0])

            step(nc.gpsimd.memset(mhalf[:, :], -0.5))
            step(nc.gpsimd.memset(gw[:, :, :, :].bitcast(F32), 0.0))
            pool.wait_ge(s["gw_ld"], 16)
            step(nc.gpsimd.tensor_tensor(gsum[:, :, :], graw[:, KD:2 * KD, :], graw[:, 2 * KD:3 * KD, :], ALU.add))
            settle()
            W = 2 * NH
            step(nc.gpsimd.tensor_copy(gw[:, 0, 0:KD, 0:W], graw[:, 0:KD, :]))
            step(nc.gpsimd.tensor_copy(gw[:, 0, KD:2 * KD, 0:W], gsum[:, :, :]))
            settle()
            nc.gpsimd.tensor_tensor(gw[:, 1, 0:KD, 0:W], graw[:, 0:KD, :], gw[:, 0, 0:KD, 0:W], ALU.subtract)\
                .then_inc(s["gw_lo"], 1)
            nc.gpsimd.tensor_tensor(gw[:, 1, KD:2 * KD, 0:W], gsum[:, :, :], gw[:, 0, KD:2 * KD, 0:W], ALU.subtract)\
                .then_inc(s["gw_lo"], 1)

            def inv_root(n):
                pool.wait_ge(s["mv_ready"], n + 1)
                nc.gpsimd.tensor_tensor(rstd[:, :], ve[:, :], mhalf[:, :], ALU.pow).then_inc(s["rstd_ready"], 1)

            def k_lo(n, kst, u):
                pool.wait_ge(s["khi_done"], n + 1)
                nc.gpsimd.tensor_tensor(kT[:, u, 1, :, :], kst, kT[:, u, 0, :, :], ALU.subtract)\
                    .then_inc(s["klo_done"], 1)

            inv_root(0)
            k_lo(0, kstA[:, :, :], 0)
            pool.dma_start(l0[:, 0, :, :, :], l0gu_in).then_inc(s["hi_ld"], 16)
            pool.dma_start(rawgu[:, :, :, :], l0gu_in).then_inc(s["hi_ld"], 16)
            pool.dma_start(l0d[:, 0, :, :], l0d_in).then_inc(s["hi_ld"], 16)
            pool.dma_start(rawd[:, :, :, :], l0d_in.rearrange("p (i m) f -> p i m f", i=2)).then_inc(s["hi_ld"], 16)
            pool.dma_start(xaw[:, 0, :, :], xaw_in).then_inc(s["hi_ld"], 16)
            pool.dma_start(rawx[:, :, :], xaw_in).then_inc(s["hi_ld"], 16)

            def lows(i, u):
                nc.gpsimd.tensor_tensor(l0[:, 1, bass.ds(i, 1), u, :], rawgu[:, bass.ds(i, 1), u, :],
                                        l0[:, 0, bass.ds(i, 1), u, :], ALU.subtract).then_inc(s["l0_lo"], 1)
                if u == 0:
                    nc.gpsimd.tensor_tensor(xaw[:, 1, bass.ds(i, 1), :], rawx[:, bass.ds(i, 1), :],
                                            xaw[:, 0, bass.ds(i, 1), :], ALU.subtract).then_inc(s["l0_lo"], 1)
                else:
                    m = bass.ds(i * (MB // 2), MB // 2)
                    nc.gpsimd.tensor_tensor(l0d[:, 1, m, :], rawd[:, bass.ds(i, 1), :, :],
                                            l0d[:, 0, m, :], ALU.subtract).then_inc(s["l0_lo"], 1)

            def h_root(b):
                pool.wait_ge(s["hstat_ready"], b + 1)
                nc.gpsimd.tensor_tensor(hrs[:, 0:1], hve[:, 0:1], mhalf[:, 0:1], ALU.pow)\
                    .then_inc(s["hrs_ready"], 1)

            inv_root(1)
            with pool.Fori(0, 2) as i:
                for u in range(2):
                    g = 2 * i + u
                    gn = g + 1 if u == 0 else G // 2
                    if u == 0:
                        k_lo(gn, kstA[:, :, :], 1 - u)
                    else:
                        with pool.If(i < 1):
                            k_lo(gn, kstA[:, :, :], 1 - u)
                    for q in range(Q):
                        if q == 2:
                            if u == 0:
                                inv_root(g + 2)
                            else:
                                with pool.If(i < 1):
                                    inv_root(3)
                        h_root(Q * g + q)
                        if q == 0:
                            pool.wait_ge(s["hi_ld"], 96)
                            lows(i, u)
            inv_root(G + 1)
            pool.wait_ge(s["xA_done"], NB)
            for u in range(2):
                k_lo(G + u, kstC[:, u, :, :], u)
            pool.wait_ge(s["flag_sums"], 1)
            pool.dma_start(w1[:, :, :], w_all_in[:, SEC_W1:SEC_W2].rearrange("p (k f) -> p k f", k=KD))\
                .then_inc(s["w_ld"], 16)
            pool.dma_start(w2[:, :, :], w_all_in[:, SEC_W2:SEC_W3].rearrange("p (k f) -> p k f", k=KD))\
                .then_inc(s["w_ld"], 16)
            pool.dma_start(w3[:, :, :], w_all_in[:, SEC_W3:SEC_H1].rearrange("p (k f) -> p k f", k=MD))\
                .then_inc(s["w_ld"], 16)
            for k in range(MD):
                pool.dma_start(h1[:, k, :], w_all_in[:, SEC_H1 + k * HD:SEC_H1 + (k + 1) * HD])\
                    .then_inc(s["h1_ld"], 16)
            with pool.Fori(0, G) as g:
                inv_root(g + G + 2)
            pool.wait_ge(s["down_done"], Q * G)
            for k in range(MD):
                pool.dma_start(h2[:, k, :], w_all_in[:, SEC_H2 + k * HD:SEC_H2 + (k + 1) * HD])\
                    .then_inc(s["h2_ld"], 16)
            with pool.Fori(0, 2) as i:
                for u in range(2):
                    g = 2 * i + u
                    gn = g + 1 if u == 0 else G // 2
                    with pool.If(i < 1):
                        k_lo(G + 2 + u, kstC[:, u, :, :], u)
                    if u == 0:
                        inv_root(2 * G + g + 2)
                    else:
                        with pool.If(i < 1):
                            inv_root(2 * G + 3)
            with pool.Fori(0, 2) as i:
                for u in range(2):
                    g = 2 * i + u
                    gn = g + 1 if u == 0 else G // 2
                    if u == 0:
                        inv_root(3 * G + gn)
                    else:
                        with pool.If(i < 1):
                            inv_root(3 * G + gn)
                    for q in range(Q):
                        pool.wait_ge(s["xD_done"], 2 + Q * g + q + 1)
                        pool.dma_start(out[Q * g + q], x[:, Q * g + q, :]).then_inc(s["out_done"], 16)
            pool.wait_ge(s["out_done"], 16 * NB)

        @block.tensor
        def _(pe):
            mm = nc.tensor.matmul
            pe.sem_inc(s["qk_done"], 4)
            pe.sem_inc(s["pv_done"], 2)
            pe.sem_inc(s["av_done"], 2 * Q)
            pe.sem_inc(s["d_out"], 1)

            def turn_x(n, first=False):
                pe.wait_ge(s["xn_ready"], n + 1)
                if not first:
                    pe.wait_ge(s["xlo_done"], KD * n)
                for c in range(KD):
                    for q in range(Q):
                        last = nc.tensor.transpose(ps[:, TR + c, q * S:(q + 1) * S], xn[:, q, c * P:(c + 1) * P],
                                                   idf[:, :])
                last.then_inc(s["tr_done"], 1)

            def three(o, lhs, rhs, first, last, weight_moves=False):
                mm(o, lhs(0), rhs(0), start=first, stop=False)
                mm(o, lhs(0), rhs(1), start=False, stop=False)
                return mm(o, lhs(1), rhs(0), start=False, stop=last)

            def two(o, lhs, rhs, first, last, weight_moves=False):
                mm(o, lhs(0), rhs(0), start=first, stop=False)
                if weight_moves:
                    return mm(o, lhs(1), rhs(0), start=False, stop=last)
                return mm(o, lhs(0), rhs(1), start=False, stop=last)

            def gates(g, u):
                pe.wait_ge(s["klo_done"], g + 1)
                pe.wait_ge(s["xlo_done"], KD * (g + 1))
                for c in range(2 * KD):
                    src = (lambda p, c=c: xT[:, u, p, c, :]) if c < KD else (lambda p, c=c: kT[:, u, p, c - KD, :])
                    last = three(tr_bank(0), lambda p, c=c: gw[:, p, c, :], src, c == 0, c == 2 * KD - 1)
                last.then_inc(s["gate_done"], 1)

            def turn_e(g):
                pe.wait_ge(s["er_ready"], g + 1)
                pe.sem_inc(s["pe_own"], 1)
                nc.tensor.transpose(ps[:, TR + 1, 0:NR], Er[:, :], idf[0:NR, 0:NR]).then_inc(s["er_turned"], 1)

            def expo(g, u, k):
                q, quad = k // 2, k % 2
                n = UN * g + k
                if k == 0:
                    pe.wait_ge(s["z_moved"], MOVES * (g + 1))
                pe.wait_ge(s["d_ready"], n + 1)
                mm(ps[:, EX + quad, :], Lr[:, u, quad, q, :], Rr[:, u, :, quad, q, :],
                   start=True, stop=False)
                mm(ps[:, EX + quad, :], idb[:, :], tri[:, :, :], start=False, stop=True)\
                    .then_inc(s["expo_done"], 1)

            def qk(g, u, k):
                q, quad = k // 2, k % 2
                n = UN * g + k
                if quad == 0:
                    pe.wait_ge(qb_ld[q % 2], 64 * (2 * g + q // 2 + 1))
                pe.wait_ge(s["c_ready"], n + 1)
                three(ps[:, QK + quad, :], lambda p: kT[:, u, p, quad, q * S:(q + 1) * S],
                      lambda p: Qb[:, q % 2, p, quad, :, :], True, True).then_inc(s["qk_done"], 1)

            def pv(i, g, u, k):
                q, quad = k // 2, k % 2
                n = UN * g + k
                if k == 0:
                    pe.wait_ge(v_ld[u], 16 * Q * (i + 1))
                pe.wait_ge(s["c_ready"], n + 3)
                pe.wait_ge(s["pv_used"], n + 1)
                for j in range(Q):
                    lo = Q * quad + j - 2 * quad
                    last = mm(ps[:, PV + quad, j * PVW:(j + 1) * PVW], Ct[:, quad, j, :], V[:, u, q, lo:lo + 3, :],
                              start=True, stop=True)
                last.then_inc(s["pv_done"], 1)

            pe.wait_ge(s["consts"], CONSTS)
            turn_x(0, True)
            pe.wait_ge(s["gw_lo"], 2)
            pe.wait_ge(s["idb_ready"], 1)
            gates(0, 0)
            turn_e(0)
            with pe.Fori(0, 2) as i:
                for u in range(2):
                    g = 2 * i + u
                    gn = g + 1 if u == 0 else G // 2
                    more = (lambda f: f()) if u == 0 else (lambda f: if_more(pe, i, f))
                    for k in range(UN):
                        expo(g, u, k)
                        if k == 0:
                            pe.wait_ge(s["gate_copied"], g + 1)
                            pe.wait_ge(s["et_ready"], g + 1)
                            turn_x(g + 1)
                        qk(g, u, k)
                        if k == 1:
                            more(lambda: gates(gn, 1 - u))
                        if k:
                            pv(i, g, u, k - 1)
                    more(lambda: turn_e(gn))
                    pv(i, g, u, UN - 1)

            pe.wait_ge(s["flag_sums"], 1)
            pe.wait_ge(s["pv_used"], UN * G + 2)
            mm(ps[0:1, OB, 0:1], fsum[:, :], onec[:, :], start=True, stop=True).then_inc(s["flag_tot"], 1)
            pe.wait_ge(s["l0_lo"], NRAW)
            pe.wait_ge(s["flag_ready"], 1)
            flag_reg = pe.value_load(fint[0:1, 0:1])

            def stage_b(general):
                by = three if general else two
                with pe.Fori(0, 2) as i:
                    for u in range(2):
                        g = 2 * i + u
                        gn = g + 1 if u == 0 else G // 2
                        pe.wait_ge(s["xlo_done"], KD * (G + g + 1))
                        for m in range(MB):
                            n = MB * g + m
                            if m == 3:
                                turn_x(G + g + 1)
                            for a, (bank, used) in enumerate(((GB, "silu_ready"), (UB, "hf_ready"))):
                                pe.wait_ge(s[used], n + 1)
                                for c in range(KD):
                                    last = by(ps[:, bank + m % 2, :],
                                                 lambda p: l0[:, p, a, c, m * P:(m + 1) * P],
                                                 lambda p: xT[:, u, p, c, :], c == 0, c == KD - 1)
                            last.then_inc(s["gu_done"], 1)
                        for q in range(Q):
                            pe.wait_ge(s["xB_done"], Q * g + q + 1)
                            for k in range(MB):
                                if q == 0:
                                    pe.wait_ge(s["hlo_ready"], MB * g + k + 3)
                                last = by(ps[:, OB + q % 2, 0:D], lambda p: hB[:, p, k, q * S:(q + 1) * S],
                                          lambda p: l0d[:, p, k, :], k == 0, k == MB - 1, weight_moves=True)
                            last.then_inc(s["down_done"], 1)

            with pe.If(flag_reg > 0):
                stage_b(True)
            with pe.Else():
                stage_b(False)

            pe.wait_ge(s["xB_done"], NB + 2)

            def keys(g, u):
                pe.wait_ge(s["klo_done"], G + g + 1)
                for m in range(KD):
                    pe.wait_ge(s["qrc_done"], KD * g + m + 1)
                    for c in range(KD):
                        last = three(ps[:, PJ + m, :], lambda p: xaw[:, p, c, m * P:(m + 1) * P],
                                     lambda p: kT[:, u, p, c, :], c == 0, c == KD - 1)
                    last.then_inc(s["kr_done"], 1)

            def queries(g, u):
                pe.wait_ge(s["xlo_done"], KD * (2 * G + g + 1))
                for m in range(KD):
                    pe.wait_ge(s["krc_done"], KD * g + m + 1)
                    for c in range(KD):
                        last = three(ps[:, PJ + m, :], lambda p: xaw[:, p, c, m * P:(m + 1) * P],
                                     lambda p: xT[:, u, p, c, :], c == 0, c == KD - 1)
                    last.then_inc(s["qr_done"], 1)

            keys(0, 0)
            queries(0, 0)
            with pe.Fori(0, 2) as i:
                for u in range(2):
                    g = 2 * i + u
                    gn = g + 1 if u == 0 else G // 2
                    more = (lambda f: f()) if u == 0 else (lambda f: if_more(pe, i, f))
                    turn_x(2 * G + g + 1)
                    pe.wait_ge(s["qrc_done"], KD * g + 2 * KD)
                    pe.wait_ge(s["sm_ready"], g + 1)
                    for q in range(Q):
                        for c in range(KD):
                            last = mm(ps[:, SCB, q * S:(q + 1) * S], qr[:, c, q * S:(q + 1) * S],
                                      kr[:, c, q * S:(q + 1) * S], start=(c == 0), stop=(c == KD - 1))
                    last.then_inc(s["sc_done"], 1)
                    more(lambda: keys(gn, 1 - u))
                    pe.wait_ge(s["at_ready"], g + 1)
                    for q in range(Q):
                        pe.wait_ge(s["al_ready"], Q * g + q + 1)
                        last = nc.tensor.transpose(ps[:, ATB, q * S:(q + 1) * S], al[:, q, :], idf[:, :])
                    last.then_inc(s["at_done"], 1)
                    more(lambda: queries(gn, 1 - u))
                    pe.wait_ge(s["at_ready"], g + 2)
                    pe.wait_ge(v_ld[u], 16 * Q * (i + 3))
                    for q in range(Q):
                        pe.wait_ge(s["xC_done"], Q * g + q + 1)
                        mm(ps[:, OB + q % 2, 0:D].rearrange("p (h d) -> p h d", d=DH), alT[:, q, :],
                           V[:, u, q, :, 0:DH], start=True, stop=True).then_inc(s["av_done"], 1)

            pe.wait_ge(s["xC_done"], NB + 2)
            pe.wait_ge(s["w_ld"], 48)
            pe.wait_ge(s["h1_ld"], 16 * MD)
            pe.wait_ge(s["h2_ld"], 16 * MD)

            def wide(o, lhs, rhs, k, n_k, general):
                for p in range(2):
                    a, b = lhs(k, p), rhs(k, p)
                    if general:
                        a, b = a.bitcast(F32), b.bitcast(F32)
                    last = mm(o, a, b, start=(k == 0 and p == 0), stop=(k == n_k - 1 and p == 1))
                return last

            def stage_d(general):
                with pe.Fori(0, 2) as i:
                    for u in range(2):
                        g = 2 * i + u
                        gn = g + 1 if u == 0 else G // 2
                        d0 = 3 * MD * g
                        item = 0

                        def block_wait():
                            if general:
                                pe.wait_ge(ring_ld[item % RING], 16 * ((ITEMS_G // RING) * g + item // RING + 1))

                        def block_free(last, name):
                            nonlocal item
                            last.then_inc(s[name], 1)
                            item += 1

                        pe.wait_ge(s["xlo_done"], KD * (3 * G + g + 1))
                        for m in range(MD):
                            block_wait()
                            if m < 2:
                                pe.wait_ge(s["d_act"], d0 + 1 + m)
                            else:
                                pe.wait_ge(s["d_act"], d0 + m + 1)
                                pe.wait_ge(s["d_h32"], MD * g + m + 1)
                            for a, (w, bank) in enumerate(((w1, 2), (w2, 4))):
                                for k in range(KD):
                                    if general:
                                        lhs = lambda k, p: ring[:, item % RING, a * KD + k, :]
                                    else:
                                        lhs = lambda k, p: w[:, k, m * P:(m + 1) * P]
                                    last = wide(ps[:, bank + m % 2, :], lhs, lambda k, p: xT[:, u, p, k, :],
                                                k, KD, general)
                            block_free(last, "d_pre")
                        for L, w in enumerate((h1, h2)):
                            src = (hA, hBt)[(L + u) % 2]
                            for m in range(MD):
                                if L == 1 and m == 4:
                                    nxt = lambda: turn_x(3 * G + gn)
                                    nxt() if u == 0 else if_more(pe, i, nxt)
                                block_wait()
                                idx = MD * (L + 1) + m
                                if L == 0 and m == 0:
                                    pe.wait_ge(s["d_act"], d0 + 2 + MD - 1)
                                if idx >= 12:
                                    pe.wait_ge(s["d_act"], d0 + 2 + idx - 3)
                                for k in range(MD):
                                    if m == 0:
                                        pe.wait_ge(s["d_lo"], d0 + 2 + MD * L + k + 1)
                                    if general:
                                        lhs = lambda k, p: ring[:, item % RING, k, :]
                                    else:
                                        lhs = lambda k, p: w[:, k, m * P:(m + 1) * P]
                                    last = wide(ps[:, 2 + m % 4, :], lhs, lambda k, p: src[:, p, k, :], k, MD, general)
                                block_free(last, "d_pre")
                        src = (hA, hBt)[u]
                        for half in range(2):
                            block_wait()
                            item += 1
                        item -= 2
                        for q in range(Q):
                            pe.wait_ge(s["xD_done"], Q * g + q + 1)
                            for k in range(MD):
                                if q == 0:
                                    pe.wait_ge(s["d_lo"], d0 + 2 + 2 * MD + k + 1)
                                if general:
                                    rhs = lambda k, p: ring[:, (item + k // Q) % RING, 2 * (k % Q):2 * (k % Q) + 2, :]
                                else:
                                    rhs = lambda k, p: w3[:, k, :]
                                last = wide(ps[:, OB + q % 2, 0:D], lambda k, p: src[:, p, k, q * S:(q + 1) * S],
                                            rhs, k, MD, general)
                            last.then_inc(s["d_out"], 1)

            with pe.If(flag_reg > 0):
                stage_d(True)
            with pe.Else():
                stage_d(False)

        @block.scalar
        def _(act):
            fn = nc.scalar.activation
            act.sem_inc(s["flag_used"], 2)
            act.sem_inc(s["d_ready"], 2)
            act.sem_inc(s["silu_ready"], 2)
            act.sem_inc(s["d_act"], 2)

            def x_hi(n, par):
                for c in range(KD):
                    act.wait_ge(s["tr_done"], n + 1)
                    fn(xT[:, par, 0, c, :], tr_bank(c), ACT.Copy).then_inc(s["xhi_done"], 1)

            def k_hi(nth, kst, par):
                act.wait_ge(ctxT_ld[par], 16 * nth)
                fn(kT[:, par, 0, :, :], kst, ACT.Copy).then_inc(s["khi_done"], 1)

            def gate_copy(g):
                act.wait_ge(s["gate_done"], g + 1)
                fn(gsb[:, :], ps[0:2 * NH, TR, :], ACT.Copy).then_inc(s["gate_copied"], 1)
                act.wait_ge(s["gate_copied"], g + 1)
                act.dma_start(gi[:, :], gsb[0:NH, :].rearrange("h (q t) -> h q t", q=Q)).then_inc(s["gate_moved"], 16)
                act.dma_start(gf[:, :], gsb[NH:2 * NH, :].rearrange("h (q t) -> h q t", q=Q))\
                    .then_inc(s["gate_moved"], 16)

            def log_part(g):
                act.wait_ge(s["ab_ready"], g + 1)
                fn(fl[:, :], fab[:, :], ACT.Exp, scale=-1.0).then_inc(s["act_own"], 1)
                act.wait_ge(s["act_own"], g + 1)
                fn(fl[:, :], fl[:, :], ACT.Ln, bias=1.0).then_inc(s["ln_ready"], 1)

            def floor_part(g):
                act.wait_ge(s["ncs_ready"], g + 1)
                fn(Er[:, :], Er[:, :], ACT.Exp).then_inc(s["er_ready"], 1)

            def low_sum(view, to):
                low = view.bitcast(U16).rearrange("p (w a) -> p w a", a=2)[:, :, 0:1]
                fn(view.rearrange("p (w a) -> p w a", a=1), low, ACT.Copy, accum_out=to).then_inc(s["raw_seen"], 1)

            k_hi(1, kstA[:, :, :], 0)
            x_hi(0, 0)
            gate_copy(0)
            log_part(0)
            floor_part(0)
            with act.Fori(0, 2) as i:
                for u in range(2):
                    g = 2 * i + u
                    gn = g + 1 if u == 0 else G // 2
                    more = (lambda f: f()) if u == 0 else (lambda f: if_more(act, i, f))
                    for k in range(UN):
                        n = UN * g + k
                        quad = k % 2
                        act.wait_ge(s["expo_done"], n + 1)
                        act.wait_ge(s["c_ready"], n + 1)
                        fn(Dt[:, quad, :, :], ps[:, EX + quad, :].rearrange("p (j t) -> p j t", j=Q), ACT.Exp,
                           scale=-1.0).then_inc(s["d_ready"], 1)
                        if k == 0:
                            more(lambda: k_hi(i + 1 if u == 0 else 2, kstA[:, :, :], 1 - u))
                            x_hi(g + 1, 1 - u)
                        if k == 1:
                            more(lambda: gate_copy(gn))
                        if k == 3:
                            more(lambda: log_part(gn))
                        if k == 5:
                            more(lambda: floor_part(gn))
                        act.wait_ge(flag_ld[k % 2], 16 * (Q * g + k // 2 + 1))
                        view = stage[:, k % 2, 0:FLAG_W]
                        low = view.bitcast(U16).rearrange("p (w a) -> p w a", a=2)[:, :, 0:1]
                        fn(view.rearrange("p (w a) -> p w a", a=1), low, ACT.Copy,
                           accum_out=facc[:, bass.ds(n, 1)]).then_inc(s["flag_used"], 1)
                    act.wait_ge(s["l0_lo"], 2 * g + 2)
                    low_sum(rawgu[:, bass.ds(i, 1), u, :].rearrange("p a w -> p (a w)"),
                            facc[:, bass.ds(FLAG_ITEMS + 2 * g, 1)])
                    if u == 1:
                        low_sum(rawd[:, bass.ds(i, 1), :, :].rearrange("p a m w -> p (a m w)"),
                                facc[:, bass.ds(FLAG_ITEMS + 2 * g + 1, 1)])
            act.wait_ge(s["flag_used"], FLAG_ITEMS + 2)
            act.wait_ge(s["raw_seen"], G + G // 2)
            fn(facc[:, :], facc[:, :], ACT.Copy, accum_out=fsum[:, :]).then_inc(s["flag_sums"], 1)

            act.wait_ge(s["xA_done"], NB)
            for u in range(2):
                k_hi(3, kstC[:, u, :, :], u)
            with act.Fori(0, 2) as i:
                for u in range(2):
                    g = 2 * i + u
                    gn = g + 1 if u == 0 else G // 2
                    for m in range(MB + 1):
                        n = MB * g + m
                        if m < MB:
                            act.wait_ge(s["gu_done"], n + 1)
                            act.wait_ge(s["hf_ready"], n + 1)
                            fn(silB[:, m % 2, :], ps[:, GB + m % 2, :], ACT.Silu, scale=SCALE_B)\
                                .then_inc(s["silu_ready"], 1)
                        if m:
                            act.wait_ge(s["hf_ready"], n + 2)
                            fn(hB[:, 0, m - 1, :], hfB[:, (m - 1) % 2, :], ACT.Copy).then_inc(s["hhi_ready"], 1)
                        if m == 3:
                            x_hi(G + g + 1, 1 - u)

            def relu_keys(g):
                for m in range(KD):
                    act.wait_ge(s["kr_done"], KD * g + m + 1)
                    fn(kr[:, m, :], ps[:, PJ + m, :], ACT.Relu).then_inc(s["krc_done"], 1)

            act.wait_ge(s["down_done"], NB)
            relu_keys(0)
            with act.Fori(0, 2) as i:
                for u in range(2):
                    g = 2 * i + u
                    gn = g + 1 if u == 0 else G // 2
                    more = (lambda f: f()) if u == 0 else (lambda f: if_more(act, i, f))
                    x_hi(2 * G + g + 1, 1 - u)
                    act.wait_ge(s["sm_ready"], g + 2)
                    for q in range(Q):
                        fn(al[:, q, :], sc[:, q, :], ACT.Exp, bias=nmx[:, q:q + 1], accum_out=rsm[:, q:q + 1])\
                            .then_inc(s["al_ready"], 1)
                    more(lambda: relu_keys(gn))
                    with act.If(i < 1):
                        k_hi(4, kstC[:, u, :, :], u)

            act.wait_ge(s["av_done"], NB + 2 * Q)
            with act.Fori(0, 2) as i:
                for u in range(2):
                    g = 2 * i + u
                    gn = g + 1 if u == 0 else G // 2
                    d0 = 3 * MD * g
                    dst = (hA, hBt)[u]
                    for m in range(MD + 1):
                        if m < MD:
                            act.wait_ge(s["d_pre"], d0 + m + 1)
                            act.wait_ge(s["d_h32"], MD * g + m + 1)
                            fn(silD[:, m % 2, :], ps[:, 2 + m % 2, :], ACT.Silu, scale=scol[:, 0, m:m + 1])\
                                .then_inc(s["d_act"], 1)
                        if m:
                            act.wait_ge(s["d_h32"], MD * g + m + 2)
                            fn(dst[:, 0, m - 1, :], h32[:, (m - 1) % 2, :], ACT.Copy).then_inc(s["d_hi"], 1)
                    for idx in range(MD, 3 * MD):
                        m, L = idx % MD, idx // MD
                        if L == 2 and m == 4:
                            nxt = lambda: x_hi(3 * G + gn, 1 - u)
                            nxt() if u == 0 else if_more(act, i, nxt)
                        act.wait_ge(s["d_pre"], d0 + idx + 1)
                        act.wait_ge(s["d_lo"], d0 + idx + 1)
                        fn(h32[:, m % 2, :], ps[:, 2 + m % 4, :], ACT.Gelu, scale=scol[:, L + 1, m:m + 1])\
                            .then_inc(s["d_act"], 1)

        @block.vector
        def _(dve):
            v = nc.vector
            dve.sem_inc(s["c_ready"], 2)
            dve.sem_inc(s["pv_used"], 2)
            dve.sem_inc(s["hf_ready"], 2)
            dve.sem_inc(s["hlo_ready"], 2)
            dve.sem_inc(s["xB_done"], 2)
            dve.sem_inc(s["xC_done"], 2)
            dve.sem_inc(s["xD_done"], 2)
            dve.sem_inc(s["mask_free"], 1)
            dve.sem_inc(s["qrc_done"], KD)
            dve.sem_inc(s["sm_ready"], 1)
            dve.sem_inc(s["at_ready"], 1)
            dve.sem_inc(s["d_h32"], 2)
            dve.sem_inc(s["d_lo"], 2)

            def x_stats(n, b0):
                ch = Chain(dve, s["dve_prep"], 2 * Q + 1, n)
                for q in range(Q):
                    ch.step(v.bn_stats(st6[:, q, :], x[:, b0 + q, :]))
                ch.settle_apart()
                for q in range(Q):
                    ch.step(v.bn_aggr(mv[:, q, :], st6[:, q, :]))
                ch.settle()
                ch.end()
                v.tensor_scalar(ve[:, :], mv[:, :, 1], 1e-5, None, ALU.add).then_inc(s["mv_ready"], 1)

            def x_norm(n, b0):
                dve.wait_ge(s["rstd_ready"], n + 1)
                for q in range(Q):
                    last = v.tensor_scalar(xn[:, q, :], x[:, b0 + q, :], mv[:, q, 0:1], rstd[:, q:q + 1],
                                           ALU.subtract, ALU.mult)
                last.then_inc(s["xn_ready"], 1)

            def x_lo(n, par):
                for c in range(KD):
                    dve.wait_ge(s["xhi_done"], KD * n + c + 1)
                    v.tensor_tensor(xT[:, par, 1, c, :], tr_bank(c), xT[:, par, 0, c, :], ALU.subtract)\
                        .then_inc(s["xlo_done"], 1)

            A2 = 9

            def gate_a(g):
                dve.wait_ge(s["gate_moved"], 32 * (g + 1))
                ch = Chain(dve, s["dve_a2"], A2, g)
                ch.step(v.tensor_scalar(fmn[:, :], gf[:, :], gb[:, 1:2], None, ALU.add))
                ch.settle()
                v.scalar_tensor_tensor(out=fab[:, :], in0=fmn[:, :], scalar=-1.0, in1=fmn[:, :], op0=ALU.mult,
                                       op1=ALU.max).then_inc(s["ab_ready"], 1)
                return ch

            def gate_b(g, ch):
                dve.wait_ge(s["ln_ready"], g + 1)
                ch.settle()
                ch.step(v.scalar_tensor_tensor(out=fl[:, :], in0=fmn[:, :], scalar=0.0, in1=fl[:, :],
                                               op0=ALU.min, op1=ALU.subtract))
                ch.settle()
                ch.step(v.tensor_tensor_scan(cs[:, :], one_r[:, :], fl[:, :], 0.0, ALU.mult, ALU.add))
                ch.settle()
                ch.step(v.scalar_tensor_tensor(out=Z[:, 1, :], in0=gi[:, :], scalar=gb[:, 0:1], in1=cs[:, :],
                                               op0=ALU.add, op1=ALU.subtract))
                ch.settle()
                ch.step(v.tensor_scalar(Z[:, 1, :], Z[:, 1, :], -1.0, None, ALU.mult))
                ch.settle()
                ch.step(v.tensor_tensor_scan(Z[:, 0, :], Z[:, 1, :], Z[:, 1, :], BIG, ALU.min, ALU.min))
                ch.settle()
                v.tensor_tensor(Er[:, :], Z[:, 0, :], cs[:, :], ALU.subtract).then_inc(s["ncs_ready"], 1)

            def gate_c(g, ch):
                ch.step(v.tensor_copy(zp[:, 0, :, :], Z[:, :, :]))
                ch.settle()
                ch.step(v.tensor_tensor(zr[:, :, :], Z[:, :, :], zp[:, 0, :, :], ALU.subtract))
                ch.settle()
                ch.step(v.tensor_copy(zp[:, 1, :, :], zr[:, :, :]))
                ch.settle()
                v.tensor_tensor(zp[:, 2, :, :], zr[:, :, :], zp[:, 1, :, :], ALU.subtract).then_inc(s["z_ready"], 1)
                ch.end()

            def floor_copy(g, par):
                dve.wait_ge(s["er_turned"], g + 1)
                v.tensor_scalar(ET[:, par, :], ps[:, TR + 1, 0:NR], EPS, None, ALU.add).then_inc(s["et_ready"], 1)

            def weigh(g, k):
                n, quad = UN * g + k, k % 2
                dve.wait_ge(s["d_ready"], n + 3)
                dve.wait_ge(s["qk_done"], n + 5)
                dve.wait_ge(s["pv_done"], n + 1)
                v.scalar_tensor_tensor(out=Ct[:, quad, :, :].rearrange("p j t -> p (j t)"), in0=ps[:, QK + quad, :],
                                       scalar=RS_DH, in1=Dt[:, quad, :, :].rearrange("p j t -> p (j t)"),
                                       op0=ALU.mult, op1=ALU.mult).then_inc(s["c_ready"], 1)

            def finish(g, u, k):
                n, q, quad = UN * g + k, k // 2, k % 2
                ch = Chain(dve, s["dve_unit"], 4, n)
                at = 2 * quad * VW
                pvb = ps[:, PV + quad, 0:Q * PVW].rearrange("p (j w) -> p j w", j=Q)
                floor = ET[:, u, :].rearrange("p (j a q) -> p j a q", a=2, q=Q)[:, :, quad, q]
                dve.wait_ge(s["pv_done"], n + 3)
                ch.step(v.tensor_scalar(den[:, 0, :], pvb[:, :, at + DH], -1.0, EPS, ALU.mult, ALU.add))
                ch.step(v.scalar_tensor_tensor(out=den[:, 1, :], in0=pvb[:, :, at + DH], scalar=EPS, in1=floor,
                                               op0=ALU.add, op1=ALU.max))
                ch.settle()
                ch.step(v.tensor_tensor(den[:, 1, :], den[:, 0, :], den[:, 1, :], ALU.max))
                ch.settle()
                ch.step(v.reciprocal(den[:, 2, :], den[:, 1, :]))
                ch.settle()
                v.tensor_tensor(hm[:, q % 2, Q * quad:Q * quad + Q, :], pvb[:, :, at:at + DH],
                                den[:, 2, :].rearrange("p (j a) -> p j a", a=1).to_broadcast([P, Q, DH]), ALU.mult)\
                    .then_inc(s["pv_used"], 1)
                ch.end()
                if quad:
                    b = Q * g + q
                    hc = Chain(dve, s["dve_b"], 3, b)
                    dve.wait_ge(s["pv_used"], n + 3)
                    hc.step(v.bn_stats(h6[:, :], hm[:, q % 2, :, :].rearrange("p h d -> p (h d)")))
                    hc.settle_apart()
                    hc.step(v.bn_aggr(hmv[:, 0, :], h6[:, :]))
                    hc.settle()
                    v.tensor_scalar(hve[:, 0:1], hmv[:, 0, 1:2], 1e-5, None, ALU.add).then_inc(s["hstat_ready"], 1)
                    hc.end()

            def head_norm(g, q):
                b = Q * g + q
                h = hm[:, q % 2, :, :].rearrange("p h d -> p (h d)")
                ch = Chain(dve, s["dve_c"], 1, b)
                dve.wait_ge(s["hrs_ready"], b + 1)
                ch.step(v.scalar_tensor_tensor(out=h, in0=h, scalar=hmv[:, 0, 0:1], in1=lns[:, :],
                                               op0=ALU.subtract, op1=ALU.mult))
                ch.settle()
                v.scalar_tensor_tensor(out=x[:, b, :], in0=h, scalar=hrs[:, 0:1], in1=x[:, b, :],
                                       op0=ALU.mult, op1=ALU.add).then_inc(s["xA_done"], 1)

            v.memset(one_r[:, :], 1.0)
            v.memset(onec[:, :], 1.0)
            v.memset(facc[:, :], 0.0)
            dve.wait_ge(s["x_first"], 16)
            x_stats(0, 0)
            v.memset(Qb[:, :, :, :, :, :].bitcast(F32), 0.0).then_inc(s["const_set"], 1)
            v.memset(V[:, :, :, :, :], 1.0).then_inc(s["const_set"], 1)
            x_norm(0, 0)
            dve.wait_ge(s["consts"], CONSTS)
            v.tensor_copy(idb[:, :], idf[:, :]).then_inc(s["idb_ready"], 1)
            x_lo(0, 0)
            dve.wait_ge(s["x_rest"], 16 * (G - 1))
            x_stats(1, Q)
            x_norm(1, Q)
            ch = gate_a(0)
            gate_b(0, ch)
            gate_c(0, ch)
            floor_copy(0, 0)
            with dve.Fori(0, 2) as i:
                for u in range(2):
                    g = 2 * i + u
                    gn = g + 1 if u == 0 else G // 2
                    more = (lambda f: f()) if u == 0 else (lambda f: if_more(dve, i, f))
                    state = {}
                    for k in range(UN):
                        weigh(g, k)
                        if k:
                            finish(g, u, k - 1)
                        if k >= 3 and k % 2:
                            head_norm(g, (k - 3) // 2)
                        if k == 0:
                            x_lo(g + 1, 1 - u)
                        if k == 3:
                            more(lambda: state.update(ch=gate_a(gn)))
                        if k == 4:
                            def rest():
                                gate_b(gn, state["ch"])
                                gate_c(gn, state["ch"])
                            more(rest)
                        if k == 5:
                            if u == 0:
                                dve.wait_ge(s["xA_done"], Q * g + 1)
                                x_stats(g + 2, 8 - 8 * i)
                            else:
                                more(lambda: x_stats(3, 3 * Q))
                        if k == 6:
                            if u == 0:
                                x_norm(g + 2, 8 - 8 * i)
                            else:
                                more(lambda: x_norm(3, 3 * Q))
                    more(lambda: floor_copy(gn, 1 - u))
                    finish(g, u, UN - 1)
                    head_norm(g, Q - 1)

            dve.wait_ge(s["flag_tot"], 1)
            v.tensor_scalar(fint[:, :], ps[0:1, OB, 0:1], 0.0, None, ALU.is_gt).then_inc(s["flag_ready"], 1)
            dve.wait_ge(s["xA_done"], NB)
            with dve.Fori(0, 2) as i:
                for u in range(2):
                    g = 2 * i + u
                    gn = g + 1 if u == 0 else G // 2
                    b1 = Q * (g + 1) if u == 0 else 8 - 8 * i
                    dve.wait_ge(s["xB_done"], Q * g + 2)
                    x_stats(G + g + 1, b1)
                    for m in range(MB + 1):
                        n = MB * g + m
                        if m == 1:
                            x_norm(G + g + 1, b1)
                        if m < MB:
                            dve.wait_ge(s["hlo_ready"], n + 1)
                            dve.wait_ge(s["silu_ready"], n + 3)
                            v.scalar_tensor_tensor(out=hfB[:, m % 2, :], in0=ps[:, UB + m % 2, :], scalar=SCALE_B,
                                                   in1=silB[:, m % 2, :], op0=ALU.mult, op1=ALU.mult)\
                                .then_inc(s["hf_ready"], 1)
                        if m:
                            dve.wait_ge(s["hhi_ready"], n)
                            v.tensor_tensor(hB[:, 1, m - 1, :], hfB[:, (m - 1) % 2, :], hB[:, 0, m - 1, :],
                                            ALU.subtract).then_inc(s["hlo_ready"], 1)
                        if m == 4:
                            x_lo(G + g + 1, 1 - u)
                    for q in range(Q):
                        dve.wait_ge(s["down_done"], Q * g + q + 1)
                        b = Q * g + q
                        v.scalar_tensor_tensor(out=x[:, b, :], in0=ps[:, OB + q % 2, 0:D], scalar=SCALE_B,
                                               in1=x[:, b, :], op0=ALU.mult, op1=ALU.add).then_inc(s["xB_done"], 1)

            dve.wait_ge(s["xB_done"], NB + 2)
            x_stats(2 * G + 1, Q)
            x_norm(2 * G + 1, Q)

            def scale_queries(g):
                for m in range(KD):
                    dve.wait_ge(s["qr_done"], KD * g + m + 1)
                    v.tensor_scalar(qr[:, m, :], ps[:, PJ + m, :], 0.0, diag[:, m:m + 1], ALU.max, ALU.mult)\
                        .then_inc(s["qrc_done"], 1)

            scale_queries(0)
            with dve.Fori(0, 2) as i:
                for u in range(2):
                    g = 2 * i + u
                    gn = g + 1 if u == 0 else G // 2
                    more = (lambda f: f()) if u == 0 else (lambda f: if_more(dve, i, f))
                    dve.wait_ge(s["mask_ld"], 16 * (g + 1))
                    v.tensor_scalar(mf[:, :, :], mk[:, :, :], -NEG, NEG, ALU.mult, ALU.add).then_inc(s["mask_free"], 1)
                    dve.wait_ge(s["sc_done"], g + 1)
                    dve.wait_ge(s["mask_free"], g + 2)
                    ch = Chain(dve, s["dve_d"], Q + 2, g)
                    ch.start_apart()
                    for q in range(Q):
                        ch.step(v.tensor_tensor_reduce(sc[:, q, :], ps[:, SCB, q * S:(q + 1) * S], mf[:, q, :], 1.0,
                                                       -BIG, ALU.add, ALU.max, smx[:, q:q + 1]))
                    ch.settle()
                    v.tensor_scalar(nmx[:, :], smx[:, :], -1.0, None, ALU.mult).then_inc(s["sm_ready"], 1)
                    x_lo(2 * G + g + 1, 1 - u)
                    dve.wait_ge(s["at_done"], g + 1)
                    v.tensor_copy(alT[:, :, :].rearrange("p q t -> p (q t)"), ps[:, ATB, :]).then_inc(s["at_ready"], 1)
                    more(lambda: scale_queries(gn))
                    ch.step(v.reciprocal(rrs[:, :], rsm[:, :]))
                    ch.settle()
                    ch.end()
                    for q in range(Q):
                        b = Q * g + q
                        dve.wait_ge(s["av_done"], b + 2 * Q + 1)
                        v.scalar_tensor_tensor(out=x[:, b, :], in0=ps[:, OB + q % 2, 0:D], scalar=rrs[:, q:q + 1],
                                               in1=x[:, b, :], op0=ALU.mult, op1=ALU.add).then_inc(s["xC_done"], 1)
                    if u == 0:
                        dve.wait_ge(s["xC_done"], Q * g + Q)
                        x_stats(2 * G + g + 2, 8 - 8 * i)
                        x_norm(2 * G + g + 2, 8 - 8 * i)
                    else:
                        def ahead():
                            dve.wait_ge(s["xC_done"], 2 * Q)
                            x_stats(2 * G + 3, 3 * Q)
                            x_norm(2 * G + 3, 3 * Q)
                        more(ahead)

            dve.wait_ge(s["av_done"], NB + 2 * Q)
            dve.wait_ge(s["xC_done"], NB + 2)
            with dve.Fori(0, 2) as i:
                for u in range(2):
                    g = 2 * i + u
                    gn = g + 1 if u == 0 else G // 2
                    d0 = 3 * MD * g
                    dst = (hA, hBt)[u]
                    for m in range(MD + 1):
                        if m < MD:
                            dve.wait_ge(s["d_lo"], d0 + m + 1)
                            dve.wait_ge(s["d_act"], d0 + m + 3)
                            v.scalar_tensor_tensor(out=h32[:, m % 2, :], in0=ps[:, 4 + m % 2, :],
                                                   scalar=scol[:, 1, m:m + 1], in1=silD[:, m % 2, :],
                                                   op0=ALU.mult, op1=ALU.mult).then_inc(s["d_h32"], 1)
                        if m:
                            dve.wait_ge(s["d_hi"], MD * g + m)
                            v.tensor_tensor(dst[:, 1, m - 1, :], h32[:, (m - 1) % 2, :], dst[:, 0, m - 1, :],
                                            ALU.subtract).then_inc(s["d_lo"], 1)
                    for idx in range(MD, 3 * MD):
                        m, L = idx % MD, idx // MD
                        dst = (hA, hBt)[(L + u) % 2]
                        if L == 2 and m == 0:
                            nxt = lambda: x_stats(3 * G + gn, Q * gn)
                            nxt() if u == 0 else if_more(dve, i, nxt)
                        if L == 2 and m == 2:
                            nxt = lambda: x_norm(3 * G + gn, Q * gn)
                            nxt() if u == 0 else if_more(dve, i, nxt)
                        if L == 2 and m == 5:
                            nxt = lambda: x_lo(3 * G + gn, 1 - u)
                            nxt() if u == 0 else if_more(dve, i, nxt)
                        dve.wait_ge(s["d_act"], d0 + idx + 3)
                        v.tensor_copy(dst[:, 0, m, :], h32[:, m % 2, :]).then_inc(s["dh_own"], 1)
                        dve.wait_ge(s["dh_own"], 2 * MD * g + idx - MD + 1)
                        v.tensor_tensor(dst[:, 1, m, :], h32[:, m % 2, :], dst[:, 0, m, :], ALU.subtract)\
                            .then_inc(s["d_lo"], 1)
                    for q in range(Q):
                        b = Q * g + q
                        dve.wait_ge(s["d_out"], b + 2)
                        dve.wait_ge(s["xD_done"], b + 1)
                        v.tensor_tensor(ot[:, q % 2, :], ps[:, OB + q % 2, 0:D], s3[:, :], ALU.mult)\
                            .then_inc(s["ot_ready"], 1)
                        dve.wait_ge(s["ot_ready"], b + 1)
                        v.tensor_tensor(x[:, b, :], x[:, b, :], ot[:, q % 2, :], ALU.add).then_inc(s["xD_done"], 1)


def if_more(eng, i, f):
    with eng.If(i < 1):
        f()


def kernel(x, ctx_1024, mask_BxS2_if1, L0_xattn_igate_w, L0_xattn_igate_b, L0_xattn_fgate_w, L0_xattn_fgate_b,
           L0_xattn_ln_scale, L0_ffn_w_gate, L0_ffn_w_up, L0_ffn_w_down, L1_xattn_W, L1_xattn_diagonal,
           L1_ffn_w1_w, L1_ffn_w1_s, L1_ffn_w2_w, L1_ffn_w2_s, L1_ffn_h1_w, L1_ffn_h1_s, L1_ffn_h2_w,
           L1_ffn_h2_s, L1_ffn_w3_w, L1_ffn_w3_s):
    import numpy as np
    import concourse.bacc as _bacc
    from concourse.bass_utils import run_bass_kernel_spmd as _run

    def rows(w):
        t = np.asarray(w).T
        return np.ascontiguousarray(t.reshape(t.shape[0] // P, P, t.shape[1]).transpose(1, 0, 2))

    def cols(v):
        return np.asarray(v).reshape(-1, P).T

    x, ctx = np.asarray(x), np.asarray(ctx_1024)
    order = np.arange(NH).reshape(NH // Q, Q).T.ravel()
    gate_w = np.concatenate([np.asarray(L0_xattn_igate_w)[order], np.asarray(L0_xattn_fgate_w)[order]], axis=0)
    gate_b = np.stack([np.repeat(np.asarray(b)[order], Q) for b in (L0_xattn_igate_b, L0_xattn_fgate_b)], 1)
    scales = np.zeros((P, 4, MD), np.float32)
    for n, v in enumerate((L1_ffn_w1_s, L1_ffn_w2_s, L1_ffn_h1_s, L1_ffn_h2_s)):
        scales[:, n, :] = cols(v)
    w_all = np.concatenate([rows(w).reshape(P, -1) for w in (L1_ffn_w1_w, L1_ffn_w2_w, L1_ffn_w3_w, L1_ffn_h1_w,
                                                             L1_ffn_h2_w)], axis=1)
    import ml_dtypes
    bf = np.dtype(ml_dtypes.bfloat16)
    tri = np.zeros((P, Q, S), np.float32)
    t_, s_ = np.meshgrid(np.arange(P), np.arange(S), indexing="ij")
    tri[:, :, :] = np.where(t_ > s_, MASKED, 0.0)[:, None, :]
    ones_rows = np.zeros((RA, Q, 2, Q, S), np.float32)
    ones_rows[0:3] = -1.0
    for r in range(3, RA):
        ones_rows[r, (r - 3) % Q] = 1.0
    arrays = {
        "x_in": x,
        "ctx_in": ctx,
        "ctxT_in": np.ascontiguousarray(ctx.reshape(NB * S, KD, P).transpose(2, 1, 0)),
        "mask_in": np.asarray(mask_BxS2_if1),
        "gw_in": rows(gate_w),
        "gb_in": gate_b,
        "lns_in": np.asarray(L0_xattn_ln_scale),
        "l0gu_in": np.stack([rows(L0_ffn_w_gate), rows(L0_ffn_w_up)], axis=1),
        "l0d_in": rows(L0_ffn_w_down),
        "xaw_in": rows(L1_xattn_W),
        "diag_in": cols(L1_xattn_diagonal),
        "w_all_in": w_all,
        "s_cols_in": scales,
        "s3_in": np.asarray(L1_ffn_w3_s),
        "ident_in": np.eye(P, dtype=np.float32),
        "tri_in": tri.astype(bf),
        "ones_rows_in": ones_rows.astype(bf),
    }
    nc = _bacc.Bacc("TRN2", target_bir_lowering=False, num_devices=1)
    arrays = {k: np.ascontiguousarray(a) for k, a in arrays.items()}
    args = {k: nc.dram_tensor(k, a.shape, mybir.dt.from_np(a.dtype), kind="ExternalInput").ap()
            for k, a in arrays.items()}
    args["out"] = nc.dram_tensor("out", (NB, S, D), F32, kind="ExternalOutput").ap()
    two_layers(nc, **args)
    r = _run(nc, [arrays], core_ids=[0])
    return r.results[0]["out"]
```

```python
from contextlib import ExitStack

import concourse.bass as bass
from concourse import mybir
from concourse.alu_op_type import AluOpType as ALU

ACT = mybir.ActivationFunctionType
F32 = mybir.dt.float32
F32R = mybir.dt.float32r
BF16 = mybir.dt.bfloat16
I32 = mybir.dt.int32
U16 = mybir.dt.uint16
AX = mybir.AxisListType

P = 128
NB, S, D = 16, 128, 256
NH, DH = 8, 32
KD = D // P
Q = 4
G = NB // Q
GT = Q * S
HB = 768
MB = HB // P
HD = 1024
MD = HD // P
VW = DH + 1
PVW = 3 * VW
UN = 2 * Q
RA = 3 + 3 * Q
MOVES = 16 * 6
MASKED = 1e30
BIG = 3e38
SCALE_B = 1.0 / 127.0
RS_DH = float(DH) ** -0.5
NEG = -10000.0
EXP_ONLY, EXP_AND_LN, SILU = 0, 6, 18
EPS = 1e-6
CONSTS = 16 * 10
NRAW = 2 * G
W_ALL = 2 * KD * HD + MD * D + 2 * MD * HD
SEC_W1, SEC_W2 = 0, KD * HD
SEC_W3 = 2 * KD * HD
SEC_H1 = SEC_W3 + MD * D
SEC_H2 = SEC_H1 + MD * HD
FLAG_BUFS = 4
FLAG_ITEMS = G * FLAG_BUFS
FLAG_W = W_ALL // FLAG_ITEMS
RING = 2
ITEMS_G = 3 * MD + 2


class Chain:

    def __init__(self, eng, sem, per, index):
        self.eng, self.sem, self.per, self.base, self.n = eng, sem, per, index * per, 0

    def step(self, ins):
        ins.then_inc(self.sem, 1)
        self.n += 1

    def settle(self):
        self.eng.wait_ge(self.sem, self.base + self.n)

    def settle_apart(self):
        self.settle()
        self.eng.sem_inc(self.sem, 1)
        self.n += 1

    def start_apart(self):
        self.eng.sem_inc(self.sem, 1)
        self.n += 1

    def end(self):
        assert self.n == self.per, (self.n, self.per)


def two_layers(nc, x_in, ctx_in, ctxT_in, mask_in, gw_in, gb_in, lns_in, l0gu_in, l0d_in, xaw_in, diag_in,
               w_all_in, s_cols_in, s3_in, ident_in, tri_in, ones_rows_in, out):
    es = ExitStack()
    base = [(nc.sbuf_base + 63) // 64 * 64]
    sizes = {F32: 4, F32R: 4, I32: 4, BF16: 2, U16: 2}

    def place(at, name, shape, dt):
        n = sizes[dt]
        for d in shape[1:]:
            n *= d
        t = nc.alloc_sbuf_tensor_at(name, shape, dt, offset=at[0])
        at[0] += (n + 31) // 32 * 32
        return t

    def sem(name):
        return es.enter_context(nc.semaphore(name))

    with es:
        x = place(base, "x", [P, NB, D], F32)
        w1 = place(base, "w1", [P, KD, HD], F32R)
        w2 = place(base, "w2", [P, KD, HD], F32R)
        w3 = place(base, "w3", [P, MD, D], F32R)
        ring_at = [base[0] - 3 * KD * HD * 4]
        rawgu = place([ring_at[0]], "rawgu", [P, 2, KD, HB], F32)
        looked = place([ring_at[0]], "looked", [P, FLAG_BUFS, FLAG_W], F32)
        assert FLAG_BUFS * FLAG_W <= 3 * KD * HD
        ring = place(ring_at, "ring", [P, RING, MD, P], F32)
        rawd_at = [ring_at[0] + 2 * KD * HB * 4 - RING * MD * P * 4]
        rawd = place(rawd_at, "rawd", [P, 2, MB // 2, D], F32)
        rawx = place(rawd_at, "rawx", [P, KD, D], F32)
        CtB = place(rawd_at, "CtB", [P, 2, Q, S], F32)
        assert rawd_at[0] <= base[0]
        xT = place(base, "xT", [P, 2, 2, KD, GT], F32R)
        xn = place(base, "xn", [P, Q, D], F32)
        stage_at = [base[0]]
        stage = place(base, "stage", [P, 2, HD], F32)
        kstC = place([stage_at[0]], "kstC", [P, 2, KD, GT], F32)
        silD = place(stage_at, "silD", [P, 2, GT], F32)
        h32 = place(stage_at, "h32", [P, 2, GT], F32)
        xaw = place(base, "xaw", [P, 2, KD, D], F32R)
        idf = place(base, "idf", [P, P], F32)
        idb = place(base, "idb", [P, P], BF16)
        tri = place(base, "tri", [P, Q, S], BF16)
        lns = place(base, "lns", [P, D], F32)
        s3 = place(base, "s3", [P, D], F32)
        st6 = place(base, "st6", [P, Q, 6], F32)
        mv = place(base, "mv", [P, Q, 2], F32)
        ve = place(base, "ve", [P, Q], F32)
        rstd = place(base, "rstd", [P, Q], F32)
        mhalf = place(base, "mhalf", [P, Q], F32)
        h6 = place(base, "h6", [P, 6], F32)
        hmv = place(base, "hmv", [P, 2, 2], F32)
        hve = place(base, "hve", [P, 2], F32)
        hrs = place(base, "hrs", [P, 2], F32)
        scol = place(base, "scol", [P, 4, MD], F32)
        diag = place(base, "diag", [P, KD], F32)
        facc = place(base, "facc", [P, 2 * G + FLAG_ITEMS], F32)
        fsum = place(base, "fsum", [P, 2], F32)
        onec = place(base, "onec", [P, 1], F32)
        probe = place(base, "probe", [P, 2], F32)
        fint = place(base, "fint", [1, 2], I32)
        ot = place(base, "ot", [P, 2, D], F32)
        den = place(base, "den", [P, 3, 2, Q], F32)
        smx = place(base, "smx", [P, Q], F32)
        nmx = place(base, "nmx", [P, Q], F32)
        rsm = place(base, "rsm", [P, Q], F32)
        rrs = place(base, "rrs", [P, Q], F32)
        r1 = [base[0]]
        l0 = place(r1, "l0", [P, 2, 2, KD, HB], F32R)
        l0d = place(r1, "l0d", [P, 2, MB, D], F32R)
        kT = place(r1, "kT", [P, 2, 2, KD, GT], F32R)
        V = place(r1, "V", [P, 2, Q, NH + 2, VW], F32)
        mk = place(r1, "mk", [P, Q, S], I32)
        c1 = [base[0]]
        qr = place(c1, "qr", [P, KD, GT], F32)
        kr = place(c1, "kr", [P, KD, GT], F32)
        mf = place(c1, "mf", [P, Q, S], F32)
        sc = place(c1, "sc", [P, Q, S], F32)
        al = place(c1, "al", [P, Q, S], F32)
        alT = place(c1, "alT", [P, Q, S], F32)
        assert c1[0] <= base[0] + 36 * 1024
        d1 = [base[0]]
        hA = place(d1, "hA", [P, 2, MD, GT], F32R)
        hBt = place(d1, "hBt", [P, 2, MD, GT], F32R)
        r2 = [max(r1[0], d1[0])]
        r2b = [r2[0] + MD * HD * 4]
        h1 = place([r2[0]], "h1", [P, MD, HD], F32R)
        h2 = place([r2b[0]], "h2", [P, MD, HD], F32R)
        a2 = [r2[0]]
        Qb = place(a2, "Qb", [P, 2, 2, KD, Q, S], F32R)
        kstA = place(a2, "kstA", [P, KD, GT], F32)
        Dt = place(a2, "Dt", [P, 2, Q, S], F32)
        Ct = place(a2, "Ct", [P, 2, Q, S], F32)
        gw = place(a2, "gw", [P, 2, 2 * KD, P], F32R)
        assert a2[0] <= r2b[0]
        a3 = [r2b[0]]
        Rr = place(a3, "Rr", [RA, 2, Q, 2, Q, S], BF16)
        Lr = place(a3, "Lr", [RA, 2, 2, Q, S], BF16)
        gsb = place(a3, "gsb", [2 * NH, GT], F32)
        NR = NH * Q
        gi = place(a3, "gi", [NR, S], F32)
        gf = place(a3, "gf", [NR, S], F32)
        gb = place(a3, "gb", [NR, 2], F32)
        fab = place(a3, "fab", [NR, S], F32)
        fmn = place(a3, "fmn", [NR, S], F32)
        fl = place(a3, "fl", [NR, S], F32)
        one_r = place(a3, "one_r", [NR, S], F32)
        cs = place(a3, "cs", [NR, S], F32)
        Z = place(a3, "Z", [NR, 2, S], F32)
        zr = place(a3, "zr", [NR, 2, S], F32)
        zp = place(a3, "zp", [NR, 3, 2, S], BF16)
        Er = place(a3, "Er", [NR, S], F32)
        ET = place(a3, "ET", [P, 2, NR], F32)
        hm = place(a3, "hm", [P, 2, NH, DH], F32)
        graw = place(a3, "graw", [P, 3 * KD, 2 * NH], F32)
        gsum = place(a3, "gsum", [P, KD, 2 * NH], F32)
        assert a3[0] <= nc.sbuf_usable_end, a3[0]
        b3 = [r2b[0]]
        hB = place(b3, "hB", [P, 2, MB, GT], F32R)
        silB = place(b3, "silB", [P, 2, GT], F32)
        hfB = place(b3, "hfB", [P, 2, GT], F32)
        assert b3[0] <= nc.sbuf_usable_end, b3[0]

        ps = es.enter_context(nc.psum_tensor("ps", [P, 8, GT], F32))
        TR, EX, QK, PV = 0, 2, 4, 6
        GB, UB, OB = 2, 4, 6
        PJ, SCB, ATB = 2, 4, 5

        names = """x_first x_second x_rest ident_ld gw_ld consts mask_ld mask_free hi_ld
            raw_seen gw_lo gw_cast const_set mv_ready rstd_ready xn_ready tr_done xhi_done xlo_done x_free
            khi_done klo_done gate_done gate_copied gate_moved ab_ready ln_ready ncs_ready er_ready z_ready
            z_moved er_turned et_ready expo_done d_ready qk_done c_ready pv_done pv_used hstat_ready hrs_ready
            flag_used flag_sums flag_tot flag_ready l0_lo gu_done silu_ready hf_ready hhi_ready hlo_ready
            down_done xA_done xB_done kr_done qr_done krc_done qrc_done sc_done sm_ready al_ready at_done at_ready
            av_done xC_done d_pre d_sil d_h32 d_hi d_lo d_act d_out xD_done
            idb_ready dh_own ot_ready dve_prep dve_a2 dve_unit dve_b centred dve_d pool_own act_own out_done pe_own w_ld h1_ld h2_ld""".split()
        s = {n: sem(n) for n in names}
        qb_ld = [sem(f"qb_ld{i}") for i in range(2)]
        flag_ld = [sem(f"flag_ld{i}") for i in range(FLAG_BUFS)]
        ring_ld = [sem(f"ring_ld{i}") for i in range(RING)]
        ctxT_ld = [sem(f"ctxT_ld{i}") for i in range(2)]
        v_ld = [sem(f"v_ld{i}") for i in range(2)]

        Cts = (Ct, CtB)

        def tr_bank(c):
            return ps[:, TR + c, :]

        def move_rows(sp, u):
            for part in range(3):
                sp.dma_start(Rr[part:part + 1, u, :, :, :, :], zp[:, part, 0, :]).then_inc(s["z_moved"], 16)
                sp.dma_start(Lr[3 + part * Q:3 + part * Q + Q, u, :, :, :], zp[:, part, 1, :])\
                    .then_inc(s["z_moved"], 16)

        block = es.enter_context(nc.Block())

        @block.sync
        def _(sp):
            sp.dma_start(x[:, 0:Q, :], x_in[0:Q].rearrange("b s d -> s b d")).then_inc(s["x_first"], 16)
            sp.dma_start(idf[:, :], ident_in).then_inc(s["ident_ld"], 16)
            sp.dma_start(kstA[:, :, :], ctxT_in[:, :, 0:GT]).then_inc(ctxT_ld[0], 16)
            sp.dma_start(graw[:, :, :], gw_in).then_inc(s["gw_ld"], 16)
            sp.dma_start(x[:, Q:2 * Q, :], x_in[Q:2 * Q].rearrange("b s d -> s b d")).then_inc(s["x_second"], 16)
            sp.dma_start(gb[:, :], gb_in).then_inc(s["consts"], 16)
            for u in range(2):
                sp.dma_start(Rr[3:RA, u, :, :, :, :], ones_rows_in[3:RA]).then_inc(s["consts"], 16)
                sp.dma_start(Lr[0:3, u, :, :, :], ones_rows_in[0:3, 0]).then_inc(s["consts"], 16)
            sp.dma_start(tri[:, :, :], tri_in).then_inc(s["consts"], 16)
            sp.dma_start(lns[:, :], lns_in.partition_broadcast(P)).then_inc(s["consts"], 16)
            sp.dma_start(s3[:, :], s3_in.partition_broadcast(P)).then_inc(s["consts"], 16)
            sp.dma_start(scol[:, :, :], s_cols_in).then_inc(s["consts"], 16)
            sp.dma_start(diag[:, :], diag_in).then_inc(s["consts"], 16)
            sp.wait_ge(s["klo_done"], 1)
            sp.dma_start(kstA[:, :, :], ctxT_in[:, :, GT:2 * GT]).then_inc(ctxT_ld[1], 16)
            sp.wait_ge(s["const_set"], 3)
            def values(g, u):
                for q in range(Q):
                    sp.dma_start(V[:, u, q, 0:NH, 0:DH],
                                 ctx_in[Q * g + q].rearrange("t (h d) -> t h d", d=DH)).then_inc(v_ld[u], 16)

            def queries_in(g, u, q):
                if q == 0:
                    sp.wait_ge(s["xlo_done"], KD * (g + 1))
                    sp.wait_ge(s["xhi_done"], KD * (g + 1))
                sp.wait_ge(s["qk_done"], UN * g + 2 * q + 2)
                for j in range(Q):
                    sp.dma_start(Qb[DH * j:DH * j + DH, q % 2, :, :, j, :].bitcast(F32),
                                 xT[DH * j:DH * j + DH, u, :, :, q * S:(q + 1) * S].bitcast(F32))\
                        .then_inc(qb_ld[q % 2], 16)

            def gates_in(g):
                sp.wait_ge(s["gate_copied"], g + 1)
                sp.dma_start(gi[:, :], gsb[0:NH, :].rearrange("h (q t) -> h q t", q=Q)).then_inc(s["gate_moved"], 16)
                sp.dma_start(gf[:, :], gsb[NH:2 * NH, :].rearrange("h (q t) -> h q t", q=Q))\
                    .then_inc(s["gate_moved"], 16)

            def lead_in(g, u):
                values(g, u)
                queries_in(g, u, 0)
                sp.wait_ge(s["z_ready"], g + 1)
                move_rows(sp, u)
                queries_in(g, u, 1)

            gates_in(0)
            for g in range(2, G):
                sp.dma_start(x[:, Q * g:Q * g + Q, :], x_in[Q * g:Q * g + Q].rearrange("b s d -> s b d"))\
                    .then_inc(s["x_rest"], 16)
            lead_in(0, 0)
            with sp.Fori(0, 2) as i:
                for u in range(2):
                    g = 2 * i + u
                    gn = g + 1 if u == 0 else G // 2
                    with sp.If(i < 1):
                        sp.wait_ge(s["klo_done"], 2 + u)
                        sp.dma_start(kstA[:, :, :], ctxT_in[:, :, (2 + u) * GT:(3 + u) * GT])\
                            .then_inc(ctxT_ld[u], 16)
                    queries_in(g, u, 2)
                    if u == 0:
                        gates_in(gn)
                    else:
                        with sp.If(i < 1):
                            gates_in(gn)
                    queries_in(g, u, 3)
                    if u == 0:
                        lead_in(gn, 1 - u)
                    else:
                        with sp.If(i < 1):
                            lead_in(gn, 1 - u)
            for u in range(2):
                sp.dma_start(kstC[:, u, :, :], ctxT_in[:, :, u * GT:(u + 1) * GT]).then_inc(ctxT_ld[u], 16)
            sp.wait_ge(s["flag_sums"], 1)
            sp.wait_ge(s["pv_done"], NB + 2)
            with sp.Fori(0, G) as g:
                for m in range(FLAG_BUFS):
                    sp.wait_ge(s["flag_used"], FLAG_BUFS * g + m + 1)
                    sp.dma_start(looked[:, m, :], w_all_in[:, bass.ds((FLAG_BUFS * g + m) * FLAG_W, FLAG_W)])\
                        .then_inc(flag_ld[m], 16)
            with sp.Fori(0, 2) as i:
                for u in range(2):
                    g = 2 * i + u
                    gn = g + 1 if u == 0 else G // 2
                    sp.wait_ge(s["av_done"], Q * g + Q)
                    for q in range(Q):
                        sp.dma_start(V[:, u, q, 0:NH, 0:DH],
                                     ctx_in[Q * g + q].rearrange("t (h d) -> t h d", d=DH))\
                            .then_inc(v_ld[u], 16)
                    sp.wait_ge(s["mask_free"], g + 1)
                    sp.dma_start(mk[:, :, :], mask_in[bass.ds(Q * g, Q), :].partition_broadcast(P))\
                        .then_inc(s["mask_ld"], 16)
                    with sp.If(i < 1):
                        sp.wait_ge(s["klo_done"], G + u + 1)
                        sp.dma_start(kstC[:, u, :, :], ctxT_in[:, :, (2 + u) * GT:(3 + u) * GT])\
                            .then_inc(ctxT_ld[u], 16)
            sp.wait_ge(s["flag_ready"], 2)
            fl_reg = sp.value_load(fint[0:1, 1:2])
            with sp.If(fl_reg > 0):
                sp.wait_ge(s["w_ld"], 48)
                with sp.Fori(0, G) as g:
                    n = 0

                    def block_in(dst, src):
                        nonlocal n
                        if n < RING:
                            sp.wait_ge(s["d_out"], Q * g + 1)
                        else:
                            sp.wait_ge(s["d_pre"], 3 * MD * g + n - RING + 1)
                        sp.dma_start(dst, src).then_inc(ring_ld[n % RING], 16)
                        n += 1
                    for m in range(MD):
                        v = w_all_in[:, SEC_W1:SEC_W3].rearrange("p (a f) -> p a f", a=2 * KD)
                        block_in(ring[:, n % RING, 0:2 * KD, :], v[:, :, m * P:(m + 1) * P])
                    for sec in (SEC_H1, SEC_H2):
                        v = w_all_in[:, sec:sec + MD * HD].rearrange("p (a f) -> p a f", a=MD)
                        for m in range(MD):
                            block_in(ring[:, n % RING, :, :], v[:, :, m * P:(m + 1) * P])
                    for half in range(2):
                        v = w_all_in[:, SEC_W3 + half * HD:SEC_W3 + (half + 1) * HD]
                        block_in(ring[:, n % RING, :, :], v.rearrange("p (a f) -> p a f", a=MD))

        @block.gpsimd
        def _(pool):
            own = [0]

            def step(ins):
                ins.then_inc(s["pool_own"], 1)
                own[0] += 1

            def settle():
                pool.wait_ge(s["pool_own"], own[0])

            step(nc.gpsimd.memset(mhalf[:, :], -0.5))
            step(nc.gpsimd.memset(gw[:, :, :, :].bitcast(F32), 0.0))
            nc.gpsimd.memset(Qb[:, 0, :, :, :, :].bitcast(F32), 0.0).then_inc(s["const_set"], 1)
            pool.wait_ge(s["gw_ld"], 16)
            step(nc.gpsimd.tensor_tensor(gsum[:, :, :], graw[:, KD:2 * KD, :], graw[:, 2 * KD:3 * KD, :], ALU.add))
            settle()

            def inv_root(n):
                pool.wait_ge(s["mv_ready"], n + 1)
                nc.gpsimd.tensor_tensor(rstd[:, :], ve[:, :], mhalf[:, :], ALU.pow).then_inc(s["rstd_ready"], 1)

            inv_root(0)
            W = 2 * NH
            step(nc.gpsimd.tensor_copy(gw[:, 0, 0:KD, 0:W], graw[:, 0:KD, :]))
            step(nc.gpsimd.tensor_copy(gw[:, 0, KD:2 * KD, 0:W], gsum[:, :, :]))
            settle()
            nc.gpsimd.tensor_tensor(gw[:, 1, 0:KD, 0:W], graw[:, 0:KD, :], gw[:, 0, 0:KD, 0:W], ALU.subtract)\
                .then_inc(s["gw_lo"], 1)
            nc.gpsimd.tensor_tensor(gw[:, 1, KD:2 * KD, 0:W], gsum[:, :, :], gw[:, 0, KD:2 * KD, 0:W], ALU.subtract)\
                .then_inc(s["gw_lo"], 1)

            def k_lo(n, kst, u):
                pool.wait_ge(s["khi_done"], n + 1)
                nc.gpsimd.tensor_tensor(kT[:, u, 1, :, :], kst, kT[:, u, 0, :, :], ALU.subtract)\
                    .then_inc(s["klo_done"], 1)

            k_lo(0, kstA[:, :, :], 0)
            nc.gpsimd.memset(V[:, :, :, :, :], 1.0).then_inc(s["const_set"], 1)
            inv_root(1)
            k_lo(1, kstA[:, :, :], 1)
            pool.wait_ge(s["z_moved"], MOVES)
            def pieces(i, u):
                gu = (slice(None), bass.ds(i, 1), u)
                pool.dma_start(l0[:, 0, bass.ds(i, 1), u, :], l0gu_in[gu]).then_inc(s["hi_ld"], 16)
                pool.dma_start(rawgu[:, bass.ds(i, 1), u, :], l0gu_in[gu]).then_inc(s["hi_ld"], 16)
                if u == 0:
                    pool.dma_start(xaw[:, 0, bass.ds(i, 1), :], xaw_in[:, bass.ds(i, 1), :]).then_inc(s["hi_ld"], 16)
                    pool.dma_start(rawx[:, bass.ds(i, 1), :], xaw_in[:, bass.ds(i, 1), :]).then_inc(s["hi_ld"], 16)
                else:
                    m = bass.ds(i * (MB // 2), MB // 2)
                    pool.dma_start(l0d[:, 0, m, :], l0d_in[:, m, :]).then_inc(s["hi_ld"], 16)
                    pool.dma_start(rawd[:, bass.ds(i, 1), :, :].rearrange("p a m w -> p (a m) w"), l0d_in[:, m, :])\
                        .then_inc(s["hi_ld"], 16)

            pieces(0, 0)

            def lows(i, u):
                nc.gpsimd.tensor_tensor(l0[:, 1, bass.ds(i, 1), u, :], rawgu[:, bass.ds(i, 1), u, :],
                                        l0[:, 0, bass.ds(i, 1), u, :], ALU.subtract).then_inc(s["l0_lo"], 1)
                if u == 0:
                    nc.gpsimd.tensor_tensor(xaw[:, 1, bass.ds(i, 1), :], rawx[:, bass.ds(i, 1), :],
                                            xaw[:, 0, bass.ds(i, 1), :], ALU.subtract).then_inc(s["l0_lo"], 1)
                else:
                    m = bass.ds(i * (MB // 2), MB // 2)
                    nc.gpsimd.tensor_tensor(l0d[:, 1, m, :], rawd[:, bass.ds(i, 1), :, :],
                                            l0d[:, 0, m, :], ALU.subtract).then_inc(s["l0_lo"], 1)

            def h_root(b, par):
                pool.wait_ge(s["hstat_ready"], b + 1)
                nc.gpsimd.tensor_tensor(hrs[:, par:par + 1], hve[:, par:par + 1], mhalf[:, 0:1], ALU.pow)\
                    .then_inc(s["hrs_ready"], 1)

            with pool.Fori(0, 2) as i:
                for u in range(2):
                    g = 2 * i + u
                    gn = g + 1 if u == 0 else G // 2
                    if u == 0:
                        with pool.If(i > 0):
                            k_lo(G - 1, kstA[:, :, :], 1)
                            h_root(2 * Q - 1, 1)
                    else:
                        with pool.If(i < 1):
                            k_lo(2, kstA[:, :, :], 0)
                        h_root(Q * g - 1, 1)
                    h_root(Q * g, 0)
                    if u == 0:
                        inv_root(g + 2)
                    else:
                        with pool.If(i < 1):
                            inv_root(3)
                    pool.wait_ge(s["hi_ld"], 64 * (g + 1))
                    lows(i, u)
                    h_root(Q * g + 1, 1)
                    if u == 0:
                        pieces(i, 1)
                    else:
                        with pool.If(i < 1):
                            pieces(1, 0)
                    h_root(Q * g + 2, 0)
            h_root(NB - 1, 1)
            inv_root(G + 1)
            pool.wait_ge(s["xA_done"], NB)
            for u in range(2):
                k_lo(G + u, kstC[:, u, :, :], u)
            for k in range(MD):
                pool.dma_start(h1[:, k, :], w_all_in[:, SEC_H1 + k * HD:SEC_H1 + (k + 1) * HD])\
                    .then_inc(s["h1_ld"], 16)
            with pool.Fori(0, G) as g:
                inv_root(g + G + 2)
            pool.wait_ge(s["flag_sums"], 2)
            pool.dma_start(w1[:, :, :], w_all_in[:, SEC_W1:SEC_W2].rearrange("p (k f) -> p k f", k=KD))\
                .then_inc(s["w_ld"], 16)
            pool.dma_start(w2[:, :, :], w_all_in[:, SEC_W2:SEC_W3].rearrange("p (k f) -> p k f", k=KD))\
                .then_inc(s["w_ld"], 16)
            pool.dma_start(w3[:, :, :], w_all_in[:, SEC_W3:SEC_H1].rearrange("p (k f) -> p k f", k=MD))\
                .then_inc(s["w_ld"], 16)
            pool.wait_ge(s["down_done"], Q * G)
            with pool.Fori(0, 2) as i:
                for u in range(2):
                    g = 2 * i + u
                    for c in range(MD // G):
                        k = g * (MD // G) + c
                        pool.dma_start(h2[:, bass.ds(k, 1), :], w_all_in[:, bass.ds(k * HD + SEC_H2, HD)])\
                            .then_inc(s["h2_ld"], 16)
                    if u == 0:
                        inv_root(2 * G + g + 2)
                    else:
                        with pool.If(i < 1):
                            inv_root(2 * G + 3)
                    with pool.If(i < 1):
                        k_lo(G + 2 + u, kstC[:, u, :, :], u)
            with pool.Fori(0, 2) as i:
                for u in range(2):
                    g = 2 * i + u
                    gn = g + 1 if u == 0 else G // 2
                    if u == 0:
                        inv_root(3 * G + gn)
                    else:
                        with pool.If(i < 1):
                            inv_root(3 * G + gn)
                    for q in range(Q):
                        pool.wait_ge(s["xD_done"], 2 + Q * g + q + 1)
                        pool.dma_start(out[Q * g + q], x[:, Q * g + q, :]).then_inc(s["out_done"], 16)
            pool.wait_ge(s["out_done"], 16 * NB)

        @block.tensor
        def _(pe):
            mm = nc.tensor.matmul
            pe.sem_inc(s["qk_done"], 4)
            pe.sem_inc(s["pv_done"], 2)
            pe.sem_inc(s["av_done"], 2 * Q)
            pe.sem_inc(s["d_out"], 1)

            def turn_x(n, first=False):
                pe.wait_ge(s["xn_ready"], n + 1)
                if not first:
                    pe.wait_ge(s["xlo_done"], KD * n)
                for c in range(KD):
                    for q in range(Q):
                        last = nc.tensor.transpose(ps[:, TR + c, q * S:(q + 1) * S], xn[:, q, c * P:(c + 1) * P],
                                                   idf[:, :])
                last.then_inc(s["tr_done"], 1)

            def three(o, lhs, rhs, first, last, weight_moves=False):
                mm(o, lhs(0), rhs(0), start=first, stop=False)
                mm(o, lhs(0), rhs(1), start=False, stop=False)
                return mm(o, lhs(1), rhs(0), start=False, stop=last)

            def two(o, lhs, rhs, first, last, weight_moves=False):
                mm(o, lhs(0), rhs(0), start=first, stop=False)
                if weight_moves:
                    return mm(o, lhs(1), rhs(0), start=False, stop=last)
                return mm(o, lhs(0), rhs(1), start=False, stop=last)

            def gates(g, u, ctx_first=False):
                bank = ps[:, QK, :] if ctx_first else tr_bank(0)
                chunks = list(range(2 * KD))
                if ctx_first:
                    chunks = chunks[KD:] + chunks[:KD]
                for n, c in enumerate(chunks):
                    if c == 0:
                        pe.wait_ge(s["xlo_done"], KD * (g + 1))
                    if c == KD:
                        pe.wait_ge(s["klo_done"], g + 1)
                    src = (lambda p, c=c: xT[:, u, p, c, :]) if c < KD else (lambda p, c=c: kT[:, u, p, c - KD, :])
                    last = three(bank, lambda p, c=c: gw[:, p, c, :], src, n == 0, n == 2 * KD - 1)
                last.then_inc(s["gate_done"], 1)

            def turn_e(g):
                pe.wait_ge(s["er_ready"], g + 1)
                pe.sem_inc(s["pe_own"], 1)
                nc.tensor.transpose(ps[:, TR + 1, 0:NR], Er[:, :], idf[0:NR, 0:NR]).then_inc(s["er_turned"], 1)

            def expo(g, u, k):
                q, quad = k // 2, k % 2
                n = UN * g + k
                if k == 0:
                    pe.wait_ge(s["z_moved"], MOVES * (g + 1))
                pe.wait_ge(s["d_ready"], n + 1)
                mm(ps[:, EX + quad, :], Lr[:, u, quad, q, :], Rr[:, u, :, quad, q, :],
                   start=True, stop=False)
                mm(ps[:, EX + quad, :], idb[:, :], tri[:, :, :], start=False, stop=True)\
                    .then_inc(s["expo_done"], 1)

            def qk(g, u, k):
                q, quad = k // 2, k % 2
                n = UN * g + k
                if quad == 0:
                    pe.wait_ge(qb_ld[q % 2], 64 * (2 * g + q // 2 + 1))
                pe.wait_ge(s["c_ready"], n + 1)
                three(ps[:, QK + quad, :], lambda p: kT[:, u, p, quad, q * S:(q + 1) * S],
                      lambda p: Qb[:, q % 2, p, quad, :, :], True, True).then_inc(s["qk_done"], 1)

            def pv(b, par, nth, q):
                if q == 0:
                    pe.wait_ge(v_ld[par], 16 * Q * nth)
                pe.wait_ge(s["pv_used"], b + 1)
                for quad in range(2):
                    pe.wait_ge(s["c_ready"], 2 * b + quad + 3)
                    for j in range(Q):
                        h = Q * quad + j
                        last = mm(ps[:, PV + quad, j * PVW:(j + 1) * PVW], Cts[q % 2][:, quad, j, :],
                                  V[:, par, q, h:h + 3, :], start=True, stop=True)
                last.then_inc(s["pv_done"], 1)

            pe.wait_ge(s["ident_ld"], 16)
            turn_x(0, True)
            pe.wait_ge(s["gw_lo"], 2)
            pe.wait_ge(s["idb_ready"], 1)
            gates(0, 0, ctx_first=True)
            turn_x(1)
            pe.wait_ge(s["gate_copied"], 1)
            pe.wait_ge(s["consts"], CONSTS)
            pe.wait_ge(s["xlo_done"], 2 * KD)
            turn_e(0)
            with pe.Fori(0, 2) as i:
                for u in range(2):
                    g = 2 * i + u
                    gn = g + 1 if u == 0 else G // 2
                    more = (lambda f: f()) if u == 0 else (lambda f: if_more(pe, i, f))
                    for q in range(Q):
                        if q == Q - 1:
                            more(lambda: turn_e(gn))
                        for k in (2 * q, 2 * q + 1):
                            expo(g, u, k)
                            qk(g, u, k)
                        if q == 0:
                            if u == 0:
                                with pe.If(i > 0):
                                    pv(2 * Q - 1, 1, 1, Q - 1)
                            else:
                                pv(Q * g - 1, 0, 1, Q - 1)
                            more(lambda: gates(gn, 1 - u))
                        else:
                            pv(Q * g + q - 1, u, i + 1, q - 1)
                    def ahead():
                        pe.wait_ge(s["gate_copied"], gn + 1)
                        pe.wait_ge(s["et_ready"], gn + 1)
                        turn_x(g + 2 if u == 0 else 3)
                    if u == 0:
                        ahead()
                    else:
                        more(ahead)
            pe.wait_ge(s["flag_sums"], 1)
            pe.wait_ge(s["d_ready"], UN * G + 2)
            mm(ps[0:1, EX, 0:1], fsum[:, 0:1], onec[:, :], start=True, stop=True).then_inc(s["flag_tot"], 1)
            pv(NB - 1, 1, 2, Q - 1)

            pe.wait_ge(s["l0_lo"], NRAW)
            pe.wait_ge(s["c_ready"], UN * G + 2)
            pe.wait_ge(s["flag_ready"], 1)
            flag_reg = pe.value_load(fint[0:1, 0:1])

            def stage_b(general):
                by = three if general else two
                with pe.Fori(0, 2) as i:
                    for u in range(2):
                        g = 2 * i + u
                        gn = g + 1 if u == 0 else G // 2
                        pe.wait_ge(s["xlo_done"], KD * (G + g + 1))
                        for m in range(MB):
                            n = MB * g + m
                            for a, (bank, used) in enumerate(((GB, "silu_ready"), (UB, "hf_ready"))):
                                pe.wait_ge(s[used], n + 1)
                                for c in range(KD):
                                    last = by(ps[:, bank + m % 2, :],
                                                 lambda p: l0[:, p, a, c, m * P:(m + 1) * P],
                                                 lambda p: xT[:, u, p, c, :], c == 0, c == KD - 1)
                            last.then_inc(s["gu_done"], 1)
                        turn_x(G + g + 1)

                        def down(q, ks):
                            for k in ks:
                                if q == 0:
                                    pe.wait_ge(s["hlo_ready"], MB * g + k + 3)
                                last = by(ps[:, OB + q % 2, 0:D], lambda p: hB[:, p, k, q * S:(q + 1) * S],
                                          lambda p: l0d[:, p, k, :], k == 0, k == MB - 1, weight_moves=True)
                            if k == MB - 1:
                                last.then_inc(s["down_done"], 1)
                        pe.wait_ge(s["pv_used"], NB + 1)
                        for q in range(2):
                            pe.wait_ge(s["xB_done"], Q * g + q + 1)
                            down(q, range(MB - 2))
                        for k in (MB - 2, MB - 1):
                            for q in range(2):
                                down(q, (k,))
                        for q in range(2, Q):
                            pe.wait_ge(s["xB_done"], Q * g + q + 1)
                            down(q, range(MB))

            with pe.If(flag_reg > 0):
                stage_b(True)
            with pe.Else():
                stage_b(False)

            pe.wait_ge(s["xB_done"], NB + 2)

            def keys(g, u):
                pe.wait_ge(s["klo_done"], G + g + 1)
                for m in range(KD):
                    pe.wait_ge(s["qrc_done"], KD * g + m + 1)
                    for c in range(KD):
                        last = three(ps[:, PJ + m, :], lambda p: xaw[:, p, c, m * P:(m + 1) * P],
                                     lambda p: kT[:, u, p, c, :], c == 0, c == KD - 1)
                    last.then_inc(s["kr_done"], 1)

            def queries(g, u):
                pe.wait_ge(s["xlo_done"], KD * (2 * G + g + 1))
                for m in range(KD):
                    pe.wait_ge(s["krc_done"], KD * g + m + 1)
                    for c in range(KD):
                        last = three(ps[:, PJ + m, :], lambda p: xaw[:, p, c, m * P:(m + 1) * P],
                                     lambda p: xT[:, u, p, c, :], c == 0, c == KD - 1)
                    last.then_inc(s["qr_done"], 1)

            pe.wait_ge(s["flag_sums"], 2)
            mm(ps[0:1, OB, 0:1], fsum[:, 1:2], onec[:, :], start=True, stop=True).then_inc(s["flag_tot"], 1)
            keys(0, 0)
            queries(0, 0)
            pe.wait_ge(s["flag_ready"], 2)
            flag_reg = pe.value_load(fint[0:1, 1:2])
            with pe.Fori(0, 2) as i:
                for u in range(2):
                    g = 2 * i + u
                    gn = g + 1 if u == 0 else G // 2
                    more = (lambda f: f()) if u == 0 else (lambda f: if_more(pe, i, f))
                    turn_x(2 * G + g + 1)
                    pe.wait_ge(s["qrc_done"], KD * g + 2 * KD)
                    pe.wait_ge(s["sm_ready"], g + 1)
                    for q in range(Q):
                        for c in range(KD):
                            last = mm(ps[:, SCB, q * S:(q + 1) * S], qr[:, c, q * S:(q + 1) * S],
                                      kr[:, c, q * S:(q + 1) * S], start=(c == 0), stop=(c == KD - 1))
                    last.then_inc(s["sc_done"], 1)
                    more(lambda: keys(gn, 1 - u))
                    pe.wait_ge(s["at_ready"], g + 1)
                    for q in range(Q):
                        pe.wait_ge(s["al_ready"], Q * g + q + 1)
                        last = nc.tensor.transpose(ps[:, ATB, q * S:(q + 1) * S], al[:, q, :], idf[:, :])
                    last.then_inc(s["at_done"], 1)
                    more(lambda: queries(gn, 1 - u))
                    pe.wait_ge(s["at_ready"], g + 2)
                    pe.wait_ge(v_ld[u], 16 * Q * (i + 3))
                    pe.wait_ge(s["xC_done"], Q * g + 2)
                    for q in range(Q):
                        mm(ps[:, OB + q // 2, (q % 2) * D:(q % 2 + 1) * D].rearrange("p (h d) -> p h d", d=DH),
                           alT[:, q, :], V[:, u, q, 0:NH, 0:DH], start=True, stop=True).then_inc(s["av_done"], 1)

            pe.wait_ge(s["w_ld"], 48)
            pe.wait_ge(s["h1_ld"], 16 * MD)
            pe.wait_ge(s["h2_ld"], 16 * MD)

            def wide(o, lhs, rhs, k, n_k, general):
                for p in range(2):
                    a, b = lhs(k, p), rhs(k, p)
                    if general:
                        a, b = a.bitcast(F32), b.bitcast(F32)
                    last = mm(o, a, b, start=(k == 0 and p == 0), stop=(k == n_k - 1 and p == 1))
                return last

            def stage_d(general):
                with pe.Fori(0, 2) as i:
                    for u in range(2):
                        g = 2 * i + u
                        gn = g + 1 if u == 0 else G // 2
                        d0 = 3 * MD * g
                        item = 0

                        def block_wait():
                            if general:
                                pe.wait_ge(ring_ld[item % RING], 16 * ((ITEMS_G // RING) * g + item // RING + 1))

                        def block_free(last, name):
                            nonlocal item
                            last.then_inc(s[name], 1)
                            item += 1

                        pe.wait_ge(s["xlo_done"], KD * (3 * G + g + 1))
                        for m in range(MD):
                            block_wait()
                            if m < 2:
                                pe.wait_ge(s["d_act"], d0 + 1 + m)
                            else:
                                pe.wait_ge(s["d_act"], d0 + m + 1)
                                pe.wait_ge(s["d_h32"], MD * g + m + 1)
                            for a, (w, bank) in enumerate(((w1, 2), (w2, 4))):
                                for k in range(KD):
                                    if general:
                                        lhs = lambda k, p: ring[:, item % RING, a * KD + k, :]
                                    else:
                                        lhs = lambda k, p: w[:, k, m * P:(m + 1) * P]
                                    last = wide(ps[:, bank + m % 2, :], lhs, lambda k, p: xT[:, u, p, k, :],
                                                k, KD, general)
                            block_free(last, "d_pre")
                        for L, w in enumerate((h1, h2)):
                            src = (hA, hBt)[(L + u) % 2]
                            for m in range(MD):
                                if L == 1 and m == 4:
                                    nxt = lambda: turn_x(3 * G + gn)
                                    nxt() if u == 0 else if_more(pe, i, nxt)
                                block_wait()
                                idx = MD * (L + 1) + m
                                if L == 0 and m == 0:
                                    pe.wait_ge(s["d_act"], d0 + 2 + MD - 1)
                                if idx >= 12:
                                    pe.wait_ge(s["d_act"], d0 + 2 + idx - 3)
                                for k in range(MD):
                                    if m == 0:
                                        pe.wait_ge(s["d_lo"], d0 + 2 + MD * L + k + 1)
                                    if general:
                                        lhs = lambda k, p: ring[:, item % RING, k, :]
                                    else:
                                        lhs = lambda k, p: w[:, k, m * P:(m + 1) * P]
                                    last = wide(ps[:, 2 + m % 4, :], lhs, lambda k, p: src[:, p, k, :], k, MD, general)
                                block_free(last, "d_pre")
                        src = (hA, hBt)[u]
                        pe.wait_ge(s["xC_done"], NB + 2)
                        for half in range(2):
                            block_wait()
                            item += 1
                        item -= 2
                        for q in range(Q):
                            pe.wait_ge(s["xD_done"], Q * g + q + 1)
                            for k in range(MD):
                                if q == 0:
                                    pe.wait_ge(s["d_lo"], d0 + 2 + 2 * MD + k + 1)
                                if general:
                                    rhs = lambda k, p: ring[:, (item + k // Q) % RING, 2 * (k % Q):2 * (k % Q) + 2, :]
                                else:
                                    rhs = lambda k, p: w3[:, k, :]
                                last = wide(ps[:, OB + q % 2, 0:D], lambda k, p: src[:, p, k, q * S:(q + 1) * S],
                                            rhs, k, MD, general)
                            last.then_inc(s["d_out"], 1)

            with pe.If(flag_reg > 0):
                stage_d(True)
            with pe.Else():
                stage_d(False)

        @block.scalar
        def _(act):
            fn = nc.scalar.activation
            act.sem_inc(s["flag_used"], FLAG_BUFS)
            act.sem_inc(s["d_ready"], 2)
            act.sem_inc(s["silu_ready"], 2)
            act.sem_inc(s["d_act"], 2)

            def x_hi(n, par):
                for c in range(KD):
                    act.wait_ge(s["tr_done"], n + 1)
                    fn(xT[:, par, 0, c, :], tr_bank(c), ACT.Copy).then_inc(s["xhi_done"], 1)

            def k_hi(nth, kst, par):
                act.wait_ge(ctxT_ld[par], 16 * nth)
                fn(kT[:, par, 0, :, :], kst, ACT.Copy).then_inc(s["khi_done"], 1)

            def gate_copy(g, bank=TR):
                act.wait_ge(s["gate_done"], g + 1)
                fn(gsb[:, :], ps[0:2 * NH, bank, :], ACT.Copy).then_inc(s["gate_copied"], 1)

            def log_part(g):
                act.wait_ge(s["ab_ready"], g + 1)
                fn(fl[:, :], fab[:, :], ACT.Exp, scale=-1.0).then_inc(s["act_own"], 1)
                act.wait_ge(s["act_own"], g + 1)
                fn(fl[:, :], fl[:, :], ACT.Ln, bias=1.0).then_inc(s["ln_ready"], 1)

            def floor_part(g):
                act.wait_ge(s["ncs_ready"], g + 1)
                fn(Er[:, :], Er[:, :], ACT.Exp).then_inc(s["er_ready"], 1)

            def low_sum(view, to, name):
                low = view.bitcast(U16).rearrange("p (w a) -> p w a", a=2)[:, :, 0:1]
                fn(view.rearrange("p (w a) -> p w a", a=1), low, ACT.Copy, accum_out=to).then_inc(s[name], 1)

            def table_set(n):
                nc.scalar.add_instruction(mybir.InstLoadActFuncSet(name=nc.get_next_instruction_name(),
                                                                   engine=mybir.EngineType.Activation,
                                                                   act_func_set_id=n))

            table_set(EXP_AND_LN)
            k_hi(1, kstA[:, :, :], 0)
            x_hi(0, 0)
            gate_copy(0, QK)
            k_hi(1, kstA[:, :, :], 1)
            log_part(0)
            x_hi(1, 1)
            floor_part(0)
            with act.Fori(0, 2) as i:
                for u in range(2):
                    g = 2 * i + u
                    gn = g + 1 if u == 0 else G // 2
                    more = (lambda f: f()) if u == 0 else (lambda f: if_more(act, i, f))
                    for k in range(UN):
                        n = UN * g + k
                        quad = k % 2
                        act.wait_ge(s["expo_done"], n + 1)
                        act.wait_ge(s["c_ready"], n + 1)
                        fn(Dt[:, quad, :, :], ps[:, EX + quad, :].rearrange("p (j t) -> p j t", j=Q), ACT.Exp,
                           scale=-1.0).then_inc(s["d_ready"], 1)
                        if k == 0:
                            if u == 0:
                                with act.If(i > 0):
                                    k_hi(2, kstA[:, :, :], 1)
                            else:
                                more(lambda: k_hi(2, kstA[:, :, :], 0))
                        if k == 1:
                            more(lambda: gate_copy(gn))
                        if k == 3:
                            more(lambda: log_part(gn))
                        if k == 4:
                            more(lambda: floor_part(gn))
                        if k == UN - 1:
                            act.wait_ge(s["l0_lo"], 2 * g + 2)
                            low_sum(rawgu[:, bass.ds(i, 1), u, :].rearrange("p a w -> p (a w)"),
                                    facc[:, bass.ds(2 * g, 1)], "raw_seen")
                            if u == 1:
                                low_sum(rawd[:, bass.ds(i, 1), :, :].rearrange("p a m w -> p (a m w)"),
                                        facc[:, bass.ds(2 * g + 1, 1)], "raw_seen")
                            if u == 0:
                                x_hi(g + 2, u)
                            else:
                                more(lambda: x_hi(3, u))
            act.wait_ge(s["raw_seen"], G + G // 2)
            fn(facc[:, 0:2 * G], facc[:, 0:2 * G], ACT.Copy, accum_out=fsum[:, 0:1]).then_inc(s["flag_sums"], 1)

            act.wait_ge(s["qk_done"], UN * G + 4)
            for u in range(2):
                k_hi(3, kstC[:, u, :, :], u)
            table_set(SILU)
            act.wait_ge(s["xA_done"], NB)

            def look(g, m):
                act.wait_ge(flag_ld[m], 16 * (g + 1))
                low_sum(looked[:, m, :], facc[:, bass.ds(FLAG_BUFS * g + m + 2 * G, 1)], "flag_used")
            with act.Fori(0, 2) as i:
                for u in range(2):
                    g = 2 * i + u
                    gn = g + 1 if u == 0 else G // 2
                    for m in range(MB + 1):
                        n = MB * g + m
                        if m < MB:
                            act.wait_ge(s["gu_done"], n + 1)
                            act.wait_ge(s["hf_ready"], n + 1)
                            fn(silB[:, m % 2, :], ps[:, GB + m % 2, :], ACT.Silu, scale=SCALE_B)\
                                .then_inc(s["silu_ready"], 1)
                        if m:
                            act.wait_ge(s["hf_ready"], n + 2)
                            fn(hB[:, 0, m - 1, :], hfB[:, (m - 1) % 2, :], ACT.Copy).then_inc(s["hhi_ready"], 1)
                        if m in (1, 3):
                            look(g, m // 2)
                    x_hi(G + g + 1, 1 - u)
                    look(g, 2)
                    look(g, 3)
            act.wait_ge(s["flag_used"], FLAG_ITEMS + FLAG_BUFS)
            fn(facc[:, 2 * G:], facc[:, 2 * G:], ACT.Copy, accum_out=fsum[:, 1:2]).then_inc(s["flag_sums"], 1)

            def relu_keys(g):
                for m in range(KD):
                    act.wait_ge(s["kr_done"], KD * g + m + 1)
                    fn(kr[:, m, :], ps[:, PJ + m, :], ACT.Relu).then_inc(s["krc_done"], 1)

            table_set(EXP_ONLY)
            act.wait_ge(s["down_done"], NB)
            relu_keys(0)
            with act.Fori(0, 2) as i:
                for u in range(2):
                    g = 2 * i + u
                    gn = g + 1 if u == 0 else G // 2
                    more = (lambda f: f()) if u == 0 else (lambda f: if_more(act, i, f))
                    x_hi(2 * G + g + 1, 1 - u)
                    act.wait_ge(s["sm_ready"], g + 2)
                    for q in range(Q):
                        fn(al[:, q, :], sc[:, q, :], ACT.Exp, bias=nmx[:, q:q + 1], accum_out=rsm[:, q:q + 1])\
                            .then_inc(s["al_ready"], 1)
                    more(lambda: relu_keys(gn))
                    with act.If(i < 1):
                        k_hi(4, kstC[:, u, :, :], u)

            table_set(SILU)
            act.wait_ge(s["av_done"], NB + 2 * Q)
            with act.Fori(0, 2) as i:
                for u in range(2):
                    g = 2 * i + u
                    gn = g + 1 if u == 0 else G // 2
                    d0 = 3 * MD * g
                    dst = (hA, hBt)[u]
                    for m in range(MD + 1):
                        if m < MD:
                            act.wait_ge(s["d_pre"], d0 + m + 1)
                            act.wait_ge(s["d_h32"], MD * g + m + 1)
                            fn(silD[:, m % 2, :], ps[:, 2 + m % 2, :], ACT.Silu, scale=scol[:, 0, m:m + 1])\
                                .then_inc(s["d_act"], 1)
                        if m:
                            act.wait_ge(s["d_h32"], MD * g + m + 2)
                            fn(dst[:, 0, m - 1, :], h32[:, (m - 1) % 2, :], ACT.Copy).then_inc(s["d_hi"], 1)
                    for idx in range(MD, 3 * MD):
                        m, L = idx % MD, idx // MD
                        if L == 2 and m == 4:
                            nxt = lambda: x_hi(3 * G + gn, 1 - u)
                            nxt() if u == 0 else if_more(act, i, nxt)
                        if idx == MD:
                            fn(probe[:, 0:1], onec[:, :], ACT.Gelu)
                        act.wait_ge(s["d_pre"], d0 + idx + 1)
                        act.wait_ge(s["d_lo"], d0 + idx + 1)
                        fn(h32[:, m % 2, :], ps[:, 2 + m % 4, :], ACT.Gelu, scale=scol[:, L + 1, m:m + 1])\
                            .then_inc(s["d_act"], 1)
                    fn(probe[:, 1:2], onec[:, :], ACT.Silu)

        @block.vector
        def _(dve):
            v = nc.vector
            dve.sem_inc(s["c_ready"], 2)
            dve.sem_inc(s["pv_used"], 1)
            dve.sem_inc(s["hf_ready"], 2)
            dve.sem_inc(s["hlo_ready"], 2)
            dve.sem_inc(s["xB_done"], 2)
            dve.sem_inc(s["xC_done"], 2)
            dve.sem_inc(s["xD_done"], 2)
            dve.sem_inc(s["mask_free"], 1)
            dve.sem_inc(s["qrc_done"], KD)
            dve.sem_inc(s["sm_ready"], 1)
            dve.sem_inc(s["at_ready"], 1)
            dve.sem_inc(s["d_h32"], 2)
            dve.sem_inc(s["d_lo"], 2)

            def x_stats(n, b0):
                ch = Chain(dve, s["dve_prep"], 2 * Q + 1, n)
                for q in range(Q):
                    ch.step(v.bn_stats(st6[:, q, :], x[:, b0 + q, :]))
                ch.settle_apart()
                for q in range(Q):
                    ch.step(v.bn_aggr(mv[:, q, :], st6[:, q, :]))
                ch.settle()
                ch.end()
                v.tensor_scalar(ve[:, :], mv[:, :, 1], 1e-5, None, ALU.add).then_inc(s["mv_ready"], 1)

            def x_norm(n, b0):
                dve.wait_ge(s["rstd_ready"], n + 1)
                for q in range(Q):
                    last = v.tensor_scalar(xn[:, q, :], x[:, b0 + q, :], mv[:, q, 0:1], rstd[:, q:q + 1],
                                           ALU.subtract, ALU.mult)
                last.then_inc(s["xn_ready"], 1)

            def x_lo(n, par):
                for c in range(KD):
                    dve.wait_ge(s["xhi_done"], KD * n + c + 1)
                    v.tensor_tensor(xT[:, par, 1, c, :], tr_bank(c), xT[:, par, 0, c, :], ALU.subtract)\
                        .then_inc(s["xlo_done"], 1)

            A2 = 9

            def gate_a(g):
                dve.wait_ge(s["gate_moved"], 32 * (g + 1))
                ch = Chain(dve, s["dve_a2"], A2, g)
                ch.step(v.tensor_scalar(fmn[:, :], gf[:, :], gb[:, 1:2], None, ALU.add))
                ch.settle()
                v.scalar_tensor_tensor(out=fab[:, :], in0=fmn[:, :], scalar=-1.0, in1=fmn[:, :], op0=ALU.mult,
                                       op1=ALU.max).then_inc(s["ab_ready"], 1)
                return ch

            def gate_b(g, ch):
                dve.wait_ge(s["ln_ready"], g + 1)
                ch.settle()
                ch.step(v.scalar_tensor_tensor(out=fl[:, :], in0=fmn[:, :], scalar=0.0, in1=fl[:, :],
                                               op0=ALU.min, op1=ALU.subtract))
                ch.settle()
                ch.step(v.tensor_tensor_scan(cs[:, :], one_r[:, :], fl[:, :], 0.0, ALU.mult, ALU.add))
                ch.settle()
                ch.step(v.scalar_tensor_tensor(out=Z[:, 1, :], in0=gi[:, :], scalar=gb[:, 0:1], in1=cs[:, :],
                                               op0=ALU.add, op1=ALU.subtract))
                ch.settle()
                ch.step(v.tensor_scalar(Z[:, 1, :], Z[:, 1, :], -1.0, None, ALU.mult))
                ch.settle()
                ch.step(v.tensor_tensor_scan(Z[:, 0, :], Z[:, 1, :], Z[:, 1, :], BIG, ALU.min, ALU.min))
                ch.settle()
                v.tensor_tensor(Er[:, :], Z[:, 0, :], cs[:, :], ALU.subtract).then_inc(s["ncs_ready"], 1)

            def gate_c(g, ch):
                ch.step(v.tensor_copy(zp[:, 0, :, :], Z[:, :, :]))
                ch.settle()
                ch.step(v.tensor_tensor(zr[:, :, :], Z[:, :, :], zp[:, 0, :, :], ALU.subtract))
                ch.settle()
                ch.step(v.tensor_copy(zp[:, 1, :, :], zr[:, :, :]))
                ch.settle()
                v.tensor_tensor(zp[:, 2, :, :], zr[:, :, :], zp[:, 1, :, :], ALU.subtract).then_inc(s["z_ready"], 1)
                ch.end()

            def floor_copy(g, par):
                dve.wait_ge(s["er_turned"], g + 1)
                v.tensor_scalar(ET[:, par, :], ps[:, TR + 1, 0:NR], EPS, None, ALU.add).then_inc(s["et_ready"], 1)

            def weigh(g, k):
                n, q, quad = UN * g + k, k // 2, k % 2
                dve.wait_ge(s["d_ready"], n + 3)
                dve.wait_ge(s["qk_done"], n + 5)
                dve.wait_ge(s["pv_done"], Q * g + q + 1)
                v.scalar_tensor_tensor(out=Cts[q % 2][:, quad, :, :].rearrange("p j t -> p (j t)"),
                                       in0=ps[:, QK + quad, :], scalar=RS_DH,
                                       in1=Dt[:, quad, :, :].rearrange("p j t -> p (j t)"),
                                       op0=ALU.mult, op1=ALU.mult).then_inc(s["c_ready"], 1)

            def centre(b, par):
                h = hm[:, par, :, :].rearrange("p h d -> p (h d)")
                dve.wait_ge(s["hrs_ready"], b + 1)
                v.scalar_tensor_tensor(out=h, in0=h, scalar=hmv[:, par, 0:1], in1=lns[:, :],
                                       op0=ALU.subtract, op1=ALU.mult).then_inc(s["centred"], 1)

            def add_on(b, par):
                dve.wait_ge(s["centred"], b + 1)
                v.scalar_tensor_tensor(out=x[:, b, :], in0=hm[:, par, :, :].rearrange("p h d -> p (h d)"),
                                       scalar=hrs[:, par:par + 1], in1=x[:, b, :],
                                       op0=ALU.mult, op1=ALU.add).then_inc(s["xA_done"], 1)

            def head_norm(b, q):
                centre(b, q % 2)
                add_on(b, q % 2)

            def finish(b, par, q, norm=False):
                if norm:
                    centre(b - 1, (q - 1) % 2)
                ch = Chain(dve, s["dve_unit"], 7, b)
                pvb = ps[:, PV:PV + 2, 0:Q * PVW].rearrange("p a (j w) -> p a j w", j=Q)
                floor = ET[:, par, :].rearrange("p (j a q) -> p a j q", a=2, q=Q)[:, :, :, q]
                flat = hm[:, q % 2, :, :].rearrange("p h d -> p (h d)")
                dve.wait_ge(s["pv_done"], b + 3)
                ch.step(v.tensor_scalar(den[:, 0, :, :], pvb[:, :, :, DH], -1.0, EPS, ALU.mult, ALU.add))
                ch.step(v.scalar_tensor_tensor(out=den[:, 1, :, :], in0=pvb[:, :, :, DH], scalar=EPS, in1=floor,
                                               op0=ALU.add, op1=ALU.max))
                if norm:
                    add_on(b - 1, (q - 1) % 2)
                ch.settle()
                ch.step(v.tensor_tensor(den[:, 1, :, :], den[:, 0, :, :], den[:, 1, :, :], ALU.max))
                ch.settle()
                ch.step(v.reciprocal(den[:, 2, :, :], den[:, 1, :, :]))
                ch.settle()
                v.tensor_tensor(hm[:, q % 2, :, :].rearrange("p (a j) d -> p a j d", a=2), pvb[:, :, :, 0:DH],
                                den[:, 2, :, :].rearrange("p a (j o) -> p a j o", o=1).to_broadcast([P, 2, Q, DH]),
                                ALU.mult).then_inc(s["pv_used"], 1)
                dve.wait_ge(s["pv_used"], b + 2)
                ch.step(v.bn_stats(h6[:, :], flat))
                ch.settle_apart()
                ch.step(v.bn_aggr(hmv[:, q % 2, :], h6[:, :]))
                ch.settle()
                v.tensor_scalar(hve[:, q % 2:q % 2 + 1], hmv[:, q % 2, 1:2], 1e-5, None, ALU.add)\
                    .then_inc(s["hstat_ready"], 1)
                ch.end()

            v.memset(one_r[:, :], 1.0)
            v.memset(onec[:, :], 1.0)
            v.memset(facc[:, :], 0.0)
            v.memset(Qb[:, 1, :, :, :, :].bitcast(F32), 0.0).then_inc(s["const_set"], 1)
            dve.wait_ge(s["x_first"], 16)
            x_stats(0, 0)
            x_norm(0, 0)
            dve.wait_ge(s["ident_ld"], 16)
            v.tensor_copy(idb[:, :], idf[:, :]).then_inc(s["idb_ready"], 1)
            x_lo(0, 0)
            dve.wait_ge(s["x_second"], 16)
            x_stats(1, Q)
            x_norm(1, Q)
            dve.wait_ge(s["consts"], CONSTS)
            ch = gate_a(0)
            gate_b(0, ch)
            gate_c(0, ch)
            x_lo(1, 1)
            floor_copy(0, 0)
            dve.wait_ge(s["x_rest"], 16 * (G - 2))
            with dve.Fori(0, 2) as i:
                for u in range(2):
                    g = 2 * i + u
                    gn = g + 1 if u == 0 else G // 2
                    more = (lambda f: f()) if u == 0 else (lambda f: if_more(dve, i, f))
                    last = 2 * Q - 1 if u == 0 else Q * g - 1
                    before = (lambda f: if_later(dve, i, f)) if u == 0 else (lambda f: f())
                    state = {}
                    for q in range(Q):
                        b = Q * g + q
                        weigh(g, 2 * q)
                        weigh(g, 2 * q + 1)
                        if q == 0:
                            def close():
                                finish(last, 1 - u, Q - 1, norm=True)
                            before(close)
                            if u == 0:
                                dve.wait_ge(s["pv_used"], Q * g + 1)
                                x_stats(g + 2, 8 - 8 * i)
                            else:
                                more(lambda: x_stats(3, 3 * Q))
                        if q == 1:
                            more(lambda: state.update(ch=gate_a(gn)))
                            finish(b - 1, u, q - 1, norm=(u == 1))
                            more(lambda: gate_b(gn, state["ch"]))
                            if u == 0:
                                before(lambda: head_norm(last, Q - 1))
                        if q == 2:
                            more(lambda: gate_c(gn, state["ch"]))
                            more(lambda: floor_copy(gn, 1 - u))
                            finish(b - 1, u, q - 1, norm=True)
                            if u == 0:
                                x_norm(g + 2, 8 - 8 * i)
                            else:
                                more(lambda: x_norm(3, 3 * Q))
                        if q == Q - 1:
                            finish(b - 1, u, q - 1, norm=True)
                            if u == 0:
                                x_lo(g + 2, u)
                            else:
                                more(lambda: x_lo(3, u))
            dve.wait_ge(s["flag_tot"], 1)
            v.tensor_scalar(fint[:, 0:1], ps[0:1, EX, 0:1], 0.0, None, ALU.is_gt).then_inc(s["flag_ready"], 1)
            finish(NB - 1, 1, Q - 1, norm=True)
            head_norm(NB - 1, Q - 1)

            dve.wait_ge(s["xA_done"], NB)
            with dve.Fori(0, 2) as i:
                for u in range(2):
                    g = 2 * i + u
                    gn = g + 1 if u == 0 else G // 2
                    b1 = Q * (g + 1) if u == 0 else 8 - 8 * i
                    dve.wait_ge(s["xB_done"], Q * g + 2)
                    x_stats(G + g + 1, b1)
                    for m in range(MB + 1):
                        n = MB * g + m
                        if m == 1:
                            x_norm(G + g + 1, b1)
                        if m < MB:
                            dve.wait_ge(s["hlo_ready"], n + 1)
                            dve.wait_ge(s["silu_ready"], n + 3)
                            v.scalar_tensor_tensor(out=hfB[:, m % 2, :], in0=ps[:, UB + m % 2, :], scalar=SCALE_B,
                                                   in1=silB[:, m % 2, :], op0=ALU.mult, op1=ALU.mult)\
                                .then_inc(s["hf_ready"], 1)
                        if m:
                            dve.wait_ge(s["hhi_ready"], n)
                            v.tensor_tensor(hB[:, 1, m - 1, :], hfB[:, (m - 1) % 2, :], hB[:, 0, m - 1, :],
                                            ALU.subtract).then_inc(s["hlo_ready"], 1)
                    for q in range(Q):
                        if q == 2:
                            x_lo(G + g + 1, 1 - u)
                        dve.wait_ge(s["down_done"], Q * g + q + 1)
                        b = Q * g + q
                        v.scalar_tensor_tensor(out=x[:, b, :], in0=ps[:, OB + q % 2, 0:D], scalar=SCALE_B,
                                               in1=x[:, b, :], op0=ALU.mult, op1=ALU.add).then_inc(s["xB_done"], 1)

            dve.wait_ge(s["xB_done"], NB + 2)
            x_stats(2 * G + 1, Q)
            x_norm(2 * G + 1, Q)

            def scale_queries(g):
                for m in range(KD):
                    dve.wait_ge(s["qr_done"], KD * g + m + 1)
                    v.tensor_scalar(qr[:, m, :], ps[:, PJ + m, :], 0.0, diag[:, m:m + 1], ALU.max, ALU.mult)\
                        .then_inc(s["qrc_done"], 1)

            dve.wait_ge(s["flag_tot"], 2)
            v.tensor_scalar(fint[:, 1:2], ps[0:1, OB, 0:1], 0.0, None, ALU.is_gt).then_inc(s["flag_ready"], 1)
            scale_queries(0)
            with dve.Fori(0, 2) as i:
                for u in range(2):
                    g = 2 * i + u
                    gn = g + 1 if u == 0 else G // 2
                    more = (lambda f: f()) if u == 0 else (lambda f: if_more(dve, i, f))
                    dve.wait_ge(s["mask_ld"], 16 * (g + 1))
                    v.tensor_scalar(mf[:, :, :], mk[:, :, :], -NEG, NEG, ALU.mult, ALU.add).then_inc(s["mask_free"], 1)
                    dve.wait_ge(s["sc_done"], g + 1)
                    dve.wait_ge(s["mask_free"], g + 2)
                    ch = Chain(dve, s["dve_d"], Q + 2, g)
                    ch.start_apart()
                    for q in range(Q):
                        ch.step(v.tensor_tensor_reduce(sc[:, q, :], ps[:, SCB, q * S:(q + 1) * S], mf[:, q, :], 1.0,
                                                       -BIG, ALU.add, ALU.max, smx[:, q:q + 1]))
                    ch.settle()
                    v.tensor_scalar(nmx[:, :], smx[:, :], -1.0, None, ALU.mult).then_inc(s["sm_ready"], 1)
                    x_lo(2 * G + g + 1, 1 - u)
                    if u == 0:
                        dve.wait_ge(s["xC_done"], Q * g + 2)
                        x_stats(2 * G + g + 2, 8 - 8 * i)
                    else:
                        more(lambda: x_stats(2 * G + 3, 3 * Q))
                    dve.wait_ge(s["at_done"], g + 1)
                    v.tensor_copy(alT[:, :, :].rearrange("p q t -> p (q t)"), ps[:, ATB, :]).then_inc(s["at_ready"], 1)
                    more(lambda: scale_queries(gn))
                    if u == 0:
                        x_norm(2 * G + g + 2, 8 - 8 * i)
                    else:
                        more(lambda: x_norm(2 * G + 3, 3 * Q))
                    ch.step(v.reciprocal(rrs[:, :], rsm[:, :]))
                    ch.settle()
                    ch.end()
                    for q in range(Q):
                        b = Q * g + q
                        if q % 2 == 0:
                            dve.wait_ge(s["av_done"], b + 2 * Q + 2)
                        v.scalar_tensor_tensor(out=x[:, b, :], in0=ps[:, OB + q // 2, (q % 2) * D:(q % 2 + 1) * D],
                                               scalar=rrs[:, q:q + 1],
                                               in1=x[:, b, :], op0=ALU.mult, op1=ALU.add).then_inc(s["xC_done"], 1)
            dve.wait_ge(s["av_done"], NB + 2 * Q)
            dve.wait_ge(s["xC_done"], NB + 2)
            with dve.Fori(0, 2) as i:
                for u in range(2):
                    g = 2 * i + u
                    gn = g + 1 if u == 0 else G // 2
                    d0 = 3 * MD * g
                    dst = (hA, hBt)[u]
                    for m in range(MD + 1):
                        if m < MD:
                            dve.wait_ge(s["d_lo"], d0 + m + 1)
                            dve.wait_ge(s["d_act"], d0 + m + 3)
                            v.scalar_tensor_tensor(out=h32[:, m % 2, :], in0=ps[:, 4 + m % 2, :],
                                                   scalar=scol[:, 1, m:m + 1], in1=silD[:, m % 2, :],
                                                   op0=ALU.mult, op1=ALU.mult).then_inc(s["d_h32"], 1)
                        if m:
                            dve.wait_ge(s["d_hi"], MD * g + m)
                            v.tensor_tensor(dst[:, 1, m - 1, :], h32[:, (m - 1) % 2, :], dst[:, 0, m - 1, :],
                                            ALU.subtract).then_inc(s["d_lo"], 1)
                    for idx in range(MD, 3 * MD):
                        m, L = idx % MD, idx // MD
                        dst = (hA, hBt)[(L + u) % 2]
                        if L == 2 and m == 0:
                            nxt = lambda: x_stats(3 * G + gn, Q * gn)
                            nxt() if u == 0 else if_more(dve, i, nxt)
                        if L == 2 and m == 2:
                            nxt = lambda: x_norm(3 * G + gn, Q * gn)
                            nxt() if u == 0 else if_more(dve, i, nxt)
                        if L == 2 and m == 5:
                            nxt = lambda: x_lo(3 * G + gn, 1 - u)
                            nxt() if u == 0 else if_more(dve, i, nxt)
                        dve.wait_ge(s["d_act"], d0 + idx + 3)
                        v.tensor_copy(dst[:, 0, m, :], h32[:, m % 2, :]).then_inc(s["dh_own"], 1)
                        dve.wait_ge(s["dh_own"], 2 * MD * g + idx - MD + 1)
                        v.tensor_tensor(dst[:, 1, m, :], h32[:, m % 2, :], dst[:, 0, m, :], ALU.subtract)\
                            .then_inc(s["d_lo"], 1)
                    for q in range(Q):
                        b = Q * g + q
                        dve.wait_ge(s["d_out"], b + 2)
                        dve.wait_ge(s["xD_done"], b + 1)
                        v.tensor_tensor(ot[:, q % 2, :], ps[:, OB + q % 2, 0:D], s3[:, :], ALU.mult)\
                            .then_inc(s["ot_ready"], 1)
                        dve.wait_ge(s["ot_ready"], b + 1)
                        v.tensor_tensor(x[:, b, :], x[:, b, :], ot[:, q % 2, :], ALU.add).then_inc(s["xD_done"], 1)


def if_later(eng, i, f):
    with eng.If(i > 0):
        f()


def if_more(eng, i, f):
    with eng.If(i < 1):
        f()


def kernel(x, ctx_1024, mask_BxS2_if1, L0_xattn_igate_w, L0_xattn_igate_b, L0_xattn_fgate_w, L0_xattn_fgate_b,
           L0_xattn_ln_scale, L0_ffn_w_gate, L0_ffn_w_up, L0_ffn_w_down, L1_xattn_W, L1_xattn_diagonal,
           L1_ffn_w1_w, L1_ffn_w1_s, L1_ffn_w2_w, L1_ffn_w2_s, L1_ffn_h1_w, L1_ffn_h1_s, L1_ffn_h2_w,
           L1_ffn_h2_s, L1_ffn_w3_w, L1_ffn_w3_s):
    import numpy as np
    import concourse.bacc as _bacc
    from concourse.bass_utils import run_bass_kernel_spmd as _run

    def rows(w):
        t = np.asarray(w).T
        return np.ascontiguousarray(t.reshape(t.shape[0] // P, P, t.shape[1]).transpose(1, 0, 2))

    def cols(v):
        return np.asarray(v).reshape(-1, P).T

    x, ctx = np.asarray(x), np.asarray(ctx_1024)
    order = np.arange(NH).reshape(NH // Q, Q).T.ravel()
    gate_w = np.concatenate([np.asarray(L0_xattn_igate_w)[order], np.asarray(L0_xattn_fgate_w)[order]], axis=0)
    gate_b = np.stack([np.repeat(np.asarray(b)[order], Q) for b in (L0_xattn_igate_b, L0_xattn_fgate_b)], 1)
    scales = np.zeros((P, 4, MD), np.float32)
    for n, v in enumerate((L1_ffn_w1_s, L1_ffn_w2_s, L1_ffn_h1_s, L1_ffn_h2_s)):
        scales[:, n, :] = cols(v)
    w_all = np.concatenate([rows(w).reshape(P, -1) for w in (L1_ffn_w1_w, L1_ffn_w2_w, L1_ffn_w3_w, L1_ffn_h1_w,
                                                             L1_ffn_h2_w)], axis=1)
    import ml_dtypes
    bf = np.dtype(ml_dtypes.bfloat16)
    tri = np.zeros((P, Q, S), np.float32)
    t_, s_ = np.meshgrid(np.arange(P), np.arange(S), indexing="ij")
    tri[:, :, :] = np.where(t_ > s_, MASKED, 0.0)[:, None, :]
    ones_rows = np.zeros((RA, Q, 2, Q, S), np.float32)
    ones_rows[0:3] = -1.0
    for r in range(3, RA):
        ones_rows[r, (r - 3) % Q] = 1.0
    arrays = {
        "x_in": x,
        "ctx_in": ctx,
        "ctxT_in": np.ascontiguousarray(ctx.reshape(NB * S, KD, P).transpose(2, 1, 0)),
        "mask_in": np.asarray(mask_BxS2_if1),
        "gw_in": rows(gate_w),
        "gb_in": gate_b,
        "lns_in": np.asarray(L0_xattn_ln_scale),
        "l0gu_in": np.stack([rows(L0_ffn_w_gate), rows(L0_ffn_w_up)], axis=1),
        "l0d_in": rows(L0_ffn_w_down),
        "xaw_in": rows(L1_xattn_W),
        "diag_in": cols(L1_xattn_diagonal),
        "w_all_in": w_all,
        "s_cols_in": scales,
        "s3_in": np.asarray(L1_ffn_w3_s),
        "ident_in": np.eye(P, dtype=np.float32),
        "tri_in": tri.astype(bf),
        "ones_rows_in": ones_rows.astype(bf),
    }
    nc = _bacc.Bacc("TRN2", target_bir_lowering=False, num_devices=1)
    arrays = {k: np.ascontiguousarray(a) for k, a in arrays.items()}
    args = {k: nc.dram_tensor(k, a.shape, mybir.dt.from_np(a.dtype), kind="ExternalInput").ap()
            for k, a in arrays.items()}
    args["out"] = nc.dram_tensor("out", (NB, S, D), F32, kind="ExternalOutput").ap()
    two_layers(nc, **args)
    r = _run(nc, [arrays], core_ids=[0])
    return r.results[0]["out"]
```
